# Optimizing a Trainium2 kernel written in Bass

```python
import numpy as np
import jax
import jax.numpy as jnp

def _softmax(x, axis=-1):
    return jax.nn.softmax(x, axis=axis)

def _gelu(x):
    return jax.nn.gelu(x, approximate=True)

def _silu(x):
    return jax.nn.silu(x)

def _sigmoid(x):
    return jax.nn.sigmoid(x)

def _layernorm(x, axis=-1, eps=1e-05):
    m = jnp.mean(x, axis=axis, keepdims=True)
    v = jnp.var(x, axis=axis, keepdims=True)
    return (x - m) / jnp.sqrt(v + eps)

def _scatter_add(tgt, idx, src, axis=0):
    return tgt.at[idx].add(src)

def _segment_sum(src, seg, n):
    return jax.ops.segment_sum(src, seg, n)
kernel_name = 'mk_vit_tower_d2_tok_img768_r4_d5325d'

def setup_inputs(seed: int=0):
    np.random.seed(seed)
    _w = jnp.asarray

    def _rec_inputs():
        import jax
        import jax.numpy as jnp
        _rk = jax.random.key(seed)
        x = -7.10856e-05 + 0.999911 * jax.random.normal(jax.random.fold_in(_rk, 1), (2, 32, 128, 128), jnp.float32)
        return x
    x = _rec_inputs()

    def _L0_tok_setup():
        import jax, jax.numpy as jnp
        import numpy as np
        B, C, H, W = (8, 32, 128, 128)
        P = 8
        D = 128
        NH, DH = (8, 64)
        M = 512
        L = 2
        DOUT = 192
        INNER = NH * DH

        def _ln(x, g, b, eps=1e-05):
            mu = x.mean(-1, keepdims=True)
            xc = x - mu
            var = (xc * xc).mean(-1, keepdims=True)
            return xc * jax.lax.rsqrt(var + eps) * g + b

        def _forward(im, conv_w, conv_b, ln1_g, ln1_b, qkv_w, out_w, out_b, ln2_g, ln2_b, ff1_w, ff1_b, ff2_w, ff2_b, lnf_g, lnf_b, head_w, head_b):
            b, c, h, w = im.shape
            hp, wp = (h // P, w // P)
            patches = im.reshape(b, c, hp, P, wp, P)
            x = jnp.einsum('bchpwq,dcpq->bhwd', patches, conv_w)
            x = x.reshape(b, hp * wp, -1) + conv_b
            n = hp * wp
            scale = DH ** (-0.5)
            for i in range(ln1_g.shape[0]):
                y = _ln(x, ln1_g[i], ln1_b[i])
                qkv = y @ qkv_w[i]
                q, k, v = jnp.split(qkv, 3, axis=-1)
                to_heads = lambda t: t.reshape(b, n, NH, DH).transpose(0, 2, 1, 3)
                q, k, v = (to_heads(q), to_heads(k), to_heads(v))
                q = jax.nn.softmax(q, axis=-1) * scale
                k = jax.nn.softmax(k, axis=-2)
                ctx = jnp.einsum('bhnd,bhne->bhde', k, v)
                att = jnp.einsum('bhnd,bhde->bhne', q, ctx)
                att = att.transpose(0, 2, 1, 3).reshape(b, n, INNER)
                x = x + att @ out_w[i] + out_b[i]
                y = _ln(x, ln2_g[i], ln2_b[i])
                hdn = jax.nn.gelu(y @ ff1_w[i] + ff1_b[i], approximate=False)
                x = x + hdn @ ff2_w[i] + ff2_b[i]
            return _ln(x, lnf_g, lnf_b) @ head_w + head_b
        key = jax.random.key(seed)
        ks = iter(jax.random.split(key, 32))
        g = lambda shape, s=0.02: (jax.random.normal(next(ks), shape) * s).astype(jnp.float32)
        inp = {'im': jax.random.normal(next(ks), (B, C, H, W), dtype=jnp.float32), 'conv_w': g((D, C, P, P)), 'conv_b': jnp.zeros((D,), jnp.float32), 'ln1_g': jnp.ones((L, D), jnp.float32), 'ln1_b': jnp.zeros((L, D), jnp.float32), 'qkv_w': g((L, D, 3 * INNER)), 'out_w': g((L, INNER, D)), 'out_b': jnp.zeros((L, D), jnp.float32), 'ln2_g': jnp.ones((L, D), jnp.float32), 'ln2_b': jnp.zeros((L, D), jnp.float32), 'ff1_w': g((L, D, M)), 'ff1_b': jnp.zeros((L, M), jnp.float32), 'ff2_w': g((L, M, D)), 'ff2_b': jnp.zeros((L, D), jnp.float32), 'lnf_g': jnp.ones((D,), jnp.float32), 'lnf_b': jnp.zeros((D,), jnp.float32), 'head_w': g((D, DOUT)), 'head_b': jnp.zeros((DOUT,), jnp.float32)}
        return inp
    _L0_tok_all = _L0_tok_setup()
    _L0_tok_in = {k: v for k, v in _L0_tok_all.items() if k in ('conv_w', 'conv_b', 'ln1_g', 'ln1_b', 'qkv_w', 'out_w', 'out_b', 'ln2_g', 'ln2_b', 'ff1_w', 'ff1_b', 'ff2_w', 'ff2_b', 'lnf_g', 'lnf_b', 'head_w', 'head_b')}
    del _L0_tok_all

    def _L0_attn_setup():
        import jax, jax.numpy as jnp
        import numpy as np
        B, L, D = (1, 512, 192)
        E = 2
        DIN = E * D
        N = 16
        K = 4
        R = (D + 15) // 16
        EPS = 1e-05
        key = jax.random.key(seed)
        ks = jax.random.split(key, 9)
        s = lambda k, shape, sc: jax.random.normal(k, shape, jnp.float32) * sc
        return {'x': s(ks[0], (B, L, D), 1.0), 'w_in': s(ks[1], (2 * DIN, D), D ** (-0.5)), 'w_conv': s(ks[2], (DIN, 1, K), K ** (-0.5)), 'b_conv': s(ks[3], (DIN,), 0.02), 'w_xproj': s(ks[4], (R + 2 * N, DIN), DIN ** (-0.5)), 'w_dt': s(ks[5], (DIN, R), R ** (-0.5)), 'b_dt': s(ks[6], (DIN,), 0.02), 'A_log': jnp.log(jnp.broadcast_to(jnp.arange(1, N + 1, dtype=jnp.float32), (DIN, N))), 'D_param': jnp.ones((DIN,), jnp.float32), 'w_out': s(ks[7], (D, DIN), DIN ** (-0.5)), 'w_norm': jnp.ones((D,), jnp.float32)}
    _L0_attn_all = _L0_attn_setup()
    _L0_attn_in = {k: v for k, v in _L0_attn_all.items() if k in ('w_in', 'w_conv', 'b_conv', 'w_xproj', 'w_dt', 'b_dt', 'A_log', 'D_param', 'w_out', 'w_norm')}
    del _L0_attn_all

    def _L0_ffn_setup():
        import jax, jax.numpy as jnp
        import numpy as np
        E = 128
        I = 464
        IS = 928
        K = 6
        G = 1
        TG = 1
        SCALE = 2.5
        CAP = 192

        def moe_forward(hidden_states, Wg, e_bias, W_gate_up, W_down, Wsg, Wsu, Wsd):
            B, S, H = hidden_states.shape
            x = hidden_states.reshape(-1, H)
            T = x.shape[0]
            logits = x.astype(jnp.float32) @ Wg.T
            sig = jax.nn.sigmoid(logits)
            choice = sig + e_bias[None, :]
            grp = choice.reshape(T, G, E // G)
            group_scores = jax.lax.top_k(grp, 2)[0].sum(-1)
            gidx = jax.lax.top_k(group_scores, TG)[1]
            gmask = jnp.zeros((T, G), jnp.float32).at[jnp.arange(T)[:, None], gidx].set(1.0)
            smask = jnp.repeat(gmask, E // G, axis=1)
            scores_for_choice = jnp.where(smask > 0, choice, 0.0)
            topk_idx = jax.lax.top_k(scores_for_choice, K)[1]
            topk_w = jnp.take_along_axis(sig, topk_idx, axis=1)
            topk_w = topk_w / (topk_w.sum(-1, keepdims=True) + 1e-20)
            topk_w = topk_w * SCALE
            P = T * K
            flat_e = topk_idx.reshape(-1)
            order = jnp.argsort(flat_e)
            se = flat_e[order]
            counts = jax.ops.segment_sum(jnp.ones(P, jnp.int32), flat_e, num_segments=E)
            starts = jnp.cumsum(counts) - counts
            pos = jnp.arange(P) - starts[se]
            buf_idx = jnp.where(pos < CAP, se * CAP + pos, E * CAP)
            tok_of_pair = (order // K).astype(jnp.int32)
            w_of_pair = topk_w.reshape(-1)[order]
            token_buf = jnp.zeros((E * CAP,), jnp.int32).at[buf_idx].set(tok_of_pair, mode='drop')
            w_buf = jnp.zeros((E * CAP,), x.dtype).at[buf_idx].set(w_of_pair.astype(x.dtype), mode='drop')
            xb = x[token_buf].reshape(E, CAP, H)
            gu = jnp.einsum('ech,ehf->ecf', xb, W_gate_up)
            g, u = jnp.split(gu, 2, axis=-1)
            inter = jax.nn.silu(g) * u
            yb = jnp.einsum('eci,eih->ech', inter, W_down)
            yb = yb * w_buf.reshape(E, CAP, 1)
            routed = jnp.zeros((T, H), x.dtype).at[token_buf].add(yb.reshape(E * CAP, H))
            shared = jax.nn.silu(x @ Wsg) * (x @ Wsu) @ Wsd
            return (routed + shared).reshape(B, S, H)
        key = jax.random.key(seed)
        ks = jax.random.split(key, 8)
        B, S, H = (1, 512, 192)
        sc = 0.02
        return {'hidden_states': jax.random.normal(ks[0], (B, S, H), jnp.float32), 'Wg': jax.random.normal(ks[1], (E, H), jnp.float32) * sc, 'e_bias': jnp.zeros((E,), jnp.float32), 'W_gate_up': jax.random.normal(ks[2], (E, H, 2 * I), jnp.float32) * sc, 'W_down': jax.random.normal(ks[3], (E, I, H), jnp.float32) * sc, 'Wsg': jax.random.normal(ks[4], (H, IS), jnp.float32) * sc, 'Wsu': jax.random.normal(ks[5], (H, IS), jnp.float32) * sc, 'Wsd': jax.random.normal(ks[6], (IS, H), jnp.float32) * sc}
    _L0_ffn_all = _L0_ffn_setup()
    _L0_ffn_in = {k: v for k, v in _L0_ffn_all.items() if k in ('Wg', 'e_bias', 'W_gate_up', 'W_down', 'Wsg', 'Wsu', 'Wsd')}
    del _L0_ffn_all

    def _L1_attn_setup():
        import jax, jax.numpy as jnp
        import numpy as np
        from jax import lax
        B, N, D = (8, 256, 192)
        H, Y = (12, 64)
        M = 768
        STEPS = 12
        ALPHA = 0.1
        BETA = 1.0 / np.sqrt(Y)
        EPS = 1e-05

        def _layer_norm(x, gamma, beta):
            mu = jnp.mean(x, axis=-1, keepdims=True)
            var = jnp.var(x, axis=-1, keepdims=True)
            return gamma * (x - mu) * lax.rsqrt(var + EPS) + beta

        def _energy(g, wq, wk, xi):
            q = jnp.einsum('hyd,bnd->bhny', wq, g)
            k = jnp.einsum('hyd,bnd->bhny', wk, g)
            logits = BETA * jnp.einsum('bhmy,bhny->bhmn', k, q)
            e_att = -(1.0 / BETA) * jnp.sum(jax.scipy.special.logsumexp(logits, axis=2))
            hid = jnp.einsum('md,bnd->bnm', xi, g)
            e_hn = -0.5 * jnp.sum(jnp.square(jax.nn.relu(hid)))
            return e_att + e_hn
        _energy_grad = jax.grad(_energy)
        key = jax.random.key(seed)
        k0, k1, k2, k3 = jax.random.split(key, 4)
        return {'x': jax.random.normal(k0, (B, N, D), dtype=jnp.float32), 'ln_gamma': jnp.ones((D,), dtype=jnp.float32), 'ln_beta': jnp.zeros((D,), dtype=jnp.float32), 'wq': jax.random.normal(k1, (H, Y, D), dtype=jnp.float32) * 0.02, 'wk': jax.random.normal(k2, (H, Y, D), dtype=jnp.float32) * 0.02, 'xi': jax.random.normal(k3, (M, D), dtype=jnp.float32) * 0.02}
    _L1_attn_all = _L1_attn_setup()
    _L1_attn_in = {k: v for k, v in _L1_attn_all.items() if k in ('ln_gamma', 'ln_beta', 'wq', 'wk', 'xi')}
    del _L1_attn_all

    def _L1_ffn_setup():
        import jax, jax.numpy as jnp
        import numpy as np
        CAPACITY_FACTOR = 1.25
        key = jax.random.key(seed)
        ks = jax.random.split(key, 5)
        B, S, D, F, E = (8, 512, 192, 768, 8)
        return {'x': jax.random.normal(ks[0], (B, S, D), jnp.float32), 'switch_w': jax.random.normal(ks[1], (D, E), jnp.float32) * 0.02, 'switch_b': jnp.zeros((E,), jnp.float32), 'w1': jax.random.normal(ks[2], (E, D, F), jnp.float32) * 0.02, 'b1': jnp.zeros((E, F), jnp.float32), 'w2': jax.random.normal(ks[3], (E, F, D), jnp.float32) * 0.02, 'b2': jnp.zeros((E, D), jnp.float32)}
    _L1_ffn_all = _L1_ffn_setup()
    _L1_ffn_in = {k: v for k, v in _L1_ffn_all.items() if k in ('switch_w', 'switch_b', 'w1', 'b1', 'w2', 'b2')}
    del _L1_ffn_all
    return {'x': x, 'L0_tok_conv_w': _L0_tok_in['conv_w'], 'L0_tok_conv_b': _L0_tok_in['conv_b'], 'L0_tok_ln1_g': _L0_tok_in['ln1_g'], 'L0_tok_ln1_b': _L0_tok_in['ln1_b'], 'L0_tok_qkv_w': _L0_tok_in['qkv_w'], 'L0_tok_out_w': _L0_tok_in['out_w'], 'L0_tok_out_b': _L0_tok_in['out_b'], 'L0_tok_ln2_g': _L0_tok_in['ln2_g'], 'L0_tok_ln2_b': _L0_tok_in['ln2_b'], 'L0_tok_ff1_w': _L0_tok_in['ff1_w'], 'L0_tok_ff1_b': _L0_tok_in['ff1_b'], 'L0_tok_ff2_w': _L0_tok_in['ff2_w'], 'L0_tok_ff2_b': _L0_tok_in['ff2_b'], 'L0_tok_lnf_g': _L0_tok_in['lnf_g'], 'L0_tok_lnf_b': _L0_tok_in['lnf_b'], 'L0_tok_head_w': _L0_tok_in['head_w'], 'L0_tok_head_b': _L0_tok_in['head_b'], 'L0_attn_w_in': _L0_attn_in['w_in'], 'L0_attn_w_conv': _L0_attn_in['w_conv'], 'L0_attn_b_conv': _L0_attn_in['b_conv'], 'L0_attn_w_xproj': _L0_attn_in['w_xproj'], 'L0_attn_w_dt': _L0_attn_in['w_dt'], 'L0_attn_b_dt': _L0_attn_in['b_dt'], 'L0_attn_A_log': _L0_attn_in['A_log'], 'L0_attn_D_param': _L0_attn_in['D_param'], 'L0_attn_w_out': _L0_attn_in['w_out'], 'L0_attn_w_norm': _L0_attn_in['w_norm'], 'L0_ffn_Wg': _L0_ffn_in['Wg'], 'L0_ffn_e_bias': _L0_ffn_in['e_bias'], 'L0_ffn_W_gate_up': _L0_ffn_in['W_gate_up'], 'L0_ffn_W_down': _L0_ffn_in['W_down'], 'L0_ffn_Wsg': _L0_ffn_in['Wsg'], 'L0_ffn_Wsu': _L0_ffn_in['Wsu'], 'L0_ffn_Wsd': _L0_ffn_in['Wsd'], 'L1_attn_ln_gamma': _L1_attn_in['ln_gamma'], 'L1_attn_ln_beta': _L1_attn_in['ln_beta'], 'L1_attn_wq': _L1_attn_in['wq'], 'L1_attn_wk': _L1_attn_in['wk'], 'L1_attn_xi': _L1_attn_in['xi'], 'L1_ffn_switch_w': _L1_ffn_in['switch_w'], 'L1_ffn_switch_b': _L1_ffn_in['switch_b'], 'L1_ffn_w1': _L1_ffn_in['w1'], 'L1_ffn_b1': _L1_ffn_in['b1'], 'L1_ffn_w2': _L1_ffn_in['w2'], 'L1_ffn_b2': _L1_ffn_in['b2']}

def reference(x, L0_tok_conv_w, L0_tok_conv_b, L0_tok_ln1_g, L0_tok_ln1_b, L0_tok_qkv_w, L0_tok_out_w, L0_tok_out_b, L0_tok_ln2_g, L0_tok_ln2_b, L0_tok_ff1_w, L0_tok_ff1_b, L0_tok_ff2_w, L0_tok_ff2_b, L0_tok_lnf_g, L0_tok_lnf_b, L0_tok_head_w, L0_tok_head_b, L0_attn_w_in, L0_attn_w_conv, L0_attn_b_conv, L0_attn_w_xproj, L0_attn_w_dt, L0_attn_b_dt, L0_attn_A_log, L0_attn_D_param, L0_attn_w_out, L0_attn_w_norm, L0_ffn_Wg, L0_ffn_e_bias, L0_ffn_W_gate_up, L0_ffn_W_down, L0_ffn_Wsg, L0_ffn_Wsu, L0_ffn_Wsd, L1_attn_ln_gamma, L1_attn_ln_beta, L1_attn_wq, L1_attn_wk, L1_attn_xi, L1_ffn_switch_w, L1_ffn_switch_b, L1_ffn_w1, L1_ffn_b1, L1_ffn_w2, L1_ffn_b2):
    import jax
    import jax.numpy as jnp

    def _L0_tok_ref(im, conv_w, conv_b, ln1_g, ln1_b, qkv_w, out_w, out_b, ln2_g, ln2_b, ff1_w, ff1_b, ff2_w, ff2_b, lnf_g, lnf_b, head_w, head_b):
        import jax, jax.numpy as jnp
        import numpy as np
        B, C, H, W = (8, 32, 128, 128)
        P = 8
        D = 128
        NH, DH = (8, 64)
        M = 512
        L = 2
        DOUT = 192
        INNER = NH * DH

        def _ln(x, g, b, eps=1e-05):
            mu = x.mean(-1, keepdims=True)
            xc = x - mu
            var = (xc * xc).mean(-1, keepdims=True)
            return xc * jax.lax.rsqrt(var + eps) * g + b

        def _forward(im, conv_w, conv_b, ln1_g, ln1_b, qkv_w, out_w, out_b, ln2_g, ln2_b, ff1_w, ff1_b, ff2_w, ff2_b, lnf_g, lnf_b, head_w, head_b):
            b, c, h, w = im.shape
            hp, wp = (h // P, w // P)
            patches = im.reshape(b, c, hp, P, wp, P)
            x = jnp.einsum('bchpwq,dcpq->bhwd', patches, conv_w)
            x = x.reshape(b, hp * wp, -1) + conv_b
            n = hp * wp
            scale = DH ** (-0.5)
            for i in range(ln1_g.shape[0]):
                y = _ln(x, ln1_g[i], ln1_b[i])
                qkv = y @ qkv_w[i]
                q, k, v = jnp.split(qkv, 3, axis=-1)
                to_heads = lambda t: t.reshape(b, n, NH, DH).transpose(0, 2, 1, 3)
                q, k, v = (to_heads(q), to_heads(k), to_heads(v))
                q = jax.nn.softmax(q, axis=-1) * scale
                k = jax.nn.softmax(k, axis=-2)
                ctx = jnp.einsum('bhnd,bhne->bhde', k, v)
                att = jnp.einsum('bhnd,bhde->bhne', q, ctx)
                att = att.transpose(0, 2, 1, 3).reshape(b, n, INNER)
                x = x + att @ out_w[i] + out_b[i]
                y = _ln(x, ln2_g[i], ln2_b[i])
                hdn = jax.nn.gelu(y @ ff1_w[i] + ff1_b[i], approximate=False)
                x = x + hdn @ ff2_w[i] + ff2_b[i]
            return _ln(x, lnf_g, lnf_b) @ head_w + head_b
        return _forward(im, conv_w, conv_b, ln1_g, ln1_b, qkv_w, out_w, out_b, ln2_g, ln2_b, ff1_w, ff1_b, ff2_w, ff2_b, lnf_g, lnf_b, head_w, head_b)

    def _L0_attn_ref(x, w_in, w_conv, b_conv, w_xproj, w_dt, b_dt, A_log, D_param, w_out, w_norm):
        import jax, jax.numpy as jnp
        import numpy as np
        B, L, D = (1, 512, 192)
        E = 2
        DIN = E * D
        N = 16
        K = 4
        R = (D + 15) // 16
        EPS = 1e-05
        b = x.shape[0]
        xz = jnp.einsum('bld,ed->ble', x, w_in)
        xin, z = jnp.split(xz, 2, axis=-1)
        xc = jax.lax.conv_general_dilated(xin.transpose(0, 2, 1), w_conv, (1,), [(K - 1, 0)], feature_group_count=DIN, dimension_numbers=('NCH', 'OIH', 'NCH'))
        xc = jax.nn.silu(xc.transpose(0, 2, 1) + b_conv)
        x_dbl = jnp.einsum('bld,ed->ble', xc, w_xproj)
        dt_in, Bm, Cm = jnp.split(x_dbl, [R, R + N], axis=-1)
        dt = jax.nn.softplus(jnp.einsum('blr,dr->bld', dt_in, w_dt) + b_dt)
        A = -jnp.exp(A_log)
        dA = jnp.exp(dt[..., None] * A)
        dBu = dt[..., None] * Bm[:, :, None, :] * xc[..., None]

        def step(h, inputs):
            a_t, b_t, c_t = inputs
            h = a_t * h + b_t
            return (h, jnp.einsum('bdn,bn->bd', h, c_t))
        h0 = jnp.zeros((b, DIN, N), xc.dtype)
        _, ys = jax.lax.scan(step, h0, (dA.transpose(1, 0, 2, 3), dBu.transpose(1, 0, 2, 3), Cm.transpose(1, 0, 2)))
        y = ys.transpose(1, 0, 2) + D_param * xc
        y = y * jax.nn.silu(z)
        out = jnp.einsum('ble,de->bld', y, w_out)
        r = out + x
        rms = r * jax.lax.rsqrt(jnp.mean(r * r, axis=-1, keepdims=True) + EPS)
        return rms * w_norm

    def _L0_ffn_ref(hidden_states, Wg, e_bias, W_gate_up, W_down, Wsg, Wsu, Wsd):
        import jax, jax.numpy as jnp
        import numpy as np
        E = 128
        I = 464
        IS = 928
        K = 6
        G = 1
        TG = 1
        SCALE = 2.5
        CAP = 192

        def moe_forward(hidden_states, Wg, e_bias, W_gate_up, W_down, Wsg, Wsu, Wsd):
            B, S, H = hidden_states.shape
            x = hidden_states.reshape(-1, H)
            T = x.shape[0]
            logits = x.astype(jnp.float32) @ Wg.T
            sig = jax.nn.sigmoid(logits)
            choice = sig + e_bias[None, :]
            grp = choice.reshape(T, G, E // G)
            group_scores = jax.lax.top_k(grp, 2)[0].sum(-1)
            gidx = jax.lax.top_k(group_scores, TG)[1]
            gmask = jnp.zeros((T, G), jnp.float32).at[jnp.arange(T)[:, None], gidx].set(1.0)
            smask = jnp.repeat(gmask, E // G, axis=1)
            scores_for_choice = jnp.where(smask > 0, choice, 0.0)
            topk_idx = jax.lax.top_k(scores_for_choice, K)[1]
            topk_w = jnp.take_along_axis(sig, topk_idx, axis=1)
            topk_w = topk_w / (topk_w.sum(-1, keepdims=True) + 1e-20)
            topk_w = topk_w * SCALE
            P = T * K
            flat_e = topk_idx.reshape(-1)
            order = jnp.argsort(flat_e)
            se = flat_e[order]
            counts = jax.ops.segment_sum(jnp.ones(P, jnp.int32), flat_e, num_segments=E)
            starts = jnp.cumsum(counts) - counts
            pos = jnp.arange(P) - starts[se]
            buf_idx = jnp.where(pos < CAP, se * CAP + pos, E * CAP)
            tok_of_pair = (order // K).astype(jnp.int32)
            w_of_pair = topk_w.reshape(-1)[order]
            token_buf = jnp.zeros((E * CAP,), jnp.int32).at[buf_idx].set(tok_of_pair, mode='drop')
            w_buf = jnp.zeros((E * CAP,), x.dtype).at[buf_idx].set(w_of_pair.astype(x.dtype), mode='drop')
            xb = x[token_buf].reshape(E, CAP, H)
            gu = jnp.einsum('ech,ehf->ecf', xb, W_gate_up)
            g, u = jnp.split(gu, 2, axis=-1)
            inter = jax.nn.silu(g) * u
            yb = jnp.einsum('eci,eih->ech', inter, W_down)
            yb = yb * w_buf.reshape(E, CAP, 1)
            routed = jnp.zeros((T, H), x.dtype).at[token_buf].add(yb.reshape(E * CAP, H))
            shared = jax.nn.silu(x @ Wsg) * (x @ Wsu) @ Wsd
            return (routed + shared).reshape(B, S, H)
        return moe_forward(hidden_states, Wg, e_bias, W_gate_up, W_down, Wsg, Wsu, Wsd)

    def _L1_attn_ref(x, ln_gamma, ln_beta, wq, wk, xi):
        import jax, jax.numpy as jnp
        import numpy as np
        from jax import lax
        B, N, D = (8, 256, 192)
        H, Y = (12, 64)
        M = 768
        STEPS = 12
        ALPHA = 0.1
        BETA = 1.0 / np.sqrt(Y)
        EPS = 1e-05

        def _layer_norm(x, gamma, beta):
            mu = jnp.mean(x, axis=-1, keepdims=True)
            var = jnp.var(x, axis=-1, keepdims=True)
            return gamma * (x - mu) * lax.rsqrt(var + EPS) + beta

        def _energy(g, wq, wk, xi):
            q = jnp.einsum('hyd,bnd->bhny', wq, g)
            k = jnp.einsum('hyd,bnd->bhny', wk, g)
            logits = BETA * jnp.einsum('bhmy,bhny->bhmn', k, q)
            e_att = -(1.0 / BETA) * jnp.sum(jax.scipy.special.logsumexp(logits, axis=2))
            hid = jnp.einsum('md,bnd->bnm', xi, g)
            e_hn = -0.5 * jnp.sum(jnp.square(jax.nn.relu(hid)))
            return e_att + e_hn
        _energy_grad = jax.grad(_energy)

        def step(x, _):
            g = _layer_norm(x, ln_gamma, ln_beta)
            grad = _energy_grad(g, wq, wk, xi)
            return (x - ALPHA * grad, None)
        x, _ = lax.scan(step, x, None, length=STEPS)
        return x

    def _L1_ffn_ref(x, switch_w, switch_b, w1, b1, w2, b2):
        import jax, jax.numpy as jnp
        import numpy as np
        CAPACITY_FACTOR = 1.25
        B, S, D = x.shape
        E = w1.shape[0]
        xf = x.reshape(-1, D)
        N = xf.shape[0]
        capacity = int(CAPACITY_FACTOR * N / E)
        probs = jax.nn.softmax(xf @ switch_w + switch_b, axis=-1)
        prob_max = jnp.max(probs, axis=-1)
        routes = jnp.argmax(probs, axis=-1)
        sort_idx = jnp.lexsort((-prob_max, routes))
        counts = jnp.bincount(routes, length=E)
        starts = jnp.concatenate([jnp.zeros((1,), counts.dtype), jnp.cumsum(counts)[:-1]])
        rank_sorted = jnp.arange(N) - starts[routes[sort_idx]]
        rank = jnp.zeros((N,), jnp.int32).at[sort_idx].set(rank_sorted.astype(jnp.int32))
        keep = rank < capacity
        dest_e = jnp.where(keep, routes, E)
        dest_c = jnp.where(keep, rank, 0)
        buf = jnp.zeros((E + 1, capacity, D), xf.dtype).at[dest_e, dest_c].set(xf)
        h = jax.nn.gelu(jnp.einsum('ecd,edf->ecf', buf[:E], w1) + b1[:, None, :], approximate=False)
        o = jnp.einsum('ecf,efd->ecd', h, w2) + b2[:, None, :]
        y_exp = o[routes, dest_c]
        y = jnp.where(keep[:, None], y_exp, xf)
        out = y * prob_max[:, None]
        return out.reshape(B, S, D)
    h = _L0_tok_ref(x, L0_tok_conv_w, L0_tok_conv_b, L0_tok_ln1_g, L0_tok_ln1_b, L0_tok_qkv_w, L0_tok_out_w, L0_tok_out_b, L0_tok_ln2_g, L0_tok_ln2_b, L0_tok_ff1_w, L0_tok_ff1_b, L0_tok_ff2_w, L0_tok_ff2_b, L0_tok_lnf_g, L0_tok_lnf_b, L0_tok_head_w, L0_tok_head_b)
    h = h + _L0_attn_ref(_layernorm(h, axis=-1), L0_attn_w_in, L0_attn_w_conv, L0_attn_b_conv, L0_attn_w_xproj, L0_attn_w_dt, L0_attn_b_dt, L0_attn_A_log, L0_attn_D_param, L0_attn_w_out, L0_attn_w_norm)
    h = h + _L0_ffn_ref(_layernorm(h, axis=-1), L0_ffn_Wg, L0_ffn_e_bias, L0_ffn_W_gate_up, L0_ffn_W_down, L0_ffn_Wsg, L0_ffn_Wsu, L0_ffn_Wsd)
    h = h + _L1_attn_ref(_layernorm(h, axis=-1), L1_attn_ln_gamma, L1_attn_ln_beta, L1_attn_wq, L1_attn_wk, L1_attn_xi)
    h = h + _L1_ffn_ref(_layernorm(h, axis=-1), L1_ffn_switch_w, L1_ffn_switch_b, L1_ffn_w1, L1_ffn_b1, L1_ffn_w2, L1_ffn_b2)
    return h

_drawn_inputs = setup_inputs


def setup_inputs(seed=0):
    import zlib

    import numpy as np

    out = dict(_drawn_inputs(seed))
    spreads = {'L0_tok_conv_b': (0.0, 0.1),
     'L0_tok_ln1_g': (1.0, 0.6),
     'L0_tok_ln1_b': (0.0, 0.8),
     'L0_tok_out_b': (0.0, 0.1),
     'L0_tok_ln2_g': (1.0, 0.6),
     'L0_tok_ln2_b': (0.0, 0.732),
     'L0_tok_ff1_b': (0.0, 0.1),
     'L0_tok_ff2_b': (0.0, 0.1),
     'L0_tok_lnf_g': (1.0, 0.2),
     'L0_tok_lnf_b': (0.0, 0.1),
     'L0_tok_head_b': (0.0, 0.1),
     'L0_attn_D_param': (1.0, 0.2),
     'L0_attn_w_norm': (1.0, 0.2),
     'L0_ffn_e_bias': (0.0, 0.419),
     'L1_attn_ln_gamma': (1.0, 0.6),
     'L1_attn_ln_beta': (0.0, 0.421),
     'L1_ffn_switch_b': (0.0, 0.403),
     'L1_ffn_b1': (0.0, 0.8),
     'L1_ffn_b2': (0.0, 0.8)}
    factors = {'L0_tok_qkv_w': 8.0,
     'L0_tok_out_w': 8.0,
     'L0_attn_b_conv': 5.201,
     'L0_attn_b_dt': 8.0,
     'L0_ffn_Wg': 4.539,
     'L0_ffn_W_gate_up': 3.878,
     'L0_ffn_W_down': 3.835,
     'L0_ffn_Wsg': 2.745,
     'L0_ffn_Wsu': 2.756,
     'L0_ffn_Wsd': 2.705,
     'L1_ffn_w1': 8.0,
     'L1_ffn_w2': 8.0}
    for name, (base, spread) in spreads.items():
        noise = np.random.default_rng([zlib.crc32(name.encode()), seed]).standard_normal(out[name].shape)
        drawn = base * np.exp(spread * noise) if base else spread * noise
        out[name] = jnp.asarray(drawn.astype(out[name].dtype))
    for name, factor in factors.items():
        out[name] = (out[name] * factor).astype(out[name].dtype)
    return out
```

```python
from contextlib import ExitStack

import numpy as np

import concourse.bass as bass
from concourse import mybir
from concourse.alu_op_type import AluOpType as ALU

fp32 = mybir.dt.float32
u32 = mybir.dt.uint32
ACT = mybir.ActivationFunctionType
AX = mybir.AxisListType

P = 128
BATCH, SEQ = 2, 256
NT = BATCH * SEQ
T = NT // P
TB = SEQ // P
D = 192
DK, DC = 96, 2
EPS = 1e-5
BANK = 512


class Shared:

    def __init__(self, nc, ctx):
        self.nc = nc
        self.h = ctx.enter_context(nc.sbuf_tensor("h", [P, T, D], fp32))
        self.u = ctx.enter_context(nc.sbuf_tensor("u", [P, T, D], fp32))
        self.uT = ctx.enter_context(nc.sbuf_tensor("uT", [DK, DC, NT], fp32))
        self.ident = ctx.enter_context(nc.sbuf_tensor("ident", [P, P], fp32))
        self.ones = ctx.enter_context(nc.sbuf_tensor("ones", [P, P], fp32))
        self.neghalf = ctx.enter_context(nc.sbuf_tensor("neghalf", [P, T], fp32))
        self.stats = ctx.enter_context(nc.sbuf_tensor("stats", [P, T, 6], fp32))
        self.mv = ctx.enter_context(nc.sbuf_tensor("mv", [P, T, 2], fp32))
        self.var = ctx.enter_context(nc.sbuf_tensor("var", [P, T], fp32))
        self.rstd = ctx.enter_context(nc.sbuf_tensor("rstd", [P, T], fp32))
        self.ps = ctx.enter_context(nc.psum_tensor("ps", [P, 8, BANK], fp32))
        self.stage_semaphores = []

    def stage_semaphore(self, name):
        self.stage_semaphores.append(self.nc.alloc_semaphore(name))
        return self.stage_semaphores[-1]

    def end_stage(self):
        self.nc.clear_and_free_semaphores(self.stage_semaphores)
        self.stage_semaphores = []
        self.nc.all_engine_barrier()


def setup_stage(nc, s):
    consts_set = s.stage_semaphore("consts_set")
    with nc.Block() as block:
        @block.gpsimd
        def _(pool):
            pool.memset(s.ident[:, :], 0.0).then_inc(consts_set, 1)
            pool.memset(s.ones[:, :], 1.0).then_inc(consts_set, 1)
            pool.memset(s.neghalf[:, :], -0.5).then_inc(consts_set, 1)
            pool.wait_ge(consts_set, 3)
            pool.affine_select(out=s.ident[:, :], in_=s.ident[:, :], compare_op=ALU.not_equal,
                               fill=1.0, base=0, pattern=[[-1, P]], channel_multiplier=1)


def ln_vector(dve, s, y, x, n, var_ready, rstd_ready):
    for t in range(T):
        dve.bn_stats(s.stats[:, t, :], x[:, t, :])
    dve.drain()
    for t in range(T):
        dve.bn_aggr(s.mv[:, t, :], s.stats[:, t, :])
    dve.drain()
    dve.tensor_scalar(s.var[:, :], s.mv[:, :, 1], EPS, None, ALU.add).then_inc(var_ready, 1)
    dve.wait_ge(rstd_ready, n + 1)
    for t in range(T):
        last = dve.tensor_scalar(y[:, t, :], x[:, t, :], s.mv[:, t, 0:1], s.rstd[:, t:t + 1],
                                 ALU.subtract, ALU.mult)
    return last


def ln_pool(pool, s, n, var_ready, rstd_ready):
    pool.wait_ge(var_ready, n + 1)
    pool.tensor_tensor(s.rstd[:, :], s.var[:, :], s.neghalf[:, :], ALU.pow).then_inc(rstd_ready, 1)


def transpose_u(pe, s):
    for c in range(DC):
        for t in range(T):
            last = pe.transpose(s.ps[0:DK, c, t * P:(t + 1) * P], s.u[:, t, c * DK:(c + 1) * DK],
                                s.ident[:, :])
    return last


TD = 128
HEADS, DH = 8, 64
INNER = HEADS * DH
IC = INNER // P
KC = 2048 // P
FM = 512
FC = FM // P
LAYERS = 2


def tok_stage(nc, s, a):
    ctx = ExitStack()
    with ctx:
        def sb(name, shape):
            return ctx.enter_context(nc.sbuf_tensor(name, shape, fp32))

        def sem(name):
            return s.stage_semaphore(name)

        patches = sb("patches", [P, KC, NT])
        conv_w = sb("conv_w", [P, KC, TD])
        conv_b = sb("conv_b", [1, TD])
        x = sb("tok_x", [P, T, TD])
        y = sb("tok_y", [P, T, TD])
        yT = sb("tok_yT", [P, NT])
        cols = sb("tok_cols", [P, 8])
        rows = sb("tok_rows", [1, 2, TD])
        wqkv = sb("tok_wqkv", [P, 3 * INNER])
        wo = sb("tok_wo", [P, IC, TD])
        w1 = sb("tok_w1", [P, FM])
        w2 = sb("tok_w2", [P, FC, TD])
        lnf = sb("tok_lnf", [P, 2])
        head_w = sb("tok_head_w", [P, D])
        head_b = sb("tok_head_b", [1, D])
        kT = sb("tok_kT", [P, IC, NT])
        kneg = sb("tok_kneg", [P, IC, BATCH])
        ksum = sb("tok_ksum", [P, IC, BATCH])
        krec = sb("tok_krec", [P, IC, BATCH])
        k = sb("tok_k", [P, T, INNER])
        q = sb("tok_q", [P, T, INNER])
        qmax = sb("tok_qmax", [P, T, HEADS])
        qsum = sb("tok_qsum", [P, T, HEADS])
        qT = sb("tok_qT", [P, IC, NT])
        v = sb("tok_v", [P, T, INNER])
        ctxT = sb("tok_ctx", [P, BATCH, IC, P])
        attT = sb("tok_attT", [P, IC, NT])
        hidT = sb("tok_hidT", [P, FC, NT])
        ps = s.ps

        patch_in = [sem(f"patch_in{g}") for g in range(4)]
        head_in = sem("tok_head_in")
        weights_in = sem("tok_weights_in")
        layer_done = sem("tok_layer_done")
        embedded = sem("tok_embedded")
        x_ready = sem("tok_x_ready")
        var_ready, rstd_ready = sem("tok_var_ready"), sem("tok_rstd_ready")
        y_ready = sem("tok_y_ready")
        y_transposed = sem("tok_y_transposed")
        yT_ready = sem("tok_yT_ready")
        kT_scores = sem("tok_kT_scores")
        k_max = sem("tok_k_max")
        k_exp = sem("tok_k_exp")
        q_scores = sem("tok_q_scores")
        q_shifted = sem("tok_q_shifted")
        q_exp = sem("tok_q_exp")
        q_normed = sem("tok_q_normed")
        v_product = sem("tok_v_product")
        v_ready = sem("tok_v_ready")
        k_transposed = sem("tok_k_transposed")
        k_ready = sem("tok_k_ready")
        q_transposed = sem("tok_q_transposed")
        qT_ready = sem("tok_qT_ready")
        ctx_zeroed = sem("tok_ctx_zeroed")
        ctx_product = sem("tok_ctx_product")
        ctx_ready = sem("tok_ctx_ready")
        att_product = sem("tok_att_product")
        att_ready = sem("tok_att_ready")
        out_product = sem("tok_out_product")
        hid_product = sem("tok_hid_product")
        hid_ready = sem("tok_hid_ready")
        ff_product = sem("tok_ff_product")
        head_product = sem("tok_head_product")

        with nc.Block() as block:
            @block.sync
            def _(sp):
                patch_v = a["patches"].rearrange("(k p) t -> p k t", p=P)
                conv_v = a["conv_w"].rearrange("(k p) d -> p k d", p=P)
                for g in range(4):
                    lot = slice(g * KC // 4, (g + 1) * KC // 4)
                    sp.dma_start(conv_w[:, lot, :], conv_v[:, lot, :]).then_inc(patch_in[g], 16)
                    sp.dma_start(patches[:, lot, :], patch_v[:, lot, :]).then_inc(patch_in[g], 16)
                sp.dma_start(conv_b[:, :], a["conv_b"]).then_inc(head_in, 16)
                sp.dma_start(lnf[:, :], a["tok_lnf"]).then_inc(head_in, 16)
                sp.dma_start(head_w[:, :], a["head_w"]).then_inc(head_in, 16)
                sp.dma_start(head_b[:, :], a["head_b"]).then_inc(head_in, 16)
                with sp.Fori(0, LAYERS) as l:
                    sp.wait_ge(layer_done, l)
                    sp.dma_start(cols[:, :], a["tok_cols"][l]).then_inc(weights_in, 16)
                    sp.dma_start(wqkv[:, :], a["qkv_w"][l]).then_inc(weights_in, 16)
                    sp.dma_start(rows[:, :, :], a["tok_rows"][l]).then_inc(weights_in, 16)
                    sp.dma_start(wo[:, :, :], a["out_w"][l].rearrange("(c p) d -> p c d", p=P)).then_inc(weights_in, 16)
                    sp.dma_start(w1[:, :], a["ff1_w"][l]).then_inc(weights_in, 16)
                    sp.dma_start(w2[:, :, :], a["ff2_w"][l].rearrange("(c p) d -> p c d", p=P)).then_inc(weights_in, 16)

            @block.gpsimd
            def _(pool):
                pool.memset(ctxT[:, :, :, :], 0.0).then_inc(ctx_zeroed, 1)
                with pool.Fori(0, 2 * LAYERS + 1) as n:
                    ln_pool(pool, s, n, var_ready, rstd_ready)

            @block.tensor
            def _(pe):
                for g in range(4):
                    pe.wait_ge(patch_in[g], 32)
                    for kc in range(g * KC // 4, (g + 1) * KC // 4):
                        for t in range(T):
                            pe.matmul(ps[:, t, 0:TD], lhsT=patches[:, kc, t * P:(t + 1) * P],
                                      rhs=conv_w[:, kc, :], start=(kc == 0), stop=False)
                pe.wait_ge(head_in, 64)
                for t in range(T):
                    last = pe.matmul(ps[:, t, 0:TD], lhsT=s.ones[0:1, :], rhs=conv_b[:, :],
                                     start=False, stop=True)
                last.then_inc(embedded, 1)

                def transpose_y(n):
                    pe.wait_ge(y_ready, n + 1)
                    for t in range(T):
                        last = pe.transpose(ps[:, 0, t * P:(t + 1) * P], y[:, t, :], s.ident[:, :])
                    last.then_inc(y_transposed, 1)
                    pe.wait_ge(yT_ready, n + 1)

                with pe.Fori(0, LAYERS) as l:
                    transpose_y(2 * l)
                    pe.wait_ge(weights_in, l * 96 + 96)
                    for c in range(IC):
                        pe.matmul(ps[:, 1 + c, :], lhsT=wqkv[:, INNER + c * P:INNER + (c + 1) * P],
                                  rhs=yT[:, :], start=True, stop=True).then_inc(kT_scores, 1)
                    for t in range(T):
                        pe.matmul(ps[:, (5 + t) % 8, :], lhsT=yT[:, t * P:(t + 1) * P],
                                  rhs=wqkv[:, 0:INNER], start=True, stop=True).then_inc(q_scores, 1)
                    for t in range(T):
                        pe.wait_ge(k_exp, l * IC + t + 1)
                        pe.matmul(ps[:, 1 + t, :], lhsT=yT[:, t * P:(t + 1) * P],
                                  rhs=wqkv[:, 2 * INNER:3 * INNER], start=True, stop=True).then_inc(v_product, 1)
                    for t in range(T):
                        pe.wait_ge(q_shifted, l * T + t + 1)
                        for c in range(IC):
                            last = pe.transpose(ps[:, (5 + t) % 8, c * P:(c + 1) * P],
                                                kT[:, c, t * P:(t + 1) * P], s.ident[:, :])
                        last.then_inc(k_transposed, 1)
                    for c in range(IC):
                        pe.wait_ge(q_normed, l * T + T)
                        pe.wait_ge(v_ready, l * T + c + 1)
                        for t in range(T):
                            last = pe.transpose(ps[:, 1 + c, t * P:(t + 1) * P],
                                                q[:, t, c * P:(c + 1) * P], s.ident[:, :])
                        last.then_inc(q_transposed, 1)
                    pe.wait_ge(k_ready, l * T + T)
                    pe.wait_ge(v_ready, l * T + T)
                    for b in range(BATCH):
                        for c in range(IC):
                            for i in range(TB):
                                last = pe.matmul(ps[:, 5 + b, c * P:(c + 1) * P],
                                                 lhsT=k[:, b * TB + i, c * P:(c + 1) * P],
                                                 rhs=v[:, b * TB + i, c * P:(c + 1) * P],
                                                 start=(i == 0), stop=(i == TB - 1))
                        last.then_inc(ctx_product, 1)
                    pe.wait_ge(ctx_ready, l + 1)
                    for c in range(IC):
                        pe.wait_ge(qT_ready, l * IC + c + 1)
                        for b in range(BATCH):
                            last = pe.matmul(ps[:, 1 + c, b * SEQ:(b + 1) * SEQ], lhsT=ctxT[:, b, c, :],
                                             rhs=qT[:, c, b * SEQ:(b + 1) * SEQ], start=True, stop=True)
                        last.then_inc(att_product, 1)
                    pe.wait_ge(att_ready, l * IC + IC)
                    for t in range(T):
                        for c in range(IC):
                            pe.matmul(ps[:, 7, t * TD:(t + 1) * TD], lhsT=attT[:, c, t * P:(t + 1) * P],
                                      rhs=wo[:, c, :], start=(c == 0), stop=False)
                        last = pe.matmul(ps[:, 7, t * TD:(t + 1) * TD], lhsT=s.ones[0:1, :],
                                         rhs=rows[:, 0, :], start=False, stop=True)
                    last.then_inc(out_product, 1)
                    transpose_y(2 * l + 1)
                    for m in range(FC):
                        pe.matmul(ps[:, 1 + m, :], lhsT=w1[:, m * P:(m + 1) * P], rhs=yT[:, :],
                                  start=True, stop=True).then_inc(hid_product, 1)
                    pe.wait_ge(hid_ready, l * FC + FC)
                    for t in range(T):
                        for m in range(FC):
                            pe.matmul(ps[:, 7, t * TD:(t + 1) * TD], lhsT=hidT[:, m, t * P:(t + 1) * P],
                                      rhs=w2[:, m, :], start=(m == 0), stop=False)
                        last = pe.matmul(ps[:, 7, t * TD:(t + 1) * TD], lhsT=s.ones[0:1, :],
                                         rhs=rows[:, 1, :], start=False, stop=True)
                    last.then_inc(ff_product, 1)
                transpose_y(2 * LAYERS)
                for t in range(T):
                    pe.matmul(ps[:, 1 + t, 0:D], lhsT=yT[:, t * P:(t + 1) * P], rhs=head_w[:, :],
                              start=True, stop=False)
                    pe.matmul(ps[:, 1 + t, 0:D], lhsT=s.ones[0:1, :], rhs=head_b[:, :],
                              start=False, stop=True).then_inc(head_product, 1)

            @block.vector
            def _(dve):
                dve.wait_ge(embedded, 1)
                dve.tensor_copy(x[:, :, :], ps[:, 0:T, 0:TD])
                dve.drain()

                def normalise(n, gain, shift):
                    ln_vector(dve, s, y, x, n, var_ready, rstd_ready).then_inc(y_ready, 1)
                    dve.wait_ge(y_transposed, n + 1)
                    dve.tensor_scalar(yT[:, :], ps[:, 0, :], gain, shift, ALU.mult, ALU.add).then_inc(yT_ready, 1)

                with dve.Fori(0, LAYERS) as l:
                    dve.wait_ge(weights_in, l * 96 + 96)
                    normalise(2 * l, cols[:, 0:1], cols[:, 1:2])
                    for c in range(IC):
                        dve.wait_ge(kT_scores, l * IC + c + 1)
                        dve.tensor_reduce(kneg[:, c, :], ps[:, 1 + c, :].rearrange("p (b n) -> p b n", b=BATCH),
                                          axis=AX.X, op=ALU.max, negate=True).then_inc(k_max, 1)
                    for t in range(T):
                        bank = ps[:, (5 + t) % 8, :].rearrange("p (h d) -> p h d", h=HEADS)
                        dve.wait_ge(q_scores, l * T + t + 1)
                        dve.reduce_max(qmax[:, t, :], bank, AX.X)
                        dve.drain()
                        dve.tensor_tensor(q[:, t, :].rearrange("p (h d) -> p h d", h=HEADS), bank,
                                          qmax[:, t, :].unsqueeze(2).broadcast_to((P, HEADS, DH)),
                                          ALU.subtract).then_inc(q_shifted, 1)
                    for t in range(T):
                        head = q[:, t, :].rearrange("p (h d) -> p h d", h=HEADS)
                        dve.wait_ge(q_exp, l * T + t + 1)
                        dve.reduce_sum(qsum[:, t, :], head, AX.X)
                        dve.drain()
                        dve.reciprocal(qsum[:, t, :], qsum[:, t, :])
                        dve.drain()
                        dve.tensor_tensor(head, head, qsum[:, t, :].unsqueeze(2).broadcast_to((P, HEADS, DH)),
                                          ALU.mult).then_inc(q_normed, 1)
                    dve.wait_ge(k_exp, l * IC + IC)
                    dve.reciprocal(krec[:, :, :], ksum[:, :, :])
                    dve.drain()
                    dve.tensor_scalar(krec[:, :, :], krec[:, :, :], float(DH) ** -0.5, None, ALU.mult)
                    for t in range(T):
                        dve.wait_ge(k_transposed, l * T + t + 1)
                        dve.tensor_copy(k[:, t, :], ps[:, (5 + t) % 8, :]).then_inc(k_ready, 1)
                    for c in range(IC):
                        dve.wait_ge(q_transposed, l * IC + c + 1)
                        dve.tensor_copy(qT[:, c, :], ps[:, 1 + c, :]).then_inc(qT_ready, 1)
                    dve.wait_ge(ctx_zeroed, 1)
                    dve.wait_ge(ctx_product, l * BATCH + BATCH)
                    for b in range(BATCH):
                        for c in range(IC):
                            for r in (slice(0, DH), slice(DH, P)):
                                last = dve.tensor_scalar(ctxT[r, b, c, r], ps[r, 5 + b, c * P + r.start:c * P + r.stop],
                                                         krec[r, c, b:b + 1], None, ALU.mult)
                    last.then_inc(ctx_ready, 1)
                    for c in range(IC):
                        dve.wait_ge(att_product, l * IC + c + 1)
                        dve.tensor_copy(attT[:, c, :], ps[:, 1 + c, :]).then_inc(att_ready, 1)
                    dve.wait_ge(out_product, l + 1)
                    dve.tensor_tensor(x[:, :, :], x[:, :, :], ps[:, 7, :].rearrange("p (t d) -> p t d", t=T), ALU.add)
                    dve.drain()
                    normalise(2 * l + 1, cols[:, 2:3], cols[:, 3:4])
                    dve.wait_ge(ff_product, l + 1)
                    dve.tensor_tensor(x[:, :, :], x[:, :, :], ps[:, 7, :].rearrange("p (t d) -> p t d", t=T),
                                      ALU.add).then_inc(layer_done, 1)
                    dve.wait_ge(layer_done, l + 1)
                dve.wait_ge(head_in, 64)
                normalise(2 * LAYERS, lnf[:, 0:1], lnf[:, 1:2])
                for t in range(T):
                    dve.wait_ge(head_product, t + 1)
                    dve.tensor_copy(s.h[:, t, :], ps[:, 1 + t, 0:D])

            @block.scalar
            def _(act):
                with act.Fori(0, LAYERS) as l:
                    for c in range(IC):
                        act.wait_ge(k_max, l * IC + c + 1)
                        for b in range(BATCH):
                            last = act.activation(kT[:, c, b * SEQ:(b + 1) * SEQ], ps[:, 1 + c, b * SEQ:(b + 1) * SEQ],
                                                  ACT.Exp, bias=kneg[:, c, b:b + 1], accum_out=ksum[:, c, b:b + 1])
                        last.then_inc(k_exp, 1)
                    for t in range(T):
                        act.wait_ge(q_shifted, l * T + t + 1)
                        act.activation(q[:, t, :], q[:, t, :], ACT.Exp).then_inc(q_exp, 1)
                    for t in range(T):
                        act.wait_ge(v_product, l * T + t + 1)
                        act.copy(v[:, t, :], ps[:, 1 + t, :]).then_inc(v_ready, 1)
                    for m in range(FC):
                        act.wait_ge(hid_product, l * FC + m + 1)
                        act.activation(hidT[:, m, :], ps[:, 1 + m, :], ACT.Gelu, bias=cols[:, 4 + m:5 + m]).then_inc(hid_ready, 1)


DIN = 2 * D
MC = DIN // P
NS = 16
KW = 4
R = (D + 15) // 16
PAD = KW - 1


def mamba_stage(nc, s, a):
    ctx = ExitStack()
    with ctx:
        def sb(name, shape):
            return ctx.enter_context(nc.sbuf_tensor(name, shape, fp32))

        def sem(name):
            return s.stage_semaphore(name)

        w_in = sb("mb_w_in", [DK, DC, 2 * DIN])
        cols = sb("mb_cols", [P, MC, KW + 3])
        a_log = sb("mb_a_log", [P, MC, NS])
        w_x = sb("mb_w_x", [P, MC, R + 2 * NS])
        w_dt = sb("mb_w_dt", [R, DIN])
        w_out = sb("mb_w_out", [P, MC, D])
        w_norm = sb("mb_w_norm", [P, D])
        xp = sb("mb_xp", [P, MC, BATCH, PAD + SEQ])
        xc = sb("mb_xc", [P, MC, NT])
        z = sb("mb_z", [P, MC, NT])
        dt_in = sb("mb_dt_in", [R, NT])
        bc = sb("mb_bc", [2 * NS, NT])
        dt = sb("mb_dt", [P, MC, NT])
        soft = sb("mb_soft", [P, MC, NT])
        dtx = sb("mb_dtx", [P, MC, NT])
        b_all = sb("mb_b_all", [P, 2, NT])
        c_all = sb("mb_c_all", [P, 2, NT])
        decay = sb("mb_decay", [P, 2, MC, NT])
        drive = sb("mb_drive", [P, MC, NT])
        state = sb("mb_state", [P, MC, NT])
        out_n = sb("mb_out_n", [P, MC, NT])
        r = sb("mb_r", [P, T, D])
        sq = sb("mb_sq", [P, T, D])
        bc_dram = nc.dram_tensor("bc_rows", [2 * NS, NT], fp32).ap()
        ps = s.ps

        weights_in = sem("mb_weights_in")
        var_ready, rstd_ready = sem("mb_var_ready"), sem("mb_rstd_ready")
        pad_zeroed = sem("mb_pad_zeroed")
        u_ready = sem("mb_u_ready")
        u_transposed = sem("mb_u_transposed")
        uT_ready = sem("mb_uT_ready")
        x_product = sem("mb_x_product")
        conv_done = sem("mb_conv_done")
        xc_ready = sem("mb_xc_ready")
        dbc_product = sem("mb_dbc_product")
        dbc_ready = sem("mb_dbc_ready")
        bc_stored = sem("mb_bc_stored")
        dt_product = sem("mb_dt_product")
        biased = sem("mb_biased")
        log_ready = sem("mb_log_ready")
        dt_ready = sem("mb_dt_ready")
        a_exp = sem("mb_a_exp")
        a_ready = sem("mb_a_ready")
        skip_ready = sem("mb_skip_ready")
        bc_in = [sem(f"mb_bc_in{k}") for k in range(2)]
        decay_ready = sem("mb_decay_ready")
        decay_free = sem("mb_decay_free")
        bc_free = sem("mb_bc_free")
        out_ready = sem("mb_out_ready")
        out_summed = sem("mb_out_summed")
        gated = sem("mb_gated")
        out_product = sem("mb_out_product")

        with nc.Block() as block:
            @block.sync
            def _(sp):
                sp.dma_start(w_in[:, :, :], a["mb_w_in"].rearrange("(c p) e -> p c e", p=DK)).then_inc(weights_in, 16)
                sp.dma_start(cols[:, :, :], a["mb_cols"].rearrange("(c p) k -> p c k", p=P)).then_inc(weights_in, 16)
                sp.dma_start(a_log[:, :, :], a["mb_a_log"].rearrange("(c p) k -> p c k", p=P)).then_inc(weights_in, 16)
                sp.dma_start(w_x[:, :, :], a["mb_w_x"].rearrange("(c p) k -> p c k", p=P)).then_inc(weights_in, 16)
                sp.dma_start(w_dt[:, :], a["mb_w_dt"]).then_inc(weights_in, 16)
                sp.dma_start(w_out[:, :, :], a["mb_w_out"].rearrange("(c p) k -> p c k", p=P)).then_inc(weights_in, 16)
                sp.dma_start(w_norm[:, :], a["mb_w_norm"].broadcast_to((P, D))).then_inc(weights_in, 16)
                sp.wait_ge(dbc_ready, 2)
                sp.dma_start(bc_dram, bc[:, :]).then_inc(bc_stored, 16)
                sp.wait_ge(bc_stored, 16)
                with sp.Fori(0, NS // 2) as i:
                    for k in range(2):
                        sp.wait_ge(bc_free, i * 2 + k)
                        sp.dma_start(b_all[:, k, :], bc_dram[bass.ds(i * 2 + k, 1), :].broadcast_to((P, NT))).then_inc(bc_in[k], 16)
                        sp.dma_start(c_all[:, k, :], bc_dram[bass.ds(i * 2 + k + NS, 1), :].broadcast_to((P, NT))).then_inc(bc_in[k], 16)

            @block.gpsimd
            def _(pool):
                pool.memset(xp[:, :, :, 0:PAD], 0.0).then_inc(pad_zeroed, 1)
                for n in range(2):
                    ln_pool(pool, s, n, var_ready, rstd_ready)

            @block.tensor
            def _(pe):
                pe.wait_ge(u_ready, 1)
                transpose_u(pe, s).then_inc(u_transposed, 1)
                pe.wait_ge(uT_ready, 1)
                pe.wait_ge(weights_in, 7 * 16)
                for c in range(2 * MC):
                    for kc in range(DC):
                        last = pe.matmul(ps[:, 2 + c, :], lhsT=w_in[:, kc, c * P:(c + 1) * P], rhs=s.uT[:, kc, :],
                                         start=(kc == 0), stop=(kc == DC - 1))
                    last.then_inc(x_product, 1)
                pe.wait_ge(xc_ready, MC)
                for bank, lo, hi in ((0, 0, R), (1, R, R + 2 * NS)):
                    for c in range(MC):
                        last = pe.matmul(ps[0:hi - lo, bank, :], lhsT=w_x[:, c, lo:hi], rhs=xc[:, c, :],
                                         start=(c == 0), stop=(c == MC - 1))
                    last.then_inc(dbc_product, 1)
                pe.wait_ge(dbc_ready, 1)
                for c in range(MC):
                    pe.matmul(ps[:, 2 + c, :], lhsT=w_dt[:, c * P:(c + 1) * P], rhs=dt_in[:, :],
                              start=True, stop=True).then_inc(dt_product, 1)
                pe.wait_ge(xc_ready, 2 * MC)
                for c in range(MC):
                    pe.wait_ge(skip_ready, c + 1)
                    pe.matmul(ps[:, 5 + c, :], lhsT=s.ident[:, :], rhs=soft[:, c, :], start=True, stop=False,
                              skip_group_check=True)
                with pe.Fori(0, NS) as n:
                    for c in range(MC):
                        pe.wait_ge(out_ready, n * MC + c + 1)
                        pe.matmul(ps[:, 5 + c, :], lhsT=s.ident[:, :], rhs=out_n[:, c, :], start=False, stop=False,
                                  skip_group_check=True).then_inc(out_summed, 1)
                pe.wait_ge(gated, 1)
                for t in range(T):
                    for c in range(MC):
                        last = pe.matmul(ps[:, t, 0:D], lhsT=xc[:, c, t * P:(t + 1) * P], rhs=w_out[:, c, :],
                                         start=(c == 0), stop=(c == MC - 1))
                last.then_inc(out_product, 1)

            @block.vector
            def _(dve):
                ln_vector(dve, s, s.u, s.h, 0, var_ready, rstd_ready).then_inc(u_ready, 1)
                dve.wait_ge(u_transposed, 1)
                dve.tensor_copy(s.uT[:, :, :], ps[0:DK, 0:DC, :]).then_inc(uT_ready, 1)
                dve.wait_ge(weights_in, 7 * 16)
                dve.wait_ge(pad_zeroed, 1)
                for c in range(MC):
                    dve.wait_ge(x_product, c + 1)
                    dve.tensor_copy(xp[:, c, :, PAD:], ps[:, 2 + c, :].rearrange("p (b n) -> p b n", b=BATCH))
                    dve.drain()
                    acc = xc[:, c, :].rearrange("p (b n) -> p b n", b=BATCH)
                    dve.tensor_scalar(acc, xp[:, c, :, 0:SEQ], cols[:, c, 0:1], None, ALU.mult)
                    for k in range(1, KW):
                        dve.drain()
                        last = dve.scalar_tensor_tensor(out=acc, in0=xp[:, c, :, k:k + SEQ], scalar=cols[:, c, k:k + 1],
                                                        in1=acc, op0=ALU.mult, op1=ALU.add)
                    last.then_inc(conv_done, 1)
                dve.wait_ge(a_exp, 1)
                dve.tensor_scalar(a_log[:, :, :], a_log[:, :, :], -1.0, None, ALU.mult).then_inc(a_ready, 1)
                for c in range(MC):
                    dve.wait_ge(dt_product, c + 1)
                    dve.tensor_scalar(dt[:, c, :], ps[:, 2 + c, :], cols[:, c, KW + 1:KW + 2], None, ALU.add).then_inc(biased, 1)
                for c in range(MC):
                    dve.wait_ge(log_ready, c + 1)
                    dve.scalar_tensor_tensor(out=dt[:, c, :], in0=dt[:, c, :], scalar=0.0, in1=soft[:, c, :],
                                             op0=ALU.max, op1=ALU.add).then_inc(dt_ready, 1)
                    dve.drain()
                    dve.tensor_tensor(dtx[:, c, :], dt[:, c, :], xc[:, c, :], ALU.mult)
                    dve.tensor_scalar(soft[:, c, :], xc[:, c, :], cols[:, c, KW + 2:KW + 3], None, ALU.mult).then_inc(skip_ready, 1)
                dve.drain()
                dve.sem_inc(decay_free, 1)
                dve.sem_inc(bc_free, 1)
                with dve.Fori(0, NS // 2) as i:
                    for k in range(2):
                        n = i * 2 + k
                        dve.wait_ge(bc_in[k], i * 32 + 32)
                        for c in range(MC):
                            dve.tensor_tensor(drive[:, c, :], dtx[:, c, :], b_all[:, k, :], ALU.mult)
                        dve.drain()
                        for c in range(MC):
                            dve.wait_ge(decay_ready, n * MC + c + 1)
                            for b in range(BATCH):
                                seq = slice(b * SEQ, (b + 1) * SEQ)
                                last = dve.tensor_tensor_scan(state[:, c, seq], decay[:, k, c, seq], drive[:, c, seq],
                                                              0.0, ALU.mult, ALU.add)
                        last.then_inc(decay_free, 1)
                        dve.drain()
                        for c in range(MC):
                            dve.wait_ge(out_summed, n * MC)
                            dve.tensor_tensor(out_n[:, c, :], state[:, c, :], c_all[:, k, :], ALU.mult).then_inc(out_ready, 1)
                        dve.drain()
                        dve.sem_inc(bc_free, 1)
                dve.wait_ge(out_summed, NS * MC)
                for c in range(MC):
                    last = dve.tensor_tensor(xc[:, c, :], ps[:, 5 + c, :], z[:, c, :], ALU.mult)
                last.then_inc(gated, 1)
                dve.wait_ge(out_product, 1)
                dve.tensor_tensor(r[:, :, :], ps[:, 0:T, 0:D], s.u[:, :, :], ALU.add)
                dve.drain()
                dve.tensor_tensor(sq[:, :, :], r[:, :, :], r[:, :, :], ALU.mult)
                dve.drain()
                dve.reduce_sum(s.var[:, :], sq[:, :, :], AX.X)
                dve.drain()
                dve.tensor_scalar(s.var[:, :], s.var[:, :], 1.0 / D, EPS, ALU.mult, ALU.add).then_inc(var_ready, 1)
                dve.wait_ge(rstd_ready, 2)
                for t in range(T):
                    dve.scalar_tensor_tensor(out=r[:, t, :], in0=r[:, t, :], scalar=s.rstd[:, t:t + 1], in1=w_norm[:, :],
                                             op0=ALU.mult, op1=ALU.mult)
                dve.drain()
                dve.tensor_tensor(s.h[:, :, :], s.h[:, :, :], r[:, :, :], ALU.add)

            @block.scalar
            def _(act):
                act.wait_ge(weights_in, 7 * 16)
                for c in range(MC):
                    act.wait_ge(conv_done, c + 1)
                    act.activation(xc[:, c, :], xc[:, c, :], ACT.Silu, bias=cols[:, c, KW:KW + 1]).then_inc(xc_ready, 1)
                for c in range(MC):
                    act.wait_ge(x_product, MC + c + 1)
                    act.activation(z[:, c, :], ps[:, 5 + c, :], ACT.Silu).then_inc(xc_ready, 1)
                act.wait_ge(dbc_product, 1)
                act.copy(dt_in[:, :], ps[0:R, 0, :]).then_inc(dbc_ready, 1)
                act.wait_ge(dbc_product, 2)
                act.copy(bc[:, :], ps[0:2 * NS, 1, :]).then_inc(dbc_ready, 1)
                act.activation(a_log[:, :, :], a_log[:, :, :], ACT.Exp).then_inc(a_exp, 1)
                for c in range(MC):
                    act.wait_ge(biased, c + 1)
                    act.activation(soft[:, c, :], dt[:, c, :], ACT.Abs)
                act.drain()
                for c in range(MC):
                    act.activation(soft[:, c, :], soft[:, c, :], ACT.Exp, scale=-1.0)
                act.drain()
                for c in range(MC):
                    act.activation(soft[:, c, :], soft[:, c, :], ACT.Ln, bias=1.0).then_inc(log_ready, 1)
                act.wait_ge(a_ready, 1)
                act.wait_ge(dt_ready, MC)
                with act.Fori(0, NS // 2) as i:
                    for k in range(2):
                        n = i * 2 + k
                        act.wait_ge(decay_free, n)
                        for c in range(MC):
                            act.activation(decay[:, k, c, :], dt[:, c, :], ACT.Exp,
                                           scale=a_log[:, c, bass.ds(n, 1)]).then_inc(decay_ready, 1)


NE = 128
TOP = 6
CAP = 192
SLOTS = 96
GROUPS = NE * CAP // SLOTS
SPARE = GROUPS
NI = 464
IK, IN_ = 116, 4
SI = 8
ROUTED_SCALE = 2.5
FAR = 100000.0


def moe_stage(nc, s, a):
    ctx = ExitStack()
    with ctx:
        def sb(name, shape, dt=fp32):
            return ctx.enter_context(nc.sbuf_tensor(name, shape, dt))

        def sem(name):
            return s.stage_semaphore(name)

        w_router = sb("moe_w_router", [DK, DC, NE])
        e_bias = sb("moe_e_bias", [P, NE])
        sig = sb("moe_sig", [P, T, NE])
        choice = sb("moe_choice", [P, T, NE])
        top8 = sb("moe_top8", [P, T, 8])
        top8_at = sb("moe_top8_at", [P, T, 8], u32)
        expert = sb("moe_expert", [P, TOP, T])
        iota_j = sb("moe_iota_j", [P, GROUPS])
        iota_p = sb("moe_iota_p", [P, 1])
        tok_id = sb("moe_tok_id", [P, T])
        before = sb("moe_before", [P, P])
        onehot = sb("moe_onehot", [P, TOP, T, NE])
        picked = sb("moe_picked", [P, TOP, T, NE])
        mask = sb("moe_mask", [P, T, NE])
        pos = sb("moe_pos", [P, T, NE])
        sig_k = sb("moe_sig_k", [P, TOP, T])
        pos_k = sb("moe_pos_k", [P, TOP, T])
        den = sb("moe_den", [P, T])
        weight = sb("moe_weight", [P, TOP, T])
        valid = sb("moe_valid", [P, TOP, T])
        slot_f = sb("moe_slot_f", [P, TOP, T])
        far_f = sb("moe_far_f", [P, TOP, T])
        write_at = sb("moe_write_at", [P, TOP, T], u32)
        read_at = sb("moe_read_at", [P, TOP, T], u32)
        count = sb("moe_count", [P, 1])
        active = sb("moe_active", [P, 2])
        rank = sb("moe_rank", [P, 2])
        chosen = sb("moe_chosen", [P, 2, GROUPS])
        group_no = sb("moe_group_no", [P, 2])
        total = sb("moe_total", [1, 1])
        pairs = sb("moe_pairs", [1, GROUPS // 2])
        list_e = sb("moe_list_e", [1, GROUPS], u32)
        list_g = sb("moe_list_g", [1, GROUPS], u32)
        n_pairs_f = sb("moe_n_pairs_f", [1, 1])
        n_pairs = sb("moe_n_pairs", [1, 1], u32)
        zeros = sb("moe_zeros", [P, (GROUPS + 1) * SLOTS * D // P // 12])
        tok_rows_sb = sb("moe_tok_rows", [P, 2, SLOTS])
        tok_at = sb("moe_tok_at", [SLOTS, GROUPS + 1], u32)
        w_sgu = sb("moe_w_sgu", [DK, DC, 2, SI * IK])
        w_sd = sb("moe_w_sd", [IK, SI, D])
        s_act = sb("moe_s_act", [IK, 2, NT])
        s_hidT = sb("moe_s_hidT", [IK, SI, NT])
        shared = sb("moe_shared", [P, T, D])
        tok_dram = nc.dram_tensor("tok_of_slot", [(GROUPS + 1) * SLOTS, 1], fp32).ap()
        u_dram = nc.dram_tensor("u_rows", [NT, D], fp32).ap()
        y_dram = nc.dram_tensor("y_of_slot", [(GROUPS + 1) * SLOTS, D], fp32).ap()
        ps = s.ps

        weights_in = sem("moe_weights_in")
        shared_in = sem("moe_shared_in")
        var_ready, rstd_ready = sem("moe_var_ready"), sem("moe_rstd_ready")
        consts = sem("moe_consts")
        zeros_ready = sem("moe_zeros_ready")
        y_cleared = sem("moe_y_cleared")
        tok_cleared = sem("moe_tok_cleared")
        u_ready = sem("moe_u_ready")
        u_stored = sem("moe_u_stored")
        u_transposed = sem("moe_u_transposed")
        uT_ready = sem("moe_uT_ready")
        logits_ready = sem("moe_logits_ready")
        sig_ready = sem("moe_sig_ready")
        mask_ready = sem("moe_mask_ready")
        pos_product = sem("moe_pos_product")
        active_ready = sem("moe_active_ready")
        rank_product = sem("moe_rank_product")
        chosen_ready = sem("moe_chosen_ready")
        list_product = sem("moe_list_product")
        slots_ready = sem("moe_slots_ready")
        tok_scattered = sem("moe_tok_scattered")
        tok_in = sem("moe_tok_in")
        tok_product = sem("moe_tok_product")
        s_product = sem("moe_s_product")
        s_silu = sem("moe_s_silu")
        s_ready = sem("moe_s_ready")
        s_out = sem("moe_s_out")

        with nc.Block() as block:
            @block.sync
            def _(sp):
                sp.dma_start(w_router[:, :, :], a["moe_w_router"].rearrange("(c p) e -> p c e", p=DK)).then_inc(weights_in, 16)
                sp.dma_start(e_bias[:, :], a["moe_e_bias"].broadcast_to((P, NE))).then_inc(weights_in, 16)
                for k in range(2):
                    sp.dma_start(w_sgu[:, :, k, :], a["moe_w_sgu"][k].rearrange("(c p) e -> p c e", p=DK)).then_inc(shared_in, 16)
                sp.dma_start(w_sd[:, :, :], a["moe_w_sd"].rearrange("(c p) e -> p c e", p=IK)).then_inc(shared_in, 16)
                sp.wait_ge(zeros_ready, 1)
                sp.dma_start(tok_dram.rearrange("(p n) o -> p (n o)", p=SLOTS), zeros[0:SLOTS, 0:GROUPS + 1]).then_inc(tok_cleared, 16)
                sp.wait_ge(u_ready, 1)
                sp.dma_start(u_dram.rearrange("(t p) d -> p t d", p=P), s.u[:, :, :]).then_inc(u_stored, 16)
                for n in range(12):
                    lot = (GROUPS + 1) * SLOTS // 12
                    sp.dma_start(y_dram[n * lot:(n + 1) * lot, :].rearrange("r d -> (r d)").rearrange("(p n) -> p n", p=P),
                                 zeros[:, :]).then_inc(y_cleared, 16)
                sp.wait_ge(tok_scattered, TOP * T * 16)
                sp.dma_start(tok_rows_sb[:, :, :],
                             tok_dram[0:GROUPS * SLOTS, :].rearrange("(g p c) o -> p g (c o)", p=P, c=SLOTS)).then_inc(tok_in, 16)
                sp.wait_ge(u_stored, 16)
                sp.wait_ge(y_cleared, 12 * 16)

            @block.gpsimd
            def _(pool):
                pool.memset(zeros[:, :], 0.0).then_inc(zeros_ready, 1)
                pool.memset(before[:, :], 1.0).then_inc(consts, 1)
                pool.iota(iota_j[:, :], [[1, GROUPS]], base=0, channel_multiplier=0, allow_small_or_imprecise_dtypes=True).then_inc(consts, 1)
                pool.iota(iota_p[:, :], [[0, 1]], base=0, channel_multiplier=1, allow_small_or_imprecise_dtypes=True).then_inc(consts, 1)
                pool.iota(tok_id[:, :], [[P, T]], base=0, channel_multiplier=1, allow_small_or_imprecise_dtypes=True).then_inc(consts, 1)
                pool.iota(group_no[:, :], [[1, 2]], base=-SPARE, channel_multiplier=2, allow_small_or_imprecise_dtypes=True).then_inc(consts, 1)
                pool.wait_ge(consts, 5)
                pool.affine_select(out=before[:, :], in_=before[:, :], compare_op=ALU.is_gt, fill=0.0, base=0,
                                   pattern=[[1, P]], channel_multiplier=-1).then_inc(consts, 1)
                ln_pool(pool, s, 0, var_ready, rstd_ready)
                pool.wait_ge(slots_ready, 1)
                pool.wait_ge(tok_cleared, 16)
                for k in range(TOP):
                    for t in range(T):
                        pool.indirect_dma_start(out=tok_dram, out_offset=bass.IndirectOffsetOnAxis(ap=write_at[:, k, t:t + 1], axis=0),
                                                in_=tok_id[:, t:t + 1], in_offset=None,
                                                bounds_check=GROUPS * SLOTS - 1, oob_is_err=False).then_inc(tok_scattered, 16)

            @block.tensor
            def _(pe):
                pe.wait_ge(u_ready, 1)
                transpose_u(pe, s).then_inc(u_transposed, 1)
                pe.wait_ge(uT_ready, 1)
                pe.wait_ge(weights_in, 32)
                for t in range(T):
                    for c in range(DC):
                        last = pe.matmul(ps[:, 2, t * NE:(t + 1) * NE], lhsT=s.uT[:, c, t * P:(t + 1) * P],
                                         rhs=w_router[:, c, :], start=(c == 0), stop=(c == DC - 1))
                last.then_inc(logits_ready, 1)
                pe.wait_ge(mask_ready, 1)
                pe.wait_ge(consts, 6)
                for t in range(T):
                    for j in range(t + 1):
                        pe.matmul(ps[:, 3, t * NE:(t + 1) * NE], lhsT=(before if j == t else s.ones)[:, :],
                                  rhs=mask[:, j, :], start=(j == 0), stop=(j == t))
                for t in range(T):
                    last = pe.matmul(ps[:, 4, 0:1], lhsT=mask[:, t, :], rhs=s.ones[:, 0:1], start=(t == 0), stop=(t == T - 1))
                last.then_inc(pos_product, 1)
                pe.wait_ge(active_ready, 1)
                pe.matmul(ps[:, 5, 0:1], lhsT=before[:, :], rhs=active[:, 0:1], start=True, stop=True)
                pe.matmul(ps[:, 5, 1:2], lhsT=s.ones[:, :], rhs=active[:, 0:1], start=True, stop=False)
                pe.matmul(ps[:, 5, 1:2], lhsT=before[:, :], rhs=active[:, 1:2], start=False, stop=True)
                for k in range(2):
                    last = pe.matmul(ps[0:1, 5, 2:3], lhsT=s.ones[:, 0:1], rhs=active[:, k:k + 1], start=(k == 0), stop=(k == 1))
                last.then_inc(rank_product, 1)
                pe.wait_ge(chosen_ready, 1)
                for at, col in ((0, [iota_p[:, 0:1]] * 2), (GROUPS, [group_no[:, 0:1], group_no[:, 1:2]])):
                    for k in range(2):
                        last = pe.matmul(ps[0:1, 6, at:at + GROUPS], lhsT=col[k], rhs=chosen[:, k, :], start=(k == 0), stop=(k == 1))
                last.then_inc(list_product, 1)
                pe.wait_ge(shared_in, 48)
                for j in range(SI):
                    if j >= 2:
                        pe.wait_ge(s_ready, j - 1)
                    for k in range(2):
                        for c in range(DC):
                            last = pe.matmul(ps[0:IK, 2 * (j % 2) + k, :], lhsT=w_sgu[:, c, k, j * IK:(j + 1) * IK],
                                             rhs=s.uT[:, c, :], start=(c == 0), stop=(c == DC - 1))
                    last.then_inc(s_product, 1)
                pe.wait_ge(s_ready, SI)
                for t in range(T):
                    for j in range(SI):
                        last = pe.matmul(ps[:, t, 0:D], lhsT=s_hidT[:, j, t * P:(t + 1) * P], rhs=w_sd[:, j, :],
                                         start=(j == 0), stop=(j == SI - 1))
                last.then_inc(s_out, 1)
                pe.wait_ge(tok_in, 16)
                for k in range(2):
                    last = pe.transpose(ps[0:SLOTS, 7, k * P:(k + 1) * P], tok_rows_sb[:, k, :], s.ident[:, :])
                last.then_inc(tok_product, 1)

            @block.scalar
            def _(act):
                act.wait_ge(logits_ready, 1)
                act.activation(sig[:, :, :], ps[:, 2, :].rearrange("p (t e) -> p t e", t=T), ACT.Sigmoid).then_inc(sig_ready, 1)
                for j in range(SI):
                    act.wait_ge(s_product, j + 1)
                    if j >= 2:
                        act.wait_ge(s_ready, j - 1)
                    act.activation(s_act[:, j % 2, :], ps[0:IK, 2 * (j % 2), :], ACT.Silu).then_inc(s_silu, 1)

            @block.vector
            def _(dve):
                ln_vector(dve, s, s.u, s.h, 0, var_ready, rstd_ready).then_inc(u_ready, 1)
                dve.wait_ge(u_transposed, 1)
                dve.tensor_copy(s.uT[:, :, :], ps[0:DK, 0:DC, :]).then_inc(uT_ready, 1)
                dve.wait_ge(weights_in, 32)
                dve.wait_ge(sig_ready, 1)
                dve.tensor_tensor(choice[:, :, :], sig[:, :, :], e_bias[:, :].unsqueeze(1).broadcast_to((P, T, NE)), ALU.add)
                dve.drain()
                for t in range(T):
                    dve.max(top8[:, t, :], choice[:, t, :])
                dve.drain()
                for t in range(T):
                    dve.max_index(top8_at[:, t, :], top8[:, t, :], choice[:, t, :])
                dve.drain()
                dve.tensor_copy(expert[:, :, :], top8_at[:, :, 0:TOP].rearrange("p t k -> p k t"))
                dve.drain()
                dve.wait_ge(consts, 6)
                for k in range(TOP):
                    dve.tensor_tensor(onehot[:, k, :, :], iota_j[:, 0:NE].unsqueeze(1).broadcast_to((P, T, NE)),
                                      expert[:, k, :].unsqueeze(2).broadcast_to((P, T, NE)), ALU.is_equal)
                dve.drain()
                dve.reduce_sum(mask[:, :, :], onehot[:, :, :, :].rearrange("p k t e -> p t e k"), AX.X).then_inc(mask_ready, 1)
                for k in range(TOP):
                    dve.tensor_tensor(picked[:, k, :, :], onehot[:, k, :, :], sig[:, :, :], ALU.mult)
                dve.drain()
                dve.reduce_sum(sig_k[:, :, :], picked[:, :, :, :], AX.X)
                dve.drain()
                dve.reduce_sum(den[:, :], sig_k[:, :, :].rearrange("p k t -> p t k"), AX.X)
                dve.wait_ge(pos_product, 1)
                dve.tensor_copy(pos[:, :, :], ps[:, 3, :].rearrange("p (t e) -> p t e", t=T))
                dve.tensor_copy(count[:, :], ps[:, 4, 0:1])
                dve.drain()
                dve.tensor_scalar(active[:, 0:1], count[:, :], 0.0, None, ALU.is_gt)
                dve.tensor_scalar(active[:, 1:2], count[:, :], float(SLOTS), None, ALU.is_gt).then_inc(active_ready, 1)
                for k in range(TOP):
                    dve.tensor_tensor(picked[:, k, :, :], onehot[:, k, :, :], pos[:, :, :], ALU.mult)
                dve.drain()
                dve.reduce_sum(pos_k[:, :, :], picked[:, :, :, :], AX.X)
                dve.tensor_scalar(den[:, :], den[:, :], 1e-20, None, ALU.add)
                dve.drain()
                dve.reciprocal(den[:, :], den[:, :])
                dve.tensor_scalar(valid[:, :, :], pos_k[:, :, :], float(CAP), None, ALU.is_lt)
                dve.drain()
                dve.tensor_tensor(weight[:, :, :], sig_k[:, :, :], den[:, :].unsqueeze(1).broadcast_to((P, TOP, T)), ALU.mult)
                dve.tensor_scalar(far_f[:, :, :], expert[:, :, :], float(NT - CAP), FAR, ALU.mult, ALU.add)
                dve.tensor_scalar(slot_f[:, :, :], expert[:, :, :], float(CAP), None, ALU.mult)
                dve.drain()
                dve.tensor_tensor(picked[:, :, 0, 0:T], far_f[:, :, :], valid[:, :, :], ALU.mult)
                dve.tensor_tensor(picked[:, :, 1, 0:T], pos_k[:, :, :], slot_f[:, :, :], ALU.add)
                dve.tensor_tensor(picked[:, :, 2, 0:T], pos_k[:, :, :], valid[:, :, :], ALU.mult)
                dve.drain()
                dve.tensor_tensor(far_f[:, :, :], far_f[:, :, :], picked[:, :, 0, 0:T], ALU.subtract)
                dve.tensor_tensor(read_at[:, :, :], picked[:, :, 2, 0:T], slot_f[:, :, :], ALU.add)
                dve.scalar_tensor_tensor(out=weight[:, :, :], in0=weight[:, :, :], scalar=ROUTED_SCALE, in1=valid[:, :, :],
                                         op0=ALU.mult, op1=ALU.mult)
                dve.drain()
                dve.tensor_tensor(write_at[:, :, :], picked[:, :, 1, 0:T], far_f[:, :, :], ALU.add).then_inc(slots_ready, 1)
                dve.wait_ge(rank_product, 1)
                dve.tensor_copy(rank[:, :], ps[:, 5, 0:2])
                dve.tensor_copy(total[:, :], ps[0:1, 5, 2:3])
                dve.drain()
                for k in range(2):
                    last = dve.tensor_scalar(chosen[:, k, :], iota_j[:, :], rank[:, k:k + 1], active[:, k:k + 1], ALU.is_equal, ALU.mult)
                last.then_inc(chosen_ready, 1)
                dve.tensor_scalar(pairs[:, :], iota_j[0:1, ::2], total[:, :], None, ALU.is_lt)
                dve.drain()
                dve.reduce_sum(n_pairs_f[:, :], pairs[:, :], AX.X)
                dve.drain()
                dve.tensor_copy(n_pairs[:, :], n_pairs_f[:, :])
                dve.wait_ge(list_product, 1)
                dve.tensor_copy(list_e[:, :], ps[0:1, 6, 0:GROUPS])
                dve.tensor_scalar(list_g[:, :], ps[0:1, 6, GROUPS:2 * GROUPS], float(SPARE), None, ALU.add)
                for j in range(SI):
                    dve.wait_ge(s_silu, j + 1)
                    dve.tensor_tensor(s_hidT[:, j, :], s_act[:, j % 2, :], ps[0:IK, 2 * (j % 2) + 1, :], ALU.mult).then_inc(s_ready, 1)
                dve.wait_ge(s_out, 1)
                dve.tensor_tensor(shared[:, :, :], ps[:, 0:T, 0:D], s.h[:, :, :], ALU.add)
                dve.wait_ge(tok_product, 1)
                dve.memset(tok_at[:, SPARE:SPARE + 1], 0)
                dve.tensor_copy(tok_at[:, 0:GROUPS], ps[0:SLOTS, 7, 0:GROUPS])

        w_gu = [sb(f"moe_w_gu{k}", [DK, DC, 2 * NI]) for k in range(2)]
        w_d = [sb(f"moe_w_d{k}", [IK, IN_, D]) for k in range(2)]
        row_at = [sb(f"moe_row_at{k}", [SLOTS, 1], u32) for k in range(2)]
        rows = [sb(f"moe_rows{k}", [SLOTS, D]) for k in range(2)]
        rowsT = [sb(f"moe_rowsT{k}", [DK, DC, SLOTS]) for k in range(2)]
        act_g = [sb(f"moe_act_g{k}", [IK, IN_, SLOTS]) for k in range(2)]
        hidT = [sb(f"moe_hidT{k}", [IK, IN_, SLOTS]) for k in range(2)]
        y = [sb(f"moe_y{k}", [SLOTS, D]) for k in range(2)]
        gu_in = [sem(f"moe_gu_in{k}") for k in range(2)]
        d_in = [sem(f"moe_d_in{k}") for k in range(2)]
        row_at_set = [sem(f"moe_row_at_set{k}") for k in range(2)]
        rows_in = [sem(f"moe_rows_in{k}") for k in range(2)]
        rows_transposed = [sem(f"moe_rows_transposed{k}") for k in range(2)]
        rowsT_ready = [sem(f"moe_rowsT_ready{k}") for k in range(2)]
        gu_product = [sem(f"moe_gu_product{k}") for k in range(2)]
        silu_ready = [sem(f"moe_silu_ready{k}") for k in range(2)]
        hid_ready = [sem(f"moe_hid_ready{k}") for k in range(2)]
        y_product = [sem(f"moe_y_product{k}") for k in range(2)]
        y_ready = [sem(f"moe_y_ready{k}") for k in range(2)]
        y_stored = [sem(f"moe_y_stored{k}") for k in range(2)]
        all_stored = sem("moe_all_stored")
        gathers_begun = sem("moe_gathers_begun")

        with nc.Block() as block:
            @block.sync
            def _(sp):
                with sp.Fori(0, sp.value_load(n_pairs[0:1, 0:1], min_val=1, max_val=GROUPS // 2)) as i:
                    for k in range(2):
                        e = sp.value_load(list_e[0:1, bass.ds(2 * i + k, 1)], min_val=0, max_val=NE - 1)
                        sp.wait_ge(gu_product[k], i)
                        sp.dma_start(w_gu[k][:, :, :], a["moe_w_gu"][bass.ds(e, 1), :, :].rearrange("o (c p) f -> p (o c) f", p=DK)).then_inc(gu_in[k], 16)
                        sp.wait_ge(y_product[k], i)
                        sp.dma_start(w_d[k][:, :, :], a["moe_w_d"][bass.ds(e, 1), :, :].rearrange("o (c p) f -> p (o c) f", p=IK)).then_inc(d_in[k], 16)

            @block.gpsimd
            def _(pool):
                with pool.Fori(0, pool.value_load(n_pairs[0:1, 0:1], min_val=1, max_val=GROUPS // 2)) as i:
                    for k in range(2):
                        g = pool.value_load(list_g[0:1, bass.ds(2 * i + k, 1)], min_val=0, max_val=GROUPS)
                        pool.wait_ge(rows_transposed[k], i)
                        pool.tensor_copy(row_at[k][:, :], tok_at[:, bass.ds(g, 1)]).then_inc(row_at_set[k], 1)
                        pool.wait_ge(row_at_set[k], i + 1)
                        pool.sem_inc(gathers_begun, 1)
                        pool.indirect_dma_start(out=rows[k][:, :], out_offset=None, in_=u_dram,
                                                in_offset=bass.IndirectOffsetOnAxis(ap=row_at[k][:, 0:1], axis=0),
                                                bounds_check=NT - 1, oob_is_err=False).then_inc(rows_in[k], 16)

            @block.tensor
            def _(pe):
                with pe.Fori(0, pe.value_load(n_pairs[0:1, 0:1], min_val=1, max_val=GROUPS // 2)) as i:
                    for k in range(2):
                        pe.wait_ge(rows_in[k], i * 16 + 16)
                        for c in range(DC):
                            last = pe.transpose(ps[0:DK, 7 * k, c * SLOTS:(c + 1) * SLOTS], rows[k][:, c * DK:(c + 1) * DK],
                                                s.ident[0:SLOTS, 0:SLOTS])
                        last.then_inc(rows_transposed[k], 1)
                    for k in range(2):
                        pe.wait_ge(rowsT_ready[k], i + 1)
                        pe.wait_ge(gu_in[k], i * 16 + 16)
                        for half in range(2):
                            for m in range(IN_):
                                at = half * NI + m * IK
                                for c in range(DC):
                                    last = pe.matmul(ps[0:IK, 1 + 2 * k + half, m * SLOTS:(m + 1) * SLOTS],
                                                     lhsT=w_gu[k][:, c, at:at + IK], rhs=rowsT[k][:, c, :],
                                                     start=(c == 0), stop=(c == DC - 1))
                        last.then_inc(gu_product[k], 1)
                    for k in range(2):
                        pe.wait_ge(hid_ready[k], i + 1)
                        pe.wait_ge(d_in[k], i * 16 + 16)
                        pe.wait_ge(y_ready[k], i)
                        for m in range(IN_):
                            last = pe.matmul(ps[0:SLOTS, 5 + k, 0:D], lhsT=hidT[k][:, m, :], rhs=w_d[k][:, m, :],
                                             start=(m == 0), stop=(m == IN_ - 1))
                        last.then_inc(y_product[k], 1)

            @block.scalar
            def _(act):
                n = act.value_load(n_pairs[0:1, 0:1], min_val=1, max_val=GROUPS // 2)
                with act.Fori(0, n) as i:
                    for k in range(2):
                        act.wait_ge(gu_product[k], i + 1)
                        act.wait_ge(hid_ready[k], i)
                        act.activation(act_g[k][:, :, :], ps[0:IK, 1 + 2 * k, 0:IN_ * SLOTS].rearrange("p (m n) -> p m n", m=IN_),
                                       ACT.Silu).then_inc(silu_ready[k], 1)
                    for k in range(2):
                        g = act.value_load(list_g[0:1, bass.ds(2 * i + k, 1)], min_val=0, max_val=GROUPS)
                        act.wait_ge(y_stored[k], i * 16)
                        act.wait_ge(y_product[k], i + 1)
                        act.copy(y[k][:, :], ps[0:SLOTS, 5 + k, 0:D]).then_inc(y_ready[k], 1)
                        act.wait_ge(y_ready[k], i + 1)
                        act.dma_start(y_dram.rearrange("(g c) d -> g c d", c=SLOTS)[bass.ds(g, 1), :, :].rearrange("o c d -> (o c) d"),
                                      y[k][:, :]).then_inc(y_stored[k], 16)
                for k in range(2):
                    act.wait_ge(y_stored[k], n * 16)
                    act.sem_inc(all_stored, 1)

            @block.vector
            def _(dve):
                with dve.Fori(0, dve.value_load(n_pairs[0:1, 0:1], min_val=1, max_val=GROUPS // 2)) as i:
                    for k in range(2):
                        dve.wait_ge(rows_transposed[k], i + 1)
                        dve.tensor_copy(rowsT[k][:, :, :], ps[0:DK, 7 * k, 0:DC * SLOTS].rearrange("p (c n) -> p c n", c=DC)).then_inc(rowsT_ready[k], 1)
                    for k in range(2):
                        dve.wait_ge(silu_ready[k], i + 1)
                        dve.tensor_tensor(hidT[k][:, :, :], act_g[k][:, :, :],
                                          ps[0:IK, 2 + 2 * k, 0:IN_ * SLOTS].rearrange("p (m n) -> p m n", m=IN_), ALU.mult).then_inc(hid_ready[k], 1)

        back = sb("moe_back", [P, TOP, T, D])
        acc = shared
        back_in = [sem(f"moe_back_in{k}") for k in range(TOP)]

        with nc.Block() as block:
            @block.gpsimd
            def _(pool):
                for k in range(TOP):
                    for t in range(T):
                        pool.indirect_dma_start(out=back[:, k, t, :], out_offset=None, in_=y_dram,
                                                in_offset=bass.IndirectOffsetOnAxis(ap=read_at[:, k, t:t + 1], axis=0),
                                                bounds_check=GROUPS * SLOTS - 1, oob_is_err=False).then_inc(back_in[k], 16)

            @block.vector
            def _(dve):
                for k in range(TOP):
                    dve.wait_ge(back_in[k], T * 16)
                    for t in range(T):
                        dve.scalar_tensor_tensor(out=acc[:, t, :], in0=back[:, k, t, :], scalar=weight[:, k, t:t + 1],
                                                 in1=acc[:, t, :], op0=ALU.mult, op1=ALU.add)
                    dve.drain()
                dve.tensor_copy(s.h[:, :, :], acc[:, :, :])


EH, EY = 12, 64
EC = EH * EY // P
EM = 768
EMC = EM // P
STEPS = 12
ALPHA = 0.1
BETA = 0.125
UNITS = EC * BATCH * 2
PRODUCTS = 4 * EC + EMC
OUT_Q, OUT_K = (6, 0), (7, 1)


def energy_stage(nc, s, a):
    ctx = ExitStack()
    with ctx:
        def sb(name, shape):
            return ctx.enter_context(nc.sbuf_tensor(name, shape, fp32))

        def sem(name):
            return s.stage_semaphore(name)

        wT = sb("en_wT", [DK, DC, 3, EM])
        wr = sb("en_wr", [P, 3, EMC, D])
        ln = sb("en_ln", [DK, DC, 2])
        x = s.u
        y = sb("en_y", [P, T, D])
        gT = s.uT
        qT = sb("en_qT", [P, EC, NT])
        kT = sb("en_kT", [P, EC, NT])
        qn = sb("en_qn", [P, T, EH * EY])
        kn = sb("en_kn", [P, T, EH * EY])
        memT = sb("en_memT", [P, EMC, NT])
        neg_max = sb("en_neg_max", [P, 4, TB])
        row_sum = sb("en_row_sum", [P, 4, TB])
        prob = [sb(f"en_prob{i}", [P, TB, SEQ]) for i in range(4)]
        probT = [sb(f"en_probT{i}", [P, TB, SEQ]) for i in range(2)]
        dqT = sb("en_dqT", [P, EC, NT])
        dkT = sb("en_dkT", [P, EC, NT])
        ps = s.ps

        weights_in = sem("en_weights_in")
        var_ready, rstd_ready = sem("en_var_ready"), sem("en_rstd_ready")
        y_ready = sem("en_y_ready")
        y_transposed = sem("en_y_transposed")
        gT_ready = sem("en_gT_ready")
        product = sem("en_product")
        even_out = sem("en_even_out")
        odd_out = sem("en_odd_out")
        scores = sem("en_scores")
        max_ready = sem("en_max_ready")
        exp_ready = sem("en_exp_ready")
        prob_ready = sem("en_prob_ready")
        transposed = sem("en_transposed")
        probT_ready = sem("en_probT_ready")
        unit_done = sem("en_unit_done")
        dq_ready, dk_ready = sem("en_dq_ready"), sem("en_dk_ready")
        grad_product = sem("en_grad_product")
        half = PRODUCTS // 2

        def unit(u):
            return u // (2 * BATCH), u // 2 % BATCH, u % 2

        with nc.Block() as block:
            @block.sync
            def _(sp):
                sp.dma_start(ln[:, :, :], a["en_ln"].rearrange("(c p) k -> p c k", p=DK)).then_inc(weights_in, 16)
                for k in range(3):
                    sp.dma_start(wT[:, :, k, :], a["en_wT"][k].rearrange("(c p) e -> p c e", p=DK)).then_inc(weights_in, 16)
                    sp.dma_start(wr[:, k, :, :], a["en_w"][k].rearrange("(c p) d -> p c d", p=P)).then_inc(weights_in, 16)

            @block.gpsimd
            def _(pool):
                with pool.Fori(0, STEPS + 1) as n:
                    ln_pool(pool, s, n, var_ready, rstd_ready)

            @block.tensor
            def _(pe):
                pe.wait_ge(weights_in, 7 * 16)
                with pe.Fori(0, STEPS) as n:
                    pe.wait_ge(y_ready, n + 1)
                    for c in range(DC):
                        for t in range(T):
                            last = pe.transpose(ps[0:DK, c, t * P:(t + 1) * P], y[:, t, c * DK:(c + 1) * DK], s.ident[:, :])
                    last.then_inc(y_transposed, 1)
                    pe.wait_ge(gT_ready, n + 1)

                    def free_bank(p):
                        if p >= 6:
                            pe.wait_ge((even_out, odd_out)[p % 2], n * half + (p - 6) // 2 + 1)

                    def project(p, k, c):
                        free_bank(p)
                        for kc in range(DC):
                            last = pe.matmul(ps[:, 2 + p % 6, :], lhsT=wT[:, kc, k, c * P:(c + 1) * P], rhs=gT[:, kc, :],
                                             start=(kc == 0), stop=(kc == DC - 1))
                        last.then_inc(product, 1)

                    for c in range(EC):
                        project(2 * c, 0, c)
                        project(2 * c + 1, 1, c)
                    for c in range(EC):
                        for k, src, out in ((0, qT, even_out), (1, kT, odd_out)):
                            p = 2 * EC + 2 * c + k
                            free_bank(p)
                            pe.wait_ge(out, n * half + c + 1)
                            for t in range(T):
                                last = pe.transpose(ps[:, 2 + p % 6, t * P:(t + 1) * P], src[:, c, t * P:(t + 1) * P], s.ident[:, :])
                            last.then_inc(product, 1)
                    for c in range(EMC):
                        project(4 * EC + c, 2, c)

                    def score(u):
                        c, b, r = unit(u)
                        if u < 2:
                            pe.wait_ge((even_out, odd_out)[u], n * half + half - 2)
                        else:
                            pe.wait_ge(exp_ready, n * UNITS + u - 1)
                        at = slice(r * EY, (r + 1) * EY)
                        for i in range(TB):
                            lo = b * SEQ + i * P
                            last = pe.matmul(ps[:, 2 + u % 2, i * SEQ:(i + 1) * SEQ], lhsT=qT[at, c, lo:lo + P],
                                             rhs=kT[at, c, b * SEQ:(b + 1) * SEQ], start=True, stop=True)
                        last.then_inc(scores, 1)

                    def transpose(u):
                        if u == 0:
                            pe.wait_ge(even_out, n * half + half)
                            pe.wait_ge(odd_out, n * half + half)
                        if u >= 2:
                            pe.wait_ge(probT_ready, n * UNITS + u - 1)
                        pe.wait_ge(prob_ready, n * UNITS + u + 1)
                        for i in range(TB):
                            for j in range(TB):
                                last = pe.transpose(ps[:, 4 + u % 2, j * SEQ + i * P:j * SEQ + (i + 1) * P],
                                                    prob[u % 4][:, i, j * P:(j + 1) * P], s.ident[:, :])
                        last.then_inc(transposed, 1)

                    def combine(u):
                        c, b, r = unit(u)
                        if u % 4 == 0 and c >= 2:
                            pe.wait_ge(dq_ready, n * EC + c - 1)
                            pe.wait_ge(dk_ready, n * EC + c - 1)
                        at = slice(r * EY, (r + 1) * EY)
                        head = slice(c * P + r * EY, c * P + (r + 1) * EY)
                        for i in range(TB):
                            pe.matmul(ps[at, OUT_K[c % 2], b * SEQ:(b + 1) * SEQ], lhsT=qn[:, b * TB + i, head],
                                      rhs=prob[u % 4][:, i, :], start=(i == 0), stop=(i == TB - 1))
                        pe.wait_ge(probT_ready, n * UNITS + u + 1)
                        for j in range(TB):
                            last = pe.matmul(ps[at, OUT_Q[c % 2], b * SEQ:(b + 1) * SEQ], lhsT=kn[:, b * TB + j, head],
                                             rhs=probT[u % 2][:, j, :], start=(j == 0), stop=(j == TB - 1))
                        last.then_inc(unit_done, 1)

                    for slot in range(UNITS + 3):
                        if slot < UNITS:
                            score(slot)
                        if 2 <= slot < UNITS + 2:
                            transpose(slot - 2)
                        if 3 <= slot:
                            combine(slot - 3)
                    for lot, src in ((2, memT), (0, dqT), (1, dkT)):
                        for c in range(EC):
                            if lot == 0:
                                pe.wait_ge(dq_ready, n * EC + c + 1)
                            if lot == 1:
                                pe.wait_ge(dk_ready, n * EC + c + 1)
                            for t in range(T):
                                last = pe.matmul(ps[:, 2 + t, 0:D], lhsT=src[:, c, t * P:(t + 1) * P], rhs=wr[:, lot, c, :],
                                                 start=(lot == 2 and c == 0), stop=(lot == 1 and c == EC - 1))
                    last.then_inc(grad_product, 1)

            @block.scalar
            def _(act):
                with act.Fori(0, STEPS) as n:
                    for p in range(0, PRODUCTS, 2):
                        act.wait_ge(product, n * PRODUCTS + p + 1)
                        bank = ps[:, 2 + p % 6, :]
                        if p < 2 * EC:
                            last = act.copy(qT[:, p // 2, :], bank)
                        elif p < 4 * EC:
                            c = p // 2 - EC
                            last = act.copy(qn[:, :, c * P:(c + 1) * P], bank.rearrange("p (t n) -> p t n", t=T))
                        else:
                            last = act.activation(memT[:, p - 4 * EC, :], bank, ACT.Relu)
                        last.then_inc(even_out, 1)

                    def exponentiate(u):
                        act.wait_ge(max_ready, n * UNITS + u + 1)
                        if u >= 4:
                            act.wait_ge(unit_done, n * UNITS + u - 3)
                        for i in range(TB):
                            last = act.activation(prob[u % 4][:, i, :], ps[:, 2 + u % 2, i * SEQ:(i + 1) * SEQ], ACT.Exp,
                                                  bias=neg_max[:, u % 4, i:i + 1], accum_out=row_sum[:, u % 4, i:i + 1])
                        last.then_inc(exp_ready, 1)

                    def keep_transposed(u):
                        act.wait_ge(transposed, n * UNITS + u + 1)
                        if u >= 2:
                            act.wait_ge(unit_done, n * UNITS + u - 1)
                        act.copy(probT[u % 2][:, :, :], ps[:, 4 + u % 2, :].rearrange("p (j n) -> p j n", j=TB)).then_inc(probT_ready, 1)

                    def keep_dq(c):
                        act.wait_ge(unit_done, n * UNITS + 4 * c + 4)
                        act.mul(dqT[:, c, :], ps[:, OUT_Q[c % 2], :], 1.0 / BETA).then_inc(dq_ready, 1)

                    for slot in range(UNITS + 2):
                        if slot < UNITS:
                            exponentiate(slot)
                        if slot >= 2:
                            u = slot - 2
                            keep_transposed(u)
                            if u % 4 == 0 and u >= 4:
                                keep_dq(u // 4 - 1)
                    keep_dq(EC - 1)

            @block.vector
            def _(dve):
                ln_vector(dve, s, x, s.h, 0, var_ready, rstd_ready)
                dve.drain()
                dve.wait_ge(weights_in, 7 * 16)
                with dve.Fori(0, STEPS) as n:
                    ln_vector(dve, s, y, x, n + 1, var_ready, rstd_ready).then_inc(y_ready, 1)
                    dve.wait_ge(y_transposed, n + 1)
                    for c in range(DC):
                        last = dve.tensor_scalar(gT[:, c, :], ps[0:DK, c, :], ln[:, c, 0:1], ln[:, c, 1:2], ALU.mult, ALU.add)
                    last.then_inc(gT_ready, 1)
                    for p in range(1, PRODUCTS, 2):
                        dve.wait_ge(product, n * PRODUCTS + p + 1)
                        bank = ps[:, 2 + p % 6, :]
                        if p < 2 * EC:
                            last = dve.tensor_scalar(kT[:, p // 2, :], bank, BETA, None, ALU.mult)
                        elif p < 4 * EC:
                            c = p // 2 - EC
                            last = dve.tensor_copy(kn[:, :, c * P:(c + 1) * P], bank.rearrange("p (t n) -> p t n", t=T))
                        else:
                            last = dve.tensor_scalar(memT[:, p - 4 * EC, :], bank, 0.0, None, ALU.max)
                        last.then_inc(odd_out, 1)

                    def maximum(u):
                        dve.wait_ge(scores, n * UNITS + u + 1)
                        dve.tensor_reduce(neg_max[:, u % 4, :], ps[:, 2 + u % 2, :].rearrange("p (i m) -> p i m", i=TB),
                                          axis=AX.X, op=ALU.max, negate=True).then_inc(max_ready, 1)

                    def normalise(u):
                        dve.wait_ge(exp_ready, n * UNITS + u + 1)
                        dve.reciprocal(row_sum[:, u % 4, :], row_sum[:, u % 4, :])
                        dve.drain()
                        for i in range(TB):
                            last = dve.tensor_scalar(prob[u % 4][:, i, :], prob[u % 4][:, i, :], row_sum[:, u % 4, i:i + 1], None, ALU.mult)
                        last.then_inc(prob_ready, 1)

                    def keep_dk(c):
                        dve.wait_ge(unit_done, n * UNITS + 4 * c + 4)
                        dve.tensor_copy(dkT[:, c, :], ps[:, OUT_K[c % 2], :]).then_inc(dk_ready, 1)

                    for slot in range(UNITS + 1):
                        if slot < UNITS:
                            maximum(slot)
                        if slot >= 1:
                            normalise(slot - 1)
                        if slot % 4 == 3 and slot >= 7:
                            keep_dk(slot // 4 - 1)
                    keep_dk(EC - 1)
                    dve.wait_ge(grad_product, n + 1)
                    for t in range(T):
                        dve.scalar_tensor_tensor(out=x[:, t, :], in0=ps[:, 2 + t, 0:D], scalar=ALPHA, in1=x[:, t, :],
                                                 op0=ALU.mult, op1=ALU.add)
                    dve.drain()
                dve.tensor_tensor(s.h[:, :, :], s.h[:, :, :], x[:, :, :], ALU.add)


SE = 8
SCAP = 5 * NT // (4 * SE)
SF = 768
SM = SF // P


def switch_stage(nc, s, a):
    ctx = ExitStack()
    with ctx:
        def sb(name, shape, dt=fp32):
            return ctx.enter_context(nc.sbuf_tensor(name, shape, dt))

        def sem(name):
            return s.stage_semaphore(name)

        slots = SE * SCAP
        w_switch = sb("sw_w_switch", [DK, DC, SE])
        b_switch = sb("sw_b_switch", [1, SE])
        w1 = [sb(f"sw_w1_{k}", [DK, DC, SF]) for k in range(2)]
        w2 = [sb(f"sw_w2_{k}", [P, SM, D]) for k in range(2)]
        b1 = [sb(f"sw_b1_{k}", [P, SM]) for k in range(2)]
        b2 = [sb(f"sw_b2_{k}", [1, D]) for k in range(2)]
        row_max = sb("sw_row_max", [P, T])
        prob = sb("sw_prob", [P, T, SE])
        top8 = sb("sw_top8", [P, T, 8])
        top8_at = sb("sw_top8_at", [P, T, 8], u32)
        p_max = sb("sw_p_max", [P, T])
        route = sb("sw_route", [P, T])
        all_p = sb("sw_all_p", [P, NT])
        all_r = sb("sw_all_r", [P, NT])
        iota_j = sb("sw_iota_j", [P, slots])
        tok_id = sb("sw_tok_id", [P, T])
        ahead = sb("sw_ahead", [P, T, NT])
        rank = sb("sw_rank", [P, T])
        keep = sb("sw_keep", [P, T])
        dest = sb("sw_dest", [P, T])
        select = sb("sw_select", [P, T, slots])
        selectT = sb("sw_selectT", [SCAP, SE, NT])
        xT = sb("sw_xT", [DK, DC, slots])
        pre = [sb(f"sw_pre{k}", [P, SM, SCAP]) for k in range(2)]
        hid = [sb(f"sw_hid{k}", [P, SM, SCAP]) for k in range(2)]
        out = sb("sw_out", [SCAP, SE, D])
        ps = s.ps

        small_in = sem("sw_small_in")
        w_in = [sem(f"sw_w_in{k}") for k in range(2)]
        var_ready, rstd_ready = sem("sw_var_ready"), sem("sw_rstd_ready")
        consts = sem("sw_consts")
        u_ready = sem("sw_u_ready")
        u_transposed = sem("sw_u_transposed")
        uT_ready = sem("sw_uT_ready")
        logits_ready = sem("sw_logits_ready")
        shifted = sem("sw_shifted")
        exp_ready = sem("sw_exp_ready")
        routed = sem("sw_routed")
        spread = sem("sw_spread")
        select_ready = sem("sw_select_ready")
        x_product = sem("sw_x_product")
        xT_ready = sem("sw_xT_ready")
        select_transposed = sem("sw_select_transposed")
        selectT_ready = sem("sw_selectT_ready")
        up_product = [sem(f"sw_up_product{k}") for k in range(2)]
        pre_ready = [sem(f"sw_pre_ready{k}") for k in range(2)]
        hid_ready = [sem(f"sw_hid_ready{k}") for k in range(2)]
        down_product = [sem(f"sw_down_product{k}") for k in range(2)]
        out_ready = [sem(f"sw_out_ready{k}") for k in range(2)]
        back_product = sem("sw_back_product")

        with nc.Block() as block:
            @block.sync
            def _(sp):
                sp.dma_start(w_switch[:, :, :], a["sw_w_switch"].rearrange("(c p) e -> p c e", p=DK)).then_inc(small_in, 16)
                sp.dma_start(b_switch[:, :], a["sw_b_switch"]).then_inc(small_in, 16)
                with sp.Fori(0, SE // 2) as i:
                    for k in range(2):
                        e = bass.ds(2 * i + k, 1)
                        sp.wait_ge(down_product[k], i)
                        sp.dma_start(w1[k][:, :, :], a["sw_w1"][e, :, :].rearrange("o (c p) f -> p (o c) f", p=DK)).then_inc(w_in[k], 16)
                        sp.dma_start(b1[k][:, :], a["sw_b1"][e, :, :].rearrange("o p m -> p (o m)")).then_inc(w_in[k], 16)
                        sp.dma_start(w2[k][:, :, :], a["sw_w2"][e, :, :].rearrange("o (c p) d -> p (o c) d", p=P)).then_inc(w_in[k], 16)
                        sp.dma_start(b2[k][:, :], a["sw_b2"][e, :]).then_inc(w_in[k], 16)

            @block.gpsimd
            def _(pool):
                pool.iota(iota_j[:, :], [[1, slots]], base=0, channel_multiplier=0, allow_small_or_imprecise_dtypes=True).then_inc(consts, 1)
                pool.iota(tok_id[:, :], [[P, T]], base=0, channel_multiplier=1, allow_small_or_imprecise_dtypes=True).then_inc(consts, 1)
                ln_pool(pool, s, 0, var_ready, rstd_ready)

            @block.tensor
            def _(pe):
                pe.wait_ge(u_ready, 1)
                transpose_u(pe, s).then_inc(u_transposed, 1)
                pe.wait_ge(uT_ready, 1)
                pe.wait_ge(small_in, 32)
                for t in range(T):
                    at = slice(t * SE, (t + 1) * SE)
                    for c in range(DC):
                        pe.matmul(ps[:, 2, at], lhsT=s.uT[:, c, t * P:(t + 1) * P], rhs=w_switch[:, c, :], start=(c == 0), stop=False)
                    last = pe.matmul(ps[:, 2, at], lhsT=s.ones[0:1, :], rhs=b_switch[:, :], start=False, stop=True)
                last.then_inc(logits_ready, 1)
                pe.wait_ge(routed, 1)
                for bank, src in ((3, p_max), (4, route)):
                    for t in range(T):
                        last = pe.matmul(ps[:, bank, t * P:(t + 1) * P], lhsT=src[:, t:t + 1].broadcast_to((P, P)),
                                         rhs=s.ident[:, :], start=True, stop=True)
                last.then_inc(spread, 1)
                pe.wait_ge(select_ready, 1)
                for c in range(DC):
                    for half in range(2):
                        for t in range(T):
                            last = pe.matmul(ps[0:DK, 2 * c + half, 0:slots // 2], lhsT=s.u[:, t, c * DK:(c + 1) * DK],
                                             rhs=select[:, t, half * slots // 2:(half + 1) * slots // 2],
                                             start=(t == 0), stop=(t == T - 1))
                last.then_inc(x_product, 1)
                for e in range(SE):
                    if e >= 4:
                        pe.wait_ge(selectT_ready, e - 3)
                    for t in range(T):
                        last = pe.transpose(ps[0:SCAP, 4 + e % 4, t * P:(t + 1) * P], select[:, t, e * SCAP:(e + 1) * SCAP], s.ident[:, :])
                    last.then_inc(select_transposed, 1)
                pe.wait_ge(xT_ready, 1)
                pe.wait_ge(selectT_ready, SE)
                with pe.Fori(0, SE // 2) as i:
                    for k in range(2):
                        pe.wait_ge(w_in[k], i * 64 + 64)
                        pe.wait_ge(pre_ready[k], i)
                        for m in range(SM):
                            for c in range(DC):
                                last = pe.matmul(ps[:, 4 + k, m * SCAP:(m + 1) * SCAP], lhsT=w1[k][:, c, m * P:(m + 1) * P],
                                                 rhs=xT[:, c, bass.ds((2 * i + k) * SCAP, SCAP)], start=(c == 0), stop=(c == DC - 1))
                        last.then_inc(up_product[k], 1)
                    for k in range(2):
                        pe.wait_ge(hid_ready[k], i + 1)
                        pe.wait_ge(out_ready[k], i)
                        for m in range(SM):
                            pe.matmul(ps[0:SCAP, 6 + k, 0:D], lhsT=hid[k][:, m, :], rhs=w2[k][:, m, :], start=(m == 0), stop=False)
                        pe.matmul(ps[0:SCAP, 6 + k, 0:D], lhsT=s.ones[0:1, 0:SCAP], rhs=b2[k][:, :], start=False, stop=True).then_inc(down_product[k], 1)
                for k in range(2):
                    pe.wait_ge(out_ready[k], SE // 2)
                for t in range(T):
                    for e in range(SE):
                        last = pe.matmul(ps[:, t, 0:D], lhsT=selectT[:, e, t * P:(t + 1) * P], rhs=out[:, e, :],
                                         start=(e == 0), stop=(e == SE - 1))
                last.then_inc(back_product, 1)

            @block.scalar
            def _(act):
                act.wait_ge(shifted, 1)
                act.activation(prob[:, :, :], prob[:, :, :], ACT.Exp).then_inc(exp_ready, 1)
                for e in range(SE):
                    act.wait_ge(select_transposed, e + 1)
                    act.copy(selectT[:, e, :], ps[0:SCAP, 4 + e % 4, :]).then_inc(selectT_ready, 1)
                with act.Fori(0, SE // 2) as i:
                    for k in range(2):
                        act.wait_ge(pre_ready[k], i + 1)
                        act.wait_ge(down_product[k], i)
                        act.activation(hid[k][:, :, :], pre[k][:, :, :], ACT.Gelu).then_inc(hid_ready[k], 1)

            @block.vector
            def _(dve):
                ln_vector(dve, s, s.u, s.h, 0, var_ready, rstd_ready).then_inc(u_ready, 1)
                dve.wait_ge(u_transposed, 1)
                dve.tensor_copy(s.uT[:, :, :], ps[0:DK, 0:DC, :]).then_inc(uT_ready, 1)
                logits = ps[:, 2, 0:T * SE].rearrange("p (t e) -> p t e", t=T)
                dve.wait_ge(logits_ready, 1)
                dve.reduce_max(row_max[:, :], logits, AX.X)
                dve.drain()
                dve.tensor_tensor(prob[:, :, :], logits, row_max[:, :].unsqueeze(2).broadcast_to((P, T, SE)), ALU.subtract).then_inc(shifted, 1)
                dve.wait_ge(exp_ready, 1)
                dve.reduce_sum(row_max[:, :], prob[:, :, :], AX.X)
                dve.drain()
                dve.reciprocal(row_max[:, :], row_max[:, :])
                dve.drain()
                dve.tensor_tensor(prob[:, :, :], prob[:, :, :], row_max[:, :].unsqueeze(2).broadcast_to((P, T, SE)), ALU.mult)
                dve.drain()
                for t in range(T):
                    dve.max(top8[:, t, :], prob[:, t, :])
                dve.drain()
                for t in range(T):
                    dve.max_index(top8_at[:, t, :], top8[:, t, :], prob[:, t, :])
                dve.drain()
                dve.tensor_copy(p_max[:, :], top8[:, :, 0])
                dve.tensor_copy(route[:, :], top8_at[:, :, 0]).then_inc(routed, 1)
                dve.wait_ge(consts, 2)
                for t in range(T):
                    dve.tensor_scalar(ahead[:, t, :], iota_j[:, 0:NT], tok_id[:, t:t + 1], None, ALU.is_lt)
                dve.wait_ge(spread, 1)
                dve.tensor_copy(all_p[:, :], ps[:, 3, :])
                dve.tensor_copy(all_r[:, :], ps[:, 4, :])
                dve.drain()
                for src, value, how in ((all_p, p_max, (ALU.is_equal, ALU.mult)), (all_p, p_max, (ALU.is_gt, ALU.add)),
                                        (all_r, route, (ALU.is_equal, ALU.mult))):
                    for t in range(T):
                        dve.scalar_tensor_tensor(out=ahead[:, t, :], in0=src[:, :], scalar=value[:, t:t + 1], in1=ahead[:, t, :],
                                                 op0=how[0], op1=how[1])
                    dve.drain()
                dve.reduce_sum(rank[:, :], ahead[:, :, :], AX.X)
                dve.drain()
                dve.tensor_scalar(keep[:, :], rank[:, :], float(SCAP), None, ALU.is_lt)
                dve.scalar_tensor_tensor(out=dest[:, :], in0=route[:, :], scalar=float(SCAP), in1=rank[:, :], op0=ALU.mult, op1=ALU.add)
                dve.drain()
                dve.scalar_tensor_tensor(out=dest[:, :], in0=dest[:, :], scalar=1.0, in1=keep[:, :], op0=ALU.add, op1=ALU.mult)
                dve.drain()
                dve.tensor_scalar(dest[:, :], dest[:, :], -1.0, None, ALU.add)
                dve.drain()
                for t in range(T):
                    last = dve.tensor_scalar(select[:, t, :], iota_j[:, :], dest[:, t:t + 1], None, ALU.is_equal)
                last.then_inc(select_ready, 1)
                dve.wait_ge(x_product, 1)
                dve.tensor_copy(xT[:, :, :].rearrange("p c (h n) -> p (c h) n", h=2), ps[0:DK, 0:2 * DC, 0:slots // 2]).then_inc(xT_ready, 1)
                with dve.Fori(0, SE // 2) as i:
                    for k in range(2):
                        dve.wait_ge(up_product[k], i + 1)
                        dve.wait_ge(w_in[k], i * 64 + 64)
                        dve.wait_ge(hid_ready[k], i)
                        dve.tensor_tensor(pre[k][:, :, :], ps[:, 4 + k, 0:SM * SCAP].rearrange("p (m n) -> p m n", m=SM),
                                          b1[k][:, :].unsqueeze(2).broadcast_to((P, SM, SCAP)), ALU.add).then_inc(pre_ready[k], 1)
                    for k in range(2):
                        dve.wait_ge(down_product[k], i + 1)
                        dve.tensor_copy(out[:, bass.ds(2 * i + k, 1), :], ps[0:SCAP, 6 + k, 0:D].unsqueeze(1)).then_inc(out_ready[k], 1)
                dve.tensor_scalar(keep[:, :], keep[:, :], -1.0, 1.0, ALU.mult, ALU.add)
                dve.drain()
                dve.wait_ge(back_product, 1)
                for t in range(T):
                    dve.scalar_tensor_tensor(out=s.u[:, t, :], in0=s.u[:, t, :], scalar=keep[:, t:t + 1], in1=ps[:, t, 0:D],
                                             op0=ALU.mult, op1=ALU.add)
                dve.drain()
                for t in range(T):
                    dve.scalar_tensor_tensor(out=s.h[:, t, :], in0=s.u[:, t, :], scalar=p_max[:, t:t + 1], in1=s.h[:, t, :],
                                             op0=ALU.mult, op1=ALU.add)


def laid_out(i):
    g = {k: np.asarray(v) for k, v in i.items()}
    put = {}

    def add(name, a):
        put[name] = np.ascontiguousarray(a)

    add("patches", g["x"].reshape(2, 32, 16, 8, 16, 8).transpose(1, 3, 5, 0, 2, 4).reshape(2048, NT))
    add("conv_w", g["L0_tok_conv_w"].reshape(TD, 2048).T)
    add("conv_b", g["L0_tok_conv_b"].reshape(1, TD))
    add("tok_cols", np.concatenate([np.stack([g["L0_tok_" + k] for k in ("ln1_g", "ln1_b", "ln2_g", "ln2_b")], axis=2),
                                    g["L0_tok_ff1_b"].reshape(LAYERS, FC, P).transpose(0, 2, 1)], axis=2))
    add("tok_rows", np.stack([g["L0_tok_out_b"], g["L0_tok_ff2_b"]], axis=1).reshape(LAYERS, 1, 2, TD))
    add("qkv_w", g["L0_tok_qkv_w"])
    add("out_w", g["L0_tok_out_w"])
    add("ff1_w", g["L0_tok_ff1_w"])
    add("ff2_w", g["L0_tok_ff2_w"])
    add("tok_lnf", np.stack([g["L0_tok_lnf_g"], g["L0_tok_lnf_b"]], axis=1))
    add("head_w", g["L0_tok_head_w"])
    add("head_b", g["L0_tok_head_b"].reshape(1, D))
    add("mb_w_in", g["L0_attn_w_in"].T)
    add("mb_cols", np.concatenate([g["L0_attn_w_conv"][:, 0, :]] + [g["L0_attn_" + k].reshape(DIN, 1)
                                   for k in ("b_conv", "b_dt", "D_param")], axis=1))
    add("mb_a_log", g["L0_attn_A_log"])
    add("mb_w_x", g["L0_attn_w_xproj"].T)
    add("mb_w_dt", g["L0_attn_w_dt"].T)
    add("mb_w_out", g["L0_attn_w_out"].T)
    add("mb_w_norm", g["L0_attn_w_norm"].reshape(1, D))
    add("moe_w_router", g["L0_ffn_Wg"].T)
    add("moe_e_bias", g["L0_ffn_e_bias"].reshape(1, NE))
    add("moe_w_gu", g["L0_ffn_W_gate_up"])
    add("moe_w_d", g["L0_ffn_W_down"])
    add("moe_w_sgu", np.stack([g["L0_ffn_Wsg"], g["L0_ffn_Wsu"]]))
    add("moe_w_sd", g["L0_ffn_Wsd"])
    add("en_ln", np.stack([g["L1_attn_ln_gamma"], g["L1_attn_ln_beta"]], axis=1))
    w = np.stack([g["L1_attn_wq"].reshape(EM, D), g["L1_attn_wk"].reshape(EM, D), g["L1_attn_xi"]])
    add("en_w", w)
    add("en_wT", w.transpose(0, 2, 1))
    add("sw_w_switch", g["L1_ffn_switch_w"])
    add("sw_b_switch", g["L1_ffn_switch_b"].reshape(1, SE))
    add("sw_w1", g["L1_ffn_w1"])
    add("sw_b1", g["L1_ffn_b1"].reshape(SE, SM, P).transpose(0, 2, 1))
    add("sw_w2", g["L1_ffn_w2"])
    add("sw_b2", g["L1_ffn_b2"])
    return put


def vit_tower(nc, a):
    with ExitStack() as ctx:
        s = Shared(nc, ctx)
        setup_stage(nc, s)
        s.end_stage()
        tok_stage(nc, s, a)
        s.end_stage()
        mamba_stage(nc, s, a)
        s.end_stage()
        moe_stage(nc, s, a)
        s.end_stage()
        energy_stage(nc, s, a)
        s.end_stage()
        switch_stage(nc, s, a)
        s.end_stage()
        h_stored = s.stage_semaphore("h_stored")
        with nc.Block() as block:
            @block.sync
            def _(sp):
                sp.dma_start(a["out"].rearrange("(t p) d -> p t d", p=P), s.h[:, :, :]).then_inc(h_stored, 16)
                sp.wait_ge(h_stored, 16)


def kernel(**inputs):
    import concourse.bacc as bacc
    from concourse.bass_utils import run_bass_kernel_spmd

    nc = bacc.Bacc("TRN2", target_bir_lowering=False, num_devices=1)
    put = laid_out(inputs)
    a = {name: nc.dram_tensor("in_" + name, v.shape, mybir.dt.from_np(v.dtype), kind="ExternalInput").ap()
         for name, v in put.items()}
    a["out"] = nc.dram_tensor("out_h", (NT, D), fp32, kind="ExternalOutput").ap()
    vit_tower(nc, a)
    r = run_bass_kernel_spmd(nc, [{"in_" + name: v for name, v in put.items()}], core_ids=[0])
    return r.results[0]["out_h"].reshape(BATCH, SEQ, D)
```

```python
from contextlib import ExitStack

import numpy as np

import concourse.bass as bass
from concourse import mybir
from concourse.alu_op_type import AluOpType as ALU

fp32 = mybir.dt.float32
f32r = mybir.dt.float32r
u32 = mybir.dt.uint32
ACT = mybir.ActivationFunctionType
AX = mybir.AxisListType

P = 128
BATCH, SEQ = 2, 256
NT = BATCH * SEQ
T = NT // P
TB = SEQ // P
D = 192
DK, DC = 96, 2
EPS = 1e-5
BANK = 512

NE = 128
TOP = 6
CAP = 192
SLOTS = 96
GROUPS = NE * CAP // SLOTS
SPARE = GROUPS
CLEARS = 12
CLEAR_COLS = (GROUPS + 1) * SLOTS * D // P // CLEARS


class Shared:

    def __init__(self, nc, ctx):
        self.nc = nc
        self.h = ctx.enter_context(nc.sbuf_tensor("h", [P, T, D], fp32))
        self.u = ctx.enter_context(nc.sbuf_tensor("u", [P, T, D], fp32))
        self.uT = ctx.enter_context(nc.sbuf_tensor("uT", [DK, DC, NT], fp32))
        self.ident = ctx.enter_context(nc.sbuf_tensor("ident", [P, P], fp32))
        self.ones = ctx.enter_context(nc.sbuf_tensor("ones", [P, P], fp32))
        self.neghalf = ctx.enter_context(nc.sbuf_tensor("neghalf", [P, T], fp32))
        self.stats = ctx.enter_context(nc.sbuf_tensor("stats", [P, T, 6], fp32))
        self.mv = ctx.enter_context(nc.sbuf_tensor("mv", [P, T, 2], fp32))
        self.var = ctx.enter_context(nc.sbuf_tensor("var", [P, T], fp32))
        self.rstd = ctx.enter_context(nc.sbuf_tensor("rstd", [P, T], fp32))
        self.ps = ctx.enter_context(nc.psum_tensor("ps", [P, 8, BANK], fp32))
        self.y_of_slot = nc.dram_tensor("y_of_slot", [(GROUPS + 1) * SLOTS, D], fp32).ap()
        self.stage_semaphores = []

    def stage_semaphore(self, name):
        self.stage_semaphores.append(self.nc.alloc_semaphore(name))
        return self.stage_semaphores[-1]

    def end_stage(self):
        self.nc.clear_and_free_semaphores(self.stage_semaphores)
        self.stage_semaphores = []
        self.nc.all_engine_barrier()


def setup_stage(nc, s):
    consts_set = s.stage_semaphore("consts_set")
    with nc.Block() as block:
        @block.gpsimd
        def _(pool):
            pool.memset(s.ident[:, :], 0.0).then_inc(consts_set, 1)
            pool.memset(s.ones[:, :], 1.0).then_inc(consts_set, 1)
            pool.memset(s.neghalf[:, :], -0.5).then_inc(consts_set, 1)
            pool.wait_ge(consts_set, 3)
            pool.affine_select(out=s.ident[:, :], in_=s.ident[:, :], compare_op=ALU.not_equal,
                               fill=1.0, base=0, pattern=[[-1, P]], channel_multiplier=1)


def clear_table(sp, s, zeros, cleared):
    lot = (GROUPS + 1) * SLOTS // CLEARS
    for n in range(CLEARS):
        sp.dma_start(s.y_of_slot[n * lot:(n + 1) * lot, :].rearrange("r d -> (r d)").rearrange("(p n) -> p n", p=P),
                     zeros[:, :]).then_inc(cleared, 16)


def ln_vector(dve, s, y, x, n, var_ready, rstd_ready):
    for t in range(T):
        dve.bn_stats(s.stats[:, t, :], x[:, t, :])
    dve.drain()
    for t in range(T):
        dve.bn_aggr(s.mv[:, t, :], s.stats[:, t, :])
    dve.drain()
    dve.tensor_scalar(s.var[:, :], s.mv[:, :, 1], EPS, None, ALU.add).then_inc(var_ready, 1)
    dve.wait_ge(rstd_ready, n + 1)
    for t in range(T):
        last = dve.tensor_scalar(y[:, t, :], x[:, t, :], s.mv[:, t, 0:1], s.rstd[:, t:t + 1],
                                 ALU.subtract, ALU.mult)
    return last


def ln_pool(pool, s, n, var_ready, rstd_ready):
    pool.wait_ge(var_ready, n + 1)
    pool.tensor_tensor(s.rstd[:, :], s.var[:, :], s.neghalf[:, :], ALU.pow).then_inc(rstd_ready, 1)


def transpose_u(pe, s):
    for c in range(DC):
        for t in range(T):
            last = pe.transpose(s.ps[0:DK, c, t * P:(t + 1) * P], s.u[:, t, c * DK:(c + 1) * DK],
                                s.ident[:, :])
    return last


TD = 128
HEADS, DH = 8, 64
INNER = HEADS * DH
IC = INNER // P
KC = 2048 // P
FM = 512
FC = FM // P
LAYERS = 2


def tok_stage(nc, s, a):
    ctx = ExitStack()
    with ctx:
        def sb(name, shape):
            return ctx.enter_context(nc.sbuf_tensor(name, shape, fp32))

        def sem(name):
            return s.stage_semaphore(name)

        patches = sb("patches", [P, KC, NT])
        conv_w = sb("conv_w", [P, KC, TD])
        conv_b = sb("conv_b", [1, TD])
        x = sb("tok_x", [P, T, TD])
        y = sb("tok_y", [P, T, TD])
        yT = sb("tok_yT", [P, NT])
        cols = sb("tok_cols", [P, 8])
        rows = sb("tok_rows", [1, 2, TD])
        wqkv = sb("tok_wqkv", [P, 3 * INNER])
        wo = sb("tok_wo", [P, IC, TD])
        w1 = sb("tok_w1", [P, FM])
        w2 = sb("tok_w2", [P, FC, TD])
        lnf = sb("tok_lnf", [P, 2])
        head_w = sb("tok_head_w", [P, D])
        head_b = sb("tok_head_b", [1, D])
        kT = sb("tok_kT", [P, IC, NT])
        kneg = sb("tok_kneg", [P, IC, BATCH])
        ksum = sb("tok_ksum", [P, IC, BATCH])
        krec = sb("tok_krec", [P, IC, BATCH])
        k = sb("tok_k", [P, T, INNER])
        q = sb("tok_q", [P, T, INNER])
        qmax = sb("tok_qmax", [P, T, HEADS])
        qsum = sb("tok_qsum", [P, T, HEADS])
        qT = sb("tok_qT", [P, IC, NT])
        v = sb("tok_v", [P, T, INNER])
        ctxT = sb("tok_ctx", [P, BATCH, IC, P])
        attT = sb("tok_attT", [P, IC, NT])
        hidT = sb("tok_hidT", [P, FC, NT])
        zeros = sb("tok_zeros", [P, CLEAR_COLS])
        ps = s.ps

        zeros_ready = sem("tok_zeros_ready")
        cleared = sem("tok_cleared")
        patch_in = [sem(f"patch_in{g}") for g in range(4)]
        head_in = sem("tok_head_in")
        weights_in = sem("tok_weights_in")
        layer_done = sem("tok_layer_done")
        embedded = sem("tok_embedded")
        x_ready = sem("tok_x_ready")
        var_ready, rstd_ready = sem("tok_var_ready"), sem("tok_rstd_ready")
        y_ready = sem("tok_y_ready")
        y_transposed = sem("tok_y_transposed")
        yT_ready = sem("tok_yT_ready")
        kT_scores = sem("tok_kT_scores")
        k_max = sem("tok_k_max")
        k_exp = sem("tok_k_exp")
        q_scores = sem("tok_q_scores")
        q_shifted = sem("tok_q_shifted")
        q_exp = sem("tok_q_exp")
        q_normed = sem("tok_q_normed")
        v_product = sem("tok_v_product")
        v_ready = sem("tok_v_ready")
        k_transposed = sem("tok_k_transposed")
        k_ready = sem("tok_k_ready")
        q_transposed = sem("tok_q_transposed")
        qT_ready = sem("tok_qT_ready")
        ctx_zeroed = sem("tok_ctx_zeroed")
        ctx_product = sem("tok_ctx_product")
        ctx_ready = sem("tok_ctx_ready")
        att_product = sem("tok_att_product")
        att_ready = sem("tok_att_ready")
        out_product = sem("tok_out_product")
        hid_product = sem("tok_hid_product")
        hid_ready = sem("tok_hid_ready")
        ff_product = sem("tok_ff_product")
        head_product = sem("tok_head_product")

        with nc.Block() as block:
            @block.sync
            def _(sp):
                patch_v = a["patches"].rearrange("(k p) t -> p k t", p=P)
                conv_v = a["conv_w"].rearrange("(k p) d -> p k d", p=P)
                for g in range(4):
                    lot = slice(g * KC // 4, (g + 1) * KC // 4)
                    sp.dma_start(conv_w[:, lot, :], conv_v[:, lot, :]).then_inc(patch_in[g], 16)
                    sp.dma_start(patches[:, lot, :], patch_v[:, lot, :]).then_inc(patch_in[g], 16)
                sp.dma_start(conv_b[:, :], a["conv_b"]).then_inc(head_in, 16)
                sp.dma_start(lnf[:, :], a["tok_lnf"]).then_inc(head_in, 16)
                sp.dma_start(head_w[:, :], a["head_w"]).then_inc(head_in, 16)
                sp.dma_start(head_b[:, :], a["head_b"]).then_inc(head_in, 16)
                with sp.Fori(0, LAYERS) as l:
                    sp.wait_ge(layer_done, l + 1)
                    sp.dma_start(cols[:, :], a["tok_cols"][l]).then_inc(weights_in, 16)
                    sp.dma_start(wqkv[:, :], a["qkv_w"][l]).then_inc(weights_in, 16)
                    sp.dma_start(rows[:, :, :], a["tok_rows"][l]).then_inc(weights_in, 16)
                    sp.dma_start(wo[:, :, :], a["out_w"][l].rearrange("(c p) d -> p c d", p=P)).then_inc(weights_in, 16)
                    sp.dma_start(w1[:, :], a["ff1_w"][l]).then_inc(weights_in, 16)
                    sp.dma_start(w2[:, :, :], a["ff2_w"][l].rearrange("(c p) d -> p c d", p=P)).then_inc(weights_in, 16)
                sp.wait_ge(zeros_ready, 1)
                clear_table(sp, s, zeros, cleared)
                sp.wait_ge(cleared, CLEARS * 16)

            @block.gpsimd
            def _(pool):
                pool.memset(ctxT[:, :, :, :], 0.0).then_inc(ctx_zeroed, 1)
                pool.wait_ge(ctx_zeroed, 1)
                pool.memset(zeros[:, :], 0.0).then_inc(zeros_ready, 1)
                pool.wait_ge(zeros_ready, 1)
                with pool.Fori(0, 2 * LAYERS + 1) as n:
                    ln_pool(pool, s, n, var_ready, rstd_ready)

            @block.tensor
            def _(pe):
                for g in range(4):
                    pe.wait_ge(patch_in[g], 32)
                    for kc in range(g * KC // 4, (g + 1) * KC // 4):
                        for t in range(T):
                            pe.matmul(ps[:, t, 0:TD], lhsT=patches[:, kc, t * P:(t + 1) * P],
                                      rhs=conv_w[:, kc, :], start=(kc == 0), stop=False)
                pe.wait_ge(head_in, 64)
                for t in range(T):
                    last = pe.matmul(ps[:, t, 0:TD], lhsT=s.ones[0:1, :], rhs=conv_b[:, :],
                                     start=False, stop=True)
                last.then_inc(embedded, 1)

                def transpose_y(n):
                    pe.wait_ge(y_ready, n + 1)
                    for t in range(T):
                        last = pe.transpose(ps[:, 0, t * P:(t + 1) * P], y[:, t, :], s.ident[:, :])
                    last.then_inc(y_transposed, 1)
                    pe.wait_ge(yT_ready, n + 1)

                with pe.Fori(0, LAYERS) as l:
                    transpose_y(2 * l)
                    pe.wait_ge(weights_in, l * 96 + 96)
                    for c in range(IC):
                        pe.matmul(ps[:, 1 + c, :], lhsT=wqkv[:, INNER + c * P:INNER + (c + 1) * P],
                                  rhs=yT[:, :], start=True, stop=True).then_inc(kT_scores, 1)
                    for t in range(T):
                        pe.matmul(ps[:, (5 + t) % 8, :], lhsT=yT[:, t * P:(t + 1) * P],
                                  rhs=wqkv[:, 0:INNER], start=True, stop=True).then_inc(q_scores, 1)
                    for t in range(T):
                        pe.wait_ge(k_exp, l * IC + t + 1)
                        pe.matmul(ps[:, 1 + t, :], lhsT=yT[:, t * P:(t + 1) * P],
                                  rhs=wqkv[:, 2 * INNER:3 * INNER], start=True, stop=True).then_inc(v_product, 1)
                    for t in range(T):
                        pe.wait_ge(q_shifted, l * T + t + 1)
                        for c in range(IC):
                            last = pe.transpose(ps[:, (5 + t) % 8, c * P:(c + 1) * P],
                                                kT[:, c, t * P:(t + 1) * P], s.ident[:, :])
                        last.then_inc(k_transposed, 1)
                    for c in range(IC):
                        pe.wait_ge(q_normed, l * T + T)
                        pe.wait_ge(v_ready, l * T + c + 1)
                        for t in range(T):
                            last = pe.transpose(ps[:, 1 + c, t * P:(t + 1) * P],
                                                q[:, t, c * P:(c + 1) * P], s.ident[:, :])
                        last.then_inc(q_transposed, 1)
                    pe.wait_ge(k_ready, l * T + T)
                    pe.wait_ge(v_ready, l * T + T)
                    for b in range(BATCH):
                        for c in range(IC):
                            for i in range(TB):
                                last = pe.matmul(ps[:, 5 + b, c * P:(c + 1) * P],
                                                 lhsT=k[:, b * TB + i, c * P:(c + 1) * P],
                                                 rhs=v[:, b * TB + i, c * P:(c + 1) * P],
                                                 start=(i == 0), stop=(i == TB - 1))
                        last.then_inc(ctx_product, 1)
                    pe.wait_ge(ctx_ready, l + 1)
                    for c in range(IC):
                        pe.wait_ge(qT_ready, l * IC + c + 1)
                        for b in range(BATCH):
                            last = pe.matmul(ps[:, 1 + c, b * SEQ:(b + 1) * SEQ], lhsT=ctxT[:, b, c, :],
                                             rhs=qT[:, c, b * SEQ:(b + 1) * SEQ], start=True, stop=True)
                        last.then_inc(att_product, 1)
                    pe.wait_ge(att_ready, l * IC + IC)
                    for t in range(T):
                        for c in range(IC):
                            pe.matmul(ps[:, 7, t * TD:(t + 1) * TD], lhsT=attT[:, c, t * P:(t + 1) * P],
                                      rhs=wo[:, c, :], start=(c == 0), stop=False)
                        last = pe.matmul(ps[:, 7, t * TD:(t + 1) * TD], lhsT=s.ones[0:1, :],
                                         rhs=rows[:, 0, :], start=False, stop=True)
                    last.then_inc(out_product, 1)
                    transpose_y(2 * l + 1)
                    for m in range(FC):
                        pe.matmul(ps[:, 1 + m, :], lhsT=w1[:, m * P:(m + 1) * P], rhs=yT[:, :],
                                  start=True, stop=True).then_inc(hid_product, 1)
                    pe.wait_ge(hid_ready, l * FC + FC)
                    for t in range(T):
                        for m in range(FC):
                            pe.matmul(ps[:, 7, t * TD:(t + 1) * TD], lhsT=hidT[:, m, t * P:(t + 1) * P],
                                      rhs=w2[:, m, :], start=(m == 0), stop=False)
                        last = pe.matmul(ps[:, 7, t * TD:(t + 1) * TD], lhsT=s.ones[0:1, :],
                                         rhs=rows[:, 1, :], start=False, stop=True)
                    last.then_inc(ff_product, 1)
                transpose_y(2 * LAYERS)
                for t in range(T):
                    pe.matmul(ps[:, 1 + t, 0:D], lhsT=yT[:, t * P:(t + 1) * P], rhs=head_w[:, :],
                              start=True, stop=False)
                    pe.matmul(ps[:, 1 + t, 0:D], lhsT=s.ones[0:1, :], rhs=head_b[:, :],
                              start=False, stop=True).then_inc(head_product, 1)

            @block.vector
            def _(dve):
                dve.sem_inc(layer_done, 1)
                dve.wait_ge(embedded, 1)
                dve.tensor_copy(x[:, :, :], ps[:, 0:T, 0:TD])
                dve.drain()

                def normalise(n, gain, shift):
                    ln_vector(dve, s, y, x, n, var_ready, rstd_ready).then_inc(y_ready, 1)
                    dve.wait_ge(y_transposed, n + 1)
                    dve.tensor_scalar(yT[:, :], ps[:, 0, :], gain, shift, ALU.mult, ALU.add).then_inc(yT_ready, 1)

                with dve.Fori(0, LAYERS) as l:
                    dve.wait_ge(weights_in, l * 96 + 96)
                    normalise(2 * l, cols[:, 0:1], cols[:, 1:2])
                    for c in range(IC):
                        dve.wait_ge(kT_scores, l * IC + c + 1)
                        dve.tensor_reduce(kneg[:, c, :], ps[:, 1 + c, :].rearrange("p (b n) -> p b n", b=BATCH),
                                          axis=AX.X, op=ALU.max, negate=True).then_inc(k_max, 1)
                    for t in range(T):
                        bank = ps[:, (5 + t) % 8, :].rearrange("p (h d) -> p h d", h=HEADS)
                        dve.wait_ge(q_scores, l * T + t + 1)
                        dve.reduce_max(qmax[:, t, :], bank, AX.X)
                        dve.drain()
                        dve.tensor_tensor(q[:, t, :].rearrange("p (h d) -> p h d", h=HEADS), bank,
                                          qmax[:, t, :].unsqueeze(2).broadcast_to((P, HEADS, DH)),
                                          ALU.subtract).then_inc(q_shifted, 1)
                    for t in range(T):
                        head = q[:, t, :].rearrange("p (h d) -> p h d", h=HEADS)
                        dve.wait_ge(q_exp, l * T + t + 1)
                        dve.reduce_sum(qsum[:, t, :], head, AX.X)
                        dve.drain()
                        dve.reciprocal(qsum[:, t, :], qsum[:, t, :])
                        dve.drain()
                        dve.tensor_tensor(head, head, qsum[:, t, :].unsqueeze(2).broadcast_to((P, HEADS, DH)),
                                          ALU.mult).then_inc(q_normed, 1)
                    dve.wait_ge(k_exp, l * IC + IC)
                    dve.reciprocal(krec[:, :, :], ksum[:, :, :])
                    dve.drain()
                    dve.tensor_scalar(krec[:, :, :], krec[:, :, :], float(DH) ** -0.5, None, ALU.mult)
                    for t in range(T):
                        dve.wait_ge(k_transposed, l * T + t + 1)
                        dve.tensor_copy(k[:, t, :], ps[:, (5 + t) % 8, :]).then_inc(k_ready, 1)
                    for c in range(IC):
                        dve.wait_ge(q_transposed, l * IC + c + 1)
                        dve.tensor_copy(qT[:, c, :], ps[:, 1 + c, :]).then_inc(qT_ready, 1)
                    dve.wait_ge(ctx_zeroed, 1)
                    dve.wait_ge(ctx_product, l * BATCH + BATCH)
                    for b in range(BATCH):
                        for c in range(IC):
                            for r in (slice(0, DH), slice(DH, P)):
                                last = dve.tensor_scalar(ctxT[r, b, c, r], ps[r, 5 + b, c * P + r.start:c * P + r.stop],
                                                         krec[r, c, b:b + 1], None, ALU.mult)
                    last.then_inc(ctx_ready, 1)
                    for c in range(IC):
                        dve.wait_ge(att_product, l * IC + c + 1)
                        dve.tensor_copy(attT[:, c, :], ps[:, 1 + c, :]).then_inc(att_ready, 1)
                    dve.wait_ge(out_product, l + 1)
                    dve.tensor_tensor(x[:, :, :], x[:, :, :], ps[:, 7, :].rearrange("p (t d) -> p t d", t=T), ALU.add)
                    dve.drain()
                    normalise(2 * l + 1, cols[:, 2:3], cols[:, 3:4])
                    dve.wait_ge(ff_product, l + 1)
                    dve.tensor_tensor(x[:, :, :], x[:, :, :], ps[:, 7, :].rearrange("p (t d) -> p t d", t=T),
                                      ALU.add).then_inc(layer_done, 1)
                    dve.wait_ge(layer_done, l + 2)
                dve.wait_ge(head_in, 64)
                normalise(2 * LAYERS, lnf[:, 0:1], lnf[:, 1:2])
                for t in range(T):
                    dve.wait_ge(head_product, t + 1)
                    dve.tensor_copy(s.h[:, t, :], ps[:, 1 + t, 0:D])

            @block.scalar
            def _(act):
                with act.Fori(0, LAYERS) as l:
                    for c in range(IC):
                        act.wait_ge(k_max, l * IC + c + 1)
                        for b in range(BATCH):
                            last = act.activation(kT[:, c, b * SEQ:(b + 1) * SEQ], ps[:, 1 + c, b * SEQ:(b + 1) * SEQ],
                                                  ACT.Exp, bias=kneg[:, c, b:b + 1], accum_out=ksum[:, c, b:b + 1])
                        last.then_inc(k_exp, 1)
                    for t in range(T):
                        act.wait_ge(q_shifted, l * T + t + 1)
                        act.activation(q[:, t, :], q[:, t, :], ACT.Exp).then_inc(q_exp, 1)
                    for t in range(T):
                        act.wait_ge(v_product, l * T + t + 1)
                        act.copy(v[:, t, :], ps[:, 1 + t, :]).then_inc(v_ready, 1)
                    for m in range(FC):
                        act.wait_ge(hid_product, l * FC + m + 1)
                        act.activation(hidT[:, m, :], ps[:, 1 + m, :], ACT.Gelu, bias=cols[:, 4 + m:5 + m]).then_inc(hid_ready, 1)


DIN = 2 * D
MC = DIN // P
NS = 16
KW = 4
R = (D + 15) // 16
PAD = KW - 1
BC_SLOTS = 4


def mamba_stage(nc, s, a):
    ctx = ExitStack()
    with ctx:
        def sb(name, shape):
            return ctx.enter_context(nc.sbuf_tensor(name, shape, fp32))

        def sem(name):
            return s.stage_semaphore(name)

        w_in = sb("mb_w_in", [DK, DC, 2 * DIN])
        cols = sb("mb_cols", [P, MC, KW + 3])
        a_log = sb("mb_a_log", [P, MC, NS])
        w_x = sb("mb_w_x", [P, MC, R + 2 * NS])
        w_dt = sb("mb_w_dt", [R, DIN])
        w_out = sb("mb_w_out", [P, MC, D])
        w_norm = sb("mb_w_norm", [P, D])
        xp = sb("mb_xp", [P, MC, BATCH, PAD + SEQ])
        xc = sb("mb_xc", [P, MC, NT])
        z = sb("mb_z", [P, MC, NT])
        dbc = sb("mb_dbc", [R + 2 * NS, NT])
        dt = sb("mb_dt", [P, MC, NT])
        soft = sb("mb_soft", [P, MC, NT])
        dtx = sb("mb_dtx", [P, MC, NT])
        b_all = sb("mb_b_all", [P, BC_SLOTS, NT])
        c_all = sb("mb_c_all", [P, BC_SLOTS, NT])
        decay = sb("mb_decay", [P, 2, MC, NT])
        drive = sb("mb_drive", [P, MC, NT])
        state = sb("mb_state", [P, 2, MC, NT])
        out_n = sb("mb_out_n", [P, 2, MC, NT])
        r = sb("mb_r", [P, T, D])
        sq = sb("mb_sq", [P, T, D])
        bc_dram = nc.dram_tensor("bc_rows", [2 * NS, NT], fp32).ap()
        ps = s.ps

        weights_in = sem("mb_weights_in")
        var_ready, rstd_ready = sem("mb_var_ready"), sem("mb_rstd_ready")
        pad_zeroed = sem("mb_pad_zeroed")
        u_ready = sem("mb_u_ready")
        u_transposed = sem("mb_u_transposed")
        uT_ready = sem("mb_uT_ready")
        x_product = sem("mb_x_product")
        conv_done = sem("mb_conv_done")
        xc_ready = sem("mb_xc_ready")
        dbc_product = sem("mb_dbc_product")
        dbc_ready = sem("mb_dbc_ready")
        bc_stored = sem("mb_bc_stored")
        dt_product = sem("mb_dt_product")
        biased = sem("mb_biased")
        log_ready = sem("mb_log_ready")
        dt_ready = sem("mb_dt_ready")
        a_exp = sem("mb_a_exp")
        a_ready = sem("mb_a_ready")
        skip_ready = sem("mb_skip_ready")
        bc_in = [sem(f"mb_bc_in{k}") for k in range(BC_SLOTS)]
        decay_ready = sem("mb_decay_ready")
        decay_free = sem("mb_decay_free")
        b_free = sem("mb_b_free")
        c_free = sem("mb_c_free")
        state_ready = sem("mb_state_ready")
        out_ready = sem("mb_out_ready")
        out_summed = sem("mb_out_summed")
        gated = sem("mb_gated")
        out_product = sem("mb_out_product")

        with nc.Block() as block:
            @block.sync
            def _(sp):
                sp.dma_start(w_in[:, :, :], a["mb_w_in"].rearrange("(c p) e -> p c e", p=DK)).then_inc(weights_in, 16)
                sp.dma_start(cols[:, :, :], a["mb_cols"].rearrange("(c p) k -> p c k", p=P)).then_inc(weights_in, 16)
                sp.dma_start(a_log[:, :, :], a["mb_a_log"].rearrange("(c p) k -> p c k", p=P)).then_inc(weights_in, 16)
                sp.dma_start(w_x[:, :, :], a["mb_w_x"].rearrange("(c p) k -> p c k", p=P)).then_inc(weights_in, 16)
                sp.dma_start(w_dt[:, :], a["mb_w_dt"]).then_inc(weights_in, 16)
                sp.dma_start(w_out[:, :, :], a["mb_w_out"].rearrange("(c p) k -> p c k", p=P)).then_inc(weights_in, 16)
                sp.dma_start(w_norm[:, :], a["mb_w_norm"].broadcast_to((P, D))).then_inc(weights_in, 16)
                sp.wait_ge(dbc_ready, 1)
                sp.dma_start(bc_dram, dbc[R:R + 2 * NS, :]).then_inc(bc_stored, 16)
                sp.wait_ge(bc_stored, 16)
                with sp.Fori(0, NS // BC_SLOTS) as i:
                    for k in range(BC_SLOTS):
                        sp.wait_ge(b_free, i * BC_SLOTS + k + 1)
                        sp.wait_ge(c_free, i * BC_SLOTS + k + 1)
                        sp.dma_start(b_all[:, k, :], bc_dram[bass.ds(i * BC_SLOTS + k, 1), :].broadcast_to((P, NT))).then_inc(bc_in[k], 16)
                        sp.dma_start(c_all[:, k, :], bc_dram[bass.ds(i * BC_SLOTS + k + NS, 1), :].broadcast_to((P, NT))).then_inc(bc_in[k], 16)

            @block.gpsimd
            def _(pool):
                pool.memset(xp[:, :, :, 0:PAD], 0.0).then_inc(pad_zeroed, 1)
                ln_pool(pool, s, 0, var_ready, rstd_ready)
                pool.sem_inc(c_free, BC_SLOTS)
                with pool.Fori(0, NS // BC_SLOTS) as i:
                    for k in range(BC_SLOTS):
                        n = i * BC_SLOTS + k
                        pool.wait_ge(bc_in[k], i * 32 + 32)
                        for c in range(MC):
                            pool.wait_ge(state_ready, n * MC + c + 1)
                            pool.wait_ge(out_summed, n * MC + c + 1)
                            pool.tensor_tensor(out_n[:, k % 2, c, :], state[:, k % 2, c, :], c_all[:, k, :], ALU.mult).then_inc(out_ready, 1)
                            pool.wait_ge(out_ready, n * MC + c + 1)
                        pool.sem_inc(c_free, 1)
                ln_pool(pool, s, 1, var_ready, rstd_ready)

            @block.tensor
            def _(pe):
                pe.wait_ge(u_ready, 1)
                transpose_u(pe, s).then_inc(u_transposed, 1)
                pe.wait_ge(uT_ready, 1)
                pe.wait_ge(weights_in, 7 * 16)
                for c in range(2 * MC):
                    for kc in range(DC):
                        last = pe.matmul(ps[:, 2 + c, :], lhsT=w_in[:, kc, c * P:(c + 1) * P], rhs=s.uT[:, kc, :],
                                         start=(kc == 0), stop=(kc == DC - 1))
                    last.then_inc(x_product, 1)
                pe.wait_ge(xc_ready, MC)
                for c in range(MC):
                    last = pe.matmul(ps[0:R + 2 * NS, 0, :], lhsT=w_x[:, c, :], rhs=xc[:, c, :],
                                     start=(c == 0), stop=(c == MC - 1))
                last.then_inc(dbc_product, 1)
                pe.wait_ge(dbc_ready, 1)
                for c in range(MC):
                    pe.matmul(ps[:, 2 + c, :], lhsT=w_dt[:, c * P:(c + 1) * P], rhs=dbc[0:R, :],
                              start=True, stop=True).then_inc(dt_product, 1)
                pe.wait_ge(xc_ready, 2 * MC)
                for c in range(MC):
                    pe.wait_ge(skip_ready, c + 1)
                    pe.matmul(ps[:, 5 + c, :], lhsT=s.ident[:, :], rhs=soft[:, c, :], start=True, stop=False,
                                     skip_group_check=True)
                pe.sem_inc(out_summed, 2 * MC)
                with pe.Fori(0, NS // 2) as i:
                    for k in range(2):
                        for c in range(MC):
                            pe.wait_ge(out_ready, (2 * i + k) * MC + c + 1)
                            pe.matmul(ps[:, 5 + c, :], lhsT=s.ident[:, :], rhs=out_n[:, k, c, :], start=False, stop=False,
                                      skip_group_check=True).then_inc(out_summed, 1)
                pe.wait_ge(gated, 1)
                for t in range(T):
                    for c in range(MC):
                        last = pe.matmul(ps[:, t, 0:D], lhsT=xc[:, c, t * P:(t + 1) * P], rhs=w_out[:, c, :],
                                         start=(c == 0), stop=(c == MC - 1))
                last.then_inc(out_product, 1)

            @block.vector
            def _(dve):
                ln_vector(dve, s, s.u, s.h, 0, var_ready, rstd_ready).then_inc(u_ready, 1)
                dve.wait_ge(u_transposed, 1)
                dve.tensor_copy(s.uT[:, :, :], ps[0:DK, 0:DC, :]).then_inc(uT_ready, 1)
                dve.wait_ge(weights_in, 7 * 16)
                dve.wait_ge(pad_zeroed, 1)
                for c in range(MC):
                    dve.wait_ge(x_product, c + 1)
                    dve.tensor_copy(xp[:, c, :, PAD:], ps[:, 2 + c, :].rearrange("p (b n) -> p b n", b=BATCH))
                    dve.drain()
                    acc = xc[:, c, :].rearrange("p (b n) -> p b n", b=BATCH)
                    dve.tensor_scalar(acc, xp[:, c, :, 0:SEQ], cols[:, c, 0:1], None, ALU.mult)
                    for k in range(1, KW):
                        dve.drain()
                        last = dve.scalar_tensor_tensor(out=acc, in0=xp[:, c, :, k:k + SEQ], scalar=cols[:, c, k:k + 1],
                                                        in1=acc, op0=ALU.mult, op1=ALU.add)
                    last.then_inc(conv_done, 1)
                dve.wait_ge(a_exp, 1)
                dve.tensor_scalar(a_log[:, :, :], a_log[:, :, :], -1.0, None, ALU.mult).then_inc(a_ready, 1)
                for c in range(MC):
                    dve.wait_ge(dt_product, c + 1)
                    dve.tensor_scalar(dt[:, c, :], ps[:, 2 + c, :], cols[:, c, KW + 1:KW + 2], None, ALU.add).then_inc(biased, 1)
                for c in range(MC):
                    dve.wait_ge(log_ready, c + 1)
                    dve.scalar_tensor_tensor(out=dt[:, c, :], in0=dt[:, c, :], scalar=0.0, in1=soft[:, c, :],
                                             op0=ALU.max, op1=ALU.add).then_inc(dt_ready, 1)
                    dve.drain()
                    dve.tensor_tensor(dtx[:, c, :], dt[:, c, :], xc[:, c, :], ALU.mult)
                    dve.tensor_scalar(soft[:, c, :], xc[:, c, :], cols[:, c, KW + 2:KW + 3], None, ALU.mult).then_inc(skip_ready, 1)
                dve.drain()
                dve.sem_inc(decay_free, 2)
                dve.sem_inc(b_free, BC_SLOTS)
                with dve.Fori(0, NS // BC_SLOTS) as i:
                    for k in range(BC_SLOTS):
                        n = i * BC_SLOTS + k
                        dve.wait_ge(bc_in[k], i * 32 + 32)
                        for c in range(MC):
                            last = dve.tensor_tensor(drive[:, c, :], dtx[:, c, :], b_all[:, k, :], ALU.mult)
                        last.then_inc(b_free, 1)
                        dve.drain()
                        dve.wait_ge(c_free, n + BC_SLOTS - 1)
                        for c in range(MC):
                            dve.wait_ge(decay_ready, n * MC + c + 1)
                            for b in range(BATCH):
                                seq = slice(b * SEQ, (b + 1) * SEQ)
                                last = dve.tensor_tensor_scan(state[:, k % 2, c, seq], decay[:, k % 2, c, seq], drive[:, c, seq],
                                                              0.0, ALU.mult, ALU.add)
                            last.then_inc(state_ready, 1)
                        dve.drain()
                        dve.sem_inc(decay_free, 1)
                dve.wait_ge(out_summed, (NS + 2) * MC)
                for c in range(MC):
                    last = dve.tensor_tensor(xc[:, c, :], ps[:, 5 + c, :], z[:, c, :], ALU.mult)
                last.then_inc(gated, 1)
                dve.wait_ge(out_product, 1)
                dve.tensor_tensor(r[:, :, :], ps[:, 0:T, 0:D], s.u[:, :, :], ALU.add)
                dve.drain()
                dve.tensor_tensor(sq[:, :, :], r[:, :, :], r[:, :, :], ALU.mult)
                dve.drain()
                dve.reduce_sum(s.var[:, :], sq[:, :, :], AX.X)
                dve.drain()
                dve.tensor_scalar(s.var[:, :], s.var[:, :], 1.0 / D, EPS, ALU.mult, ALU.add).then_inc(var_ready, 1)
                dve.wait_ge(rstd_ready, 2)
                for t in range(T):
                    dve.scalar_tensor_tensor(out=r[:, t, :], in0=r[:, t, :], scalar=s.rstd[:, t:t + 1], in1=w_norm[:, :],
                                             op0=ALU.mult, op1=ALU.mult)
                dve.drain()
                dve.tensor_tensor(s.h[:, :, :], s.h[:, :, :], r[:, :, :], ALU.add)

            @block.scalar
            def _(act):
                act.wait_ge(weights_in, 7 * 16)
                for c in range(MC):
                    act.wait_ge(conv_done, c + 1)
                    act.activation(xc[:, c, :], xc[:, c, :], ACT.Silu, bias=cols[:, c, KW:KW + 1]).then_inc(xc_ready, 1)
                for c in range(MC):
                    act.wait_ge(x_product, MC + c + 1)
                    act.activation(z[:, c, :], ps[:, 5 + c, :], ACT.Silu).then_inc(xc_ready, 1)
                act.wait_ge(dbc_product, 1)
                act.copy(dbc[:, :], ps[0:R + 2 * NS, 0, :]).then_inc(dbc_ready, 1)
                act.activation(a_log[:, :, :], a_log[:, :, :], ACT.Exp).then_inc(a_exp, 1)
                for c in range(MC):
                    act.wait_ge(biased, c + 1)
                    act.activation(soft[:, c, :], dt[:, c, :], ACT.Abs)
                act.drain()
                for c in range(MC):
                    act.activation(soft[:, c, :], soft[:, c, :], ACT.Exp, scale=-1.0)
                act.drain()
                for c in range(MC):
                    act.activation(soft[:, c, :], soft[:, c, :], ACT.Ln, bias=1.0).then_inc(log_ready, 1)
                act.wait_ge(a_ready, 1)
                act.wait_ge(dt_ready, MC)
                with act.Fori(0, NS // 2) as i:
                    for k in range(2):
                        n = i * 2 + k
                        act.wait_ge(decay_free, n + 1)
                        for c in range(MC):
                            act.activation(decay[:, k, c, :], dt[:, c, :], ACT.Exp,
                                           scale=a_log[:, c, bass.ds(n, 1)]).then_inc(decay_ready, 1)


NI = 464
IK, IN_ = 116, 4
SI = 8
S_POOL = 5
ROUTED_SCALE = 2.5
S_BANKS = ((0, 1), (2, 7))


def moe_stage(nc, s, a):
    ctx = ExitStack()
    with ctx:
        def sb(name, shape, dt=fp32):
            return ctx.enter_context(nc.sbuf_tensor(name, shape, dt))

        def sem(name):
            return s.stage_semaphore(name)

        w_router = sb("moe_w_router", [DK, DC, NE])
        e_bias = sb("moe_e_bias", [P, NE])
        sig = sb("moe_sig", [P, T, NE])
        choice = sb("moe_choice", [P, T, NE])
        top8 = sb("moe_top8", [P, T, 8])
        top8_at = sb("moe_top8_at", [P, T, 8], u32)
        expert = sb("moe_expert", [P, TOP, T])
        iota_j = sb("moe_iota_j", [P, GROUPS])
        iota_p = sb("moe_iota_p", [P, 1])
        tok_id = sb("moe_tok_id", [P, T])
        before = sb("moe_before", [P, P])
        onehot = sb("moe_onehot", [P, TOP, T, NE])
        picked = sb("moe_picked", [P, TOP, T, NE])
        mask = sb("moe_mask", [P, T, NE])
        pos = sb("moe_pos", [P, T, NE])
        sig_k = sb("moe_sig_k", [P, TOP, T])
        pos_k = sb("moe_pos_k", [P, TOP, T])
        den = sb("moe_den", [P, T])
        weight = sb("moe_weight", [P, TOP, T])
        valid = sb("moe_valid", [P, TOP, T])
        slot_f = sb("moe_slot_f", [P, TOP, T])
        pos_v = sb("moe_pos_v", [P, TOP, T])
        tok_here = sb("moe_tok_here", [P, TOP, T, CAP])
        read_at = sb("moe_read_at", [P, TOP, T], u32)
        count = sb("moe_count", [P, 1])
        active = sb("moe_active", [P, 2])
        rank = sb("moe_rank", [P, 2])
        chosen = sb("moe_chosen", [P, 2, GROUPS])
        group_no = sb("moe_group_no", [P, 2])
        total = sb("moe_total", [1, 1])
        pairs = sb("moe_pairs", [1, GROUPS // 2])
        list_e = sb("moe_list_e", [1, GROUPS], u32)
        list_g = sb("moe_list_g", [1, GROUPS], u32)
        n_pairs_f = sb("moe_n_pairs_f", [1, 1])
        n_pairs = sb("moe_n_pairs", [1, 1], u32)
        tok_at = sb("moe_tok_at", [SLOTS, GROUPS + 1], u32)
        w_sgu = sb("moe_w_sgu", [DK, DC, 2, SI * IK])
        w_sd = sb("moe_w_sd", [IK, SI, D])
        s_act = sb("moe_s_act", [IK, 2, NT])
        s_hidT = sb("moe_s_hidT", [IK, SI, NT])
        acc = sb("moe_acc", [P, T, D])
        y_dram = s.y_of_slot
        u_dram = nc.dram_tensor("u_rows", [NT, D], fp32).ap()
        ps = s.ps

        weights_in = sem("moe_weights_in")
        shared_in = sem("moe_shared_in")
        var_ready, rstd_ready = sem("moe_var_ready"), sem("moe_rstd_ready")
        consts = sem("moe_consts")
        u_ready = sem("moe_u_ready")
        u_stored = sem("moe_u_stored")
        u_transposed = sem("moe_u_transposed")
        uT_ready = sem("moe_uT_ready")
        logits_ready = sem("moe_logits_ready")
        sig_ready = sem("moe_sig_ready")
        mask_ready = sem("moe_mask_ready")
        pos_product = sem("moe_pos_product")
        active_ready = sem("moe_active_ready")
        rank_product = sem("moe_rank_product")
        chosen_ready = sem("moe_chosen_ready")
        list_product = sem("moe_list_product")
        here_ready = sem("moe_here_ready")
        tok_product = sem("moe_tok_product")
        s_product = sem("moe_s_product")
        s_silu = sem("moe_s_silu")
        s_ready_g = sem("moe_s_ready_g")
        s_ready_v = sem("moe_s_ready_v")
        list_ready = sem("moe_list_ready")
        tok_at_ready = sem("moe_tok_at_ready")
        read_at_ready = sem("moe_read_at_ready")
        s_out = sem("moe_s_out")

        w_gu = [sb(f"moe_w_gu{k}", [DK, DC, 2 * NI]) for k in range(2)]
        w_d = [sb(f"moe_w_d{k}", [IK, IN_, D]) for k in range(2)]
        row_at = [sb(f"moe_row_at{k}", [SLOTS, 1], u32) for k in range(2)]
        rows = [sb(f"moe_rows{k}", [SLOTS, D]) for k in range(2)]
        rowsT = [sb(f"moe_rowsT{k}", [DK, DC, SLOTS]) for k in range(2)]
        act_g = [sb(f"moe_act_g{k}", [IK, IN_, SLOTS]) for k in range(2)]
        hidT = [sb(f"moe_hidT{k}", [IK, IN_, SLOTS]) for k in range(2)]
        y = [sb(f"moe_y{k}", [SLOTS, D]) for k in range(2)]
        gu_in = [sem(f"moe_gu_in{k}") for k in range(2)]
        d_in = [sem(f"moe_d_in{k}") for k in range(2)]
        row_at_set = [sem(f"moe_row_at_set{k}") for k in range(2)]
        rows_in = [sem(f"moe_rows_in{k}") for k in range(2)]
        rows_transposed = [sem(f"moe_rows_transposed{k}") for k in range(2)]
        rowsT_ready = [sem(f"moe_rowsT_ready{k}") for k in range(2)]
        gu_product = [sem(f"moe_gu_product{k}") for k in range(2)]
        silu_ready = [sem(f"moe_silu_ready{k}") for k in range(2)]
        hid_ready = [sem(f"moe_hid_ready{k}") for k in range(2)]
        y_product = [sem(f"moe_y_product{k}") for k in range(2)]
        y_ready = [sem(f"moe_y_ready{k}") for k in range(2)]
        y_stored = [sem(f"moe_y_stored{k}") for k in range(2)]
        all_stored = sem("moe_all_stored")
        row_at_seen = sem("moe_row_at_seen")
        back = sb("moe_back", [P, TOP, T, D])
        back_in = [sem(f"moe_back_in{k}") for k in range(TOP)]

        def s_used(eng, j):
            if j < S_POOL:
                eng.wait_ge(s_ready_g, j + 1)
            else:
                eng.wait_ge(s_ready_v, j + 1 - S_POOL)

        with nc.Block() as block:
            @block.sync
            def _(sp):
                sp.dma_start(w_router[:, :, :], a["moe_w_router"].rearrange("(c p) e -> p c e", p=DK)).then_inc(weights_in, 16)
                sp.dma_start(e_bias[:, :], a["moe_e_bias"].broadcast_to((P, NE))).then_inc(weights_in, 16)
                for k in range(2):
                    sp.dma_start(w_sgu[:, :, k, :], a["moe_w_sgu"][k].rearrange("(c p) e -> p c e", p=DK)).then_inc(shared_in, 16)
                sp.dma_start(w_sd[:, :, :], a["moe_w_sd"].rearrange("(c p) e -> p c e", p=IK)).then_inc(shared_in, 16)
                sp.wait_ge(u_ready, 1)
                sp.dma_start(u_dram.rearrange("(t p) d -> p t d", p=P), s.u[:, :, :]).then_inc(u_stored, 16)
                sp.wait_ge(list_ready, 1)
                with sp.Fori(0, sp.value_load(n_pairs[0:1, 0:1], min_val=1, max_val=GROUPS // 2)) as i:
                    for k in range(2):
                        e = sp.value_load(list_e[0:1, bass.ds(2 * i + k, 1)], min_val=0, max_val=NE - 1)
                        sp.wait_ge(gu_product[k], i + 1)
                        sp.dma_start(w_gu[k][:, :, :], a["moe_w_gu"][bass.ds(e, 1), :, :].rearrange("o (c p) f -> p (o c) f", p=DK)).then_inc(gu_in[k], 16)
                        sp.wait_ge(y_product[k], i + 1)
                        sp.dma_start(w_d[k][:, :, :], a["moe_w_d"][bass.ds(e, 1), :, :].rearrange("o (c p) f -> p (o c) f", p=IK)).then_inc(d_in[k], 16)

            @block.gpsimd
            def _(pool):
                pool.memset(before[:, :], 1.0).then_inc(consts, 1)
                pool.iota(iota_j[:, :], [[1, GROUPS]], base=0, channel_multiplier=0, allow_small_or_imprecise_dtypes=True).then_inc(consts, 1)
                pool.iota(iota_p[:, :], [[0, 1]], base=0, channel_multiplier=1, allow_small_or_imprecise_dtypes=True).then_inc(consts, 1)
                pool.iota(tok_id[:, :], [[P, T]], base=0, channel_multiplier=1, allow_small_or_imprecise_dtypes=True).then_inc(consts, 1)
                pool.iota(group_no[:, :], [[1, 2]], base=-SPARE, channel_multiplier=2, allow_small_or_imprecise_dtypes=True).then_inc(consts, 1)
                pool.wait_ge(consts, 5)
                pool.affine_select(out=before[:, :], in_=before[:, :], compare_op=ALU.is_gt, fill=0.0, base=0,
                                   pattern=[[1, P]], channel_multiplier=-1).then_inc(consts, 1)
                ln_pool(pool, s, 0, var_ready, rstd_ready)
                for j in range(S_POOL):
                    pool.wait_ge(s_silu, j + 1)
                    pool.tensor_tensor(s_hidT[:, j, :], s_act[:, j % 2, :], s_hidT[:, j, :], ALU.mult).then_inc(s_ready_g, 1)
                    pool.wait_ge(s_ready_g, j + 1)
                pool.wait_ge(u_stored, 16)
                pool.wait_ge(list_ready, 1)
                pool.wait_ge(tok_at_ready, 1)
                with pool.Fori(0, pool.value_load(n_pairs[0:1, 0:1], min_val=1, max_val=GROUPS // 2)) as i:
                    for k in range(2):
                        g = pool.value_load(list_g[0:1, bass.ds(2 * i + k, 1)], min_val=0, max_val=GROUPS)
                        pool.wait_ge(rows_transposed[k], i + 1)
                        pool.tensor_copy(row_at[k][:, :], tok_at[:, bass.ds(g, 1)]).then_inc(row_at_set[k], 1)
                        pool.wait_ge(row_at_set[k], i + 1)
                        pool.sem_inc(row_at_seen, 1)
                        pool.indirect_dma_start(out=rows[k][:, :], out_offset=None, in_=u_dram,
                                                in_offset=bass.IndirectOffsetOnAxis(ap=row_at[k][:, 0:1], axis=0),
                                                bounds_check=NT - 1, oob_is_err=False).then_inc(rows_in[k], 16)
                pool.wait_ge(read_at_ready, 1)
                pool.wait_ge(all_stored, 2)
                for k in range(TOP):
                    for t in range(T):
                        pool.indirect_dma_start(out=back[:, k, t, :], out_offset=None, in_=y_dram,
                                                in_offset=bass.IndirectOffsetOnAxis(ap=read_at[:, k, t:t + 1], axis=0),
                                                bounds_check=GROUPS * SLOTS - 1, oob_is_err=False).then_inc(back_in[k], 16)

            @block.tensor
            def _(pe):
                for k in range(2):
                    pe.sem_inc(gu_product[k], 1)
                    pe.sem_inc(y_product[k], 1)
                    pe.sem_inc(rows_transposed[k], 1)
                pe.wait_ge(u_ready, 1)
                transpose_u(pe, s).then_inc(u_transposed, 1)
                pe.wait_ge(uT_ready, 1)
                pe.wait_ge(weights_in, 32)
                for t in range(T):
                    for c in range(DC):
                        last = pe.matmul(ps[:, 2, t * NE:(t + 1) * NE], lhsT=s.uT[:, c, t * P:(t + 1) * P],
                                         rhs=w_router[:, c, :], start=(c == 0), stop=(c == DC - 1))
                last.then_inc(logits_ready, 1)

                def shared_up(j):
                    if j == 1:
                        pe.wait_ge(sig_ready, 1)
                    if j >= 2:
                        pe.wait_ge(s_silu, j - 1)
                    for k in range(2):
                        for c in range(DC):
                            last = pe.matmul(ps[0:IK, S_BANKS[j % 2][k], :], lhsT=w_sgu[:, c, k, j * IK:(j + 1) * IK],
                                             rhs=s.uT[:, c, :], start=(c == 0), stop=(c == DC - 1))
                    last.then_inc(s_product, 1)

                pe.wait_ge(shared_in, 48)
                for j in range(3):
                    shared_up(j)
                pe.wait_ge(mask_ready, 1)
                pe.wait_ge(consts, 6)
                for t in range(T):
                    for j in range(t + 1):
                        pe.matmul(ps[:, 3, t * NE:(t + 1) * NE], lhsT=(before if j == t else s.ones)[:, :],
                                  rhs=mask[:, j, :], start=(j == 0), stop=(j == t))
                for t in range(T):
                    last = pe.matmul(ps[:, 4, 0:1], lhsT=mask[:, t, :], rhs=s.ones[:, 0:1], start=(t == 0), stop=(t == T - 1))
                last.then_inc(pos_product, 1)
                for j in range(3, 5):
                    shared_up(j)
                pe.wait_ge(active_ready, 1)
                pe.matmul(ps[:, 5, 0:1], lhsT=before[:, :], rhs=active[:, 0:1], start=True, stop=True)
                pe.matmul(ps[:, 5, 1:2], lhsT=s.ones[:, :], rhs=active[:, 0:1], start=True, stop=False)
                pe.matmul(ps[:, 5, 1:2], lhsT=before[:, :], rhs=active[:, 1:2], start=False, stop=True)
                for k in range(2):
                    last = pe.matmul(ps[0:1, 5, 2:3], lhsT=s.ones[:, 0:1], rhs=active[:, k:k + 1], start=(k == 0), stop=(k == 1))
                last.then_inc(rank_product, 1)
                pe.wait_ge(chosen_ready, 1)
                for at, col in ((0, [iota_p[:, 0:1]] * 2), (GROUPS, [group_no[:, 0:1], group_no[:, 1:2]])):
                    for k in range(2):
                        last = pe.matmul(ps[0:1, 6, at:at + GROUPS], lhsT=col[k], rhs=chosen[:, k, :], start=(k == 0), stop=(k == 1))
                last.then_inc(list_product, 1)
                for k in range(TOP):
                    pe.wait_ge(here_ready, k + 1)
                    for t in range(T):
                        for half in range(2):
                            last = pe.matmul(ps[0:SLOTS, 3 + half, 0:NE], lhsT=tok_here[:, k, t, half * SLOTS:(half + 1) * SLOTS],
                                             rhs=onehot[:, k, t, :], start=(k == 0 and t == 0), stop=(k == TOP - 1 and t == T - 1))
                last.then_inc(tok_product, 1)
                pe.wait_ge(tok_at_ready, 1)
                with pe.Fori(0, pe.value_load(n_pairs[0:1, 0:1], min_val=1, max_val=GROUPS // 2)) as i:
                    for k in range(2):
                        pe.wait_ge(rows_in[k], i * 16 + 16)
                        for c in range(DC):
                            last = pe.transpose(ps[0:DK, 7 * k, c * SLOTS:(c + 1) * SLOTS], rows[k][:, c * DK:(c + 1) * DK],
                                                s.ident[0:SLOTS, 0:SLOTS])
                        last.then_inc(rows_transposed[k], 1)
                    for k in range(2):
                        pe.wait_ge(rowsT_ready[k], i + 1)
                        pe.wait_ge(gu_in[k], i * 16 + 16)
                        for half in range(2):
                            for m in range(IN_):
                                at = half * NI + m * IK
                                for c in range(DC):
                                    last = pe.matmul(ps[0:IK, 1 + 2 * k + half, m * SLOTS:(m + 1) * SLOTS],
                                                     lhsT=w_gu[k][:, c, at:at + IK], rhs=rowsT[k][:, c, :],
                                                     start=(c == 0), stop=(c == DC - 1))
                        last.then_inc(gu_product[k], 1)
                    for k in range(2):
                        pe.wait_ge(hid_ready[k], i + 2)
                        pe.wait_ge(d_in[k], i * 16 + 16)
                        pe.wait_ge(y_ready[k], i + 1)
                        for m in range(IN_):
                            last = pe.matmul(ps[0:SLOTS, 5 + k, 0:D], lhsT=hidT[k][:, m, :], rhs=w_d[k][:, m, :],
                                             start=(m == 0), stop=(m == IN_ - 1))
                        last.then_inc(y_product[k], 1)
                for j in range(S_POOL, SI):
                    shared_up(j)
                s_used(pe, SI - 1)
                for t in range(T):
                    for j in range(SI):
                        last = pe.matmul(ps[:, t, 0:D], lhsT=s_hidT[:, j, t * P:(t + 1) * P], rhs=w_sd[:, j, :],
                                         start=(j == 0), stop=(j == SI - 1))
                last.then_inc(s_out, 1)

            @block.scalar
            def _(act):
                act.wait_ge(logits_ready, 1)
                act.activation(sig[:, :, :], ps[:, 2, :].rearrange("p (t e) -> p t e", t=T), ACT.Sigmoid).then_inc(sig_ready, 1)

                def s_silu_of(j):
                    act.wait_ge(s_product, j + 1)
                    if j >= 2:
                        s_used(act, j - 2)
                    act.activation(s_act[:, j % 2, :], ps[0:IK, S_BANKS[j % 2][0], :], ACT.Silu)
                    act.copy(s_hidT[:, j, :], ps[0:IK, S_BANKS[j % 2][1], :]).then_inc(s_silu, 1)

                for j in range(S_POOL):
                    s_silu_of(j)
                act.wait_ge(list_ready, 1)
                for k in range(2):
                    act.sem_inc(y_ready[k], 1)
                    act.sem_inc(y_stored[k], 16)
                n = act.value_load(n_pairs[0:1, 0:1], min_val=1, max_val=GROUPS // 2)
                with act.Fori(0, n) as i:
                    for k in range(2):
                        act.wait_ge(gu_product[k], i + 2)
                        act.wait_ge(hid_ready[k], i + 1)
                        act.activation(act_g[k][:, :, :], ps[0:IK, 1 + 2 * k, 0:IN_ * SLOTS].rearrange("p (m n) -> p m n", m=IN_),
                                       ACT.Silu).then_inc(silu_ready[k], 1)
                    for k in range(2):
                        g = act.value_load(list_g[0:1, bass.ds(2 * i + k, 1)], min_val=0, max_val=GROUPS)
                        act.wait_ge(y_stored[k], i * 16 + 16)
                        act.wait_ge(y_product[k], i + 2)
                        act.copy(y[k][:, :], ps[0:SLOTS, 5 + k, 0:D]).then_inc(y_ready[k], 1)
                        act.wait_ge(y_ready[k], i + 2)
                        act.dma_start(y_dram.rearrange("(g c) d -> g c d", c=SLOTS)[bass.ds(g, 1), :, :].rearrange("o c d -> (o c) d"),
                                      y[k][:, :]).then_inc(y_stored[k], 16)
                for k in range(2):
                    act.wait_ge(y_stored[k], n * 16 + 16)
                    act.sem_inc(all_stored, 1)
                for j in range(S_POOL, SI):
                    s_silu_of(j)

            @block.vector
            def _(dve):
                ln_vector(dve, s, s.u, s.h, 0, var_ready, rstd_ready).then_inc(u_ready, 1)
                dve.wait_ge(u_transposed, 1)
                dve.tensor_copy(s.uT[:, :, :], ps[0:DK, 0:DC, :]).then_inc(uT_ready, 1)
                dve.wait_ge(weights_in, 32)
                dve.wait_ge(sig_ready, 1)
                dve.tensor_tensor(choice[:, :, :], sig[:, :, :], e_bias[:, :].unsqueeze(1).broadcast_to((P, T, NE)), ALU.add)
                dve.drain()
                for t in range(T):
                    dve.max(top8[:, t, :], choice[:, t, :])
                dve.drain()
                for t in range(T):
                    dve.max_index(top8_at[:, t, :], top8[:, t, :], choice[:, t, :])
                dve.drain()
                dve.tensor_copy(expert[:, :, :], top8_at[:, :, 0:TOP].rearrange("p t k -> p k t"))
                dve.drain()
                dve.wait_ge(consts, 6)
                for k in range(TOP):
                    dve.tensor_tensor(onehot[:, k, :, :], iota_j[:, 0:NE].unsqueeze(1).broadcast_to((P, T, NE)),
                                      expert[:, k, :].unsqueeze(2).broadcast_to((P, T, NE)), ALU.is_equal)
                dve.drain()
                dve.reduce_sum(mask[:, :, :], onehot[:, :, :, :].rearrange("p k t e -> p t e k"), AX.X).then_inc(mask_ready, 1)
                dve.wait_ge(pos_product, 1)
                dve.tensor_copy(pos[:, :, :], ps[:, 3, :].rearrange("p (t e) -> p t e", t=T))
                dve.tensor_copy(count[:, :], ps[:, 4, 0:1])
                dve.drain()
                dve.tensor_scalar(active[:, 0:1], count[:, :], 0.0, None, ALU.is_gt)
                dve.tensor_scalar(active[:, 1:2], count[:, :], float(SLOTS), None, ALU.is_gt).then_inc(active_ready, 1)
                for k in range(TOP):
                    dve.tensor_tensor(picked[:, k, :, :], onehot[:, k, :, :], pos[:, :, :], ALU.mult)
                dve.drain()
                dve.reduce_sum(pos_k[:, :, :], picked[:, :, :, :], AX.X)
                dve.wait_ge(rank_product, 1)
                dve.tensor_copy(rank[:, :], ps[:, 5, 0:2])
                dve.tensor_copy(total[:, :], ps[0:1, 5, 2:3])
                dve.drain()
                for k in range(2):
                    last = dve.tensor_scalar(chosen[:, k, :], iota_j[:, :], rank[:, k:k + 1], active[:, k:k + 1], ALU.is_equal, ALU.mult)
                last.then_inc(chosen_ready, 1)
                for k in range(TOP):
                    for t in range(T):
                        last = dve.tensor_scalar(tok_here[:, k, t, :], iota_j[:, 0:CAP], pos_k[:, k, t:t + 1], tok_id[:, t:t + 1],
                                                 ALU.is_equal, ALU.mult)
                    last.then_inc(here_ready, 1)
                dve.tensor_scalar(pairs[:, :], iota_j[0:1, ::2], total[:, :], None, ALU.is_lt)
                dve.drain()
                dve.reduce_sum(n_pairs_f[:, :], pairs[:, :], AX.X)
                dve.drain()
                dve.tensor_copy(n_pairs[:, :], n_pairs_f[:, :])
                dve.wait_ge(list_product, 1)
                dve.tensor_copy(list_e[:, :], ps[0:1, 6, 0:GROUPS])
                dve.tensor_scalar(list_g[:, :], ps[0:1, 6, GROUPS:2 * GROUPS], float(SPARE), None, ALU.add)
                dve.drain()
                dve.sem_inc(list_ready, 1)
                dve.memset(tok_at[:, SPARE:SPARE + 1], 0)
                dve.wait_ge(tok_product, 1)
                for half in range(2):
                    dve.tensor_copy(tok_at[:, half:GROUPS:2], ps[0:SLOTS, 3 + half, 0:NE])
                dve.drain()
                dve.sem_inc(tok_at_ready, 1)
                for k in range(TOP):
                    dve.tensor_tensor(picked[:, k, :, :], onehot[:, k, :, :], sig[:, :, :], ALU.mult)
                dve.drain()
                dve.reduce_sum(sig_k[:, :, :], picked[:, :, :, :], AX.X)
                dve.drain()
                dve.reduce_sum(den[:, :], sig_k[:, :, :].rearrange("p k t -> p t k"), AX.X)
                dve.drain()
                dve.tensor_scalar(den[:, :], den[:, :], 1e-20, None, ALU.add)
                dve.tensor_scalar(valid[:, :, :], pos_k[:, :, :], float(CAP), None, ALU.is_lt)
                dve.tensor_scalar(slot_f[:, :, :], expert[:, :, :], float(CAP), None, ALU.mult)
                dve.drain()
                dve.reciprocal(den[:, :], den[:, :])
                dve.tensor_tensor(pos_v[:, :, :], pos_k[:, :, :], valid[:, :, :], ALU.mult)
                dve.drain()
                dve.tensor_tensor(weight[:, :, :], sig_k[:, :, :], den[:, :].unsqueeze(1).broadcast_to((P, TOP, T)), ALU.mult)
                dve.tensor_tensor(read_at[:, :, :], pos_v[:, :, :], slot_f[:, :, :], ALU.add).then_inc(read_at_ready, 1)
                dve.drain()
                dve.scalar_tensor_tensor(out=weight[:, :, :], in0=weight[:, :, :], scalar=ROUTED_SCALE, in1=valid[:, :, :],
                                         op0=ALU.mult, op1=ALU.mult)
                for k in range(2):
                    dve.sem_inc(hid_ready[k], 1)
                with dve.Fori(0, dve.value_load(n_pairs[0:1, 0:1], min_val=1, max_val=GROUPS // 2)) as i:
                    for k in range(2):
                        dve.wait_ge(rows_transposed[k], i + 2)
                        dve.tensor_copy(rowsT[k][:, :, :], ps[0:DK, 7 * k, 0:DC * SLOTS].rearrange("p (c n) -> p c n", c=DC)).then_inc(rowsT_ready[k], 1)
                    for k in range(2):
                        dve.wait_ge(silu_ready[k], i + 1)
                        dve.tensor_tensor(hidT[k][:, :, :], act_g[k][:, :, :],
                                          ps[0:IK, 2 + 2 * k, 0:IN_ * SLOTS].rearrange("p (m n) -> p m n", m=IN_), ALU.mult).then_inc(hid_ready[k], 1)
                for j in range(S_POOL, SI):
                    dve.wait_ge(s_silu, j + 1)
                    dve.tensor_tensor(s_hidT[:, j, :], s_act[:, j % 2, :], s_hidT[:, j, :], ALU.mult).then_inc(s_ready_v, 1)
                dve.wait_ge(s_out, 1)
                dve.tensor_tensor(acc[:, :, :], ps[:, 0:T, 0:D], s.h[:, :, :], ALU.add)
                dve.drain()
                for k in range(TOP):
                    dve.wait_ge(back_in[k], T * 16)
                    for t in range(T):
                        dve.scalar_tensor_tensor(out=acc[:, t, :], in0=back[:, k, t, :], scalar=weight[:, k, t:t + 1],
                                                 in1=acc[:, t, :], op0=ALU.mult, op1=ALU.add)
                    dve.drain()
                dve.tensor_copy(s.h[:, :, :], acc[:, :, :])


EH, EY = 12, 64
EC = EH * EY // P
EM = 768
DJ = 3
EMC = EM // P
STEPS = 12
ALPHA = 0.1
BETA = 0.125
PAIRS = EC * BATCH
SLOTS_W = PAIRS + 2
OUT_Q, OUT_K = 6, 7
Y_BANKS = (6, 7, 2)
ITEMS_OF = {-1: [("q", 0), ("k", 0), ("q", 1), ("k", 1), ("q_tok", 0), ("mem", 0)]}
for _s in range(SLOTS_W):
    _c = _s // 2
    ITEMS_OF[_s] = [("q_tok", _c + 1), ("k", _c + 2)] if _s % 2 else [("k_tok", _c), ("q", _c + 2)]
    ITEMS_OF[_s] = [_i for _i in ITEMS_OF[_s] if _i[1] < EC]
for _c, _s in ((1, 8), (2, 9), (3, 11), (4, PAIRS), (5, PAIRS)):
    ITEMS_OF[_s].append(("mem", _c))
ITEMS = [_i for _s in range(-1, SLOTS_W) for _i in ITEMS_OF[_s]]
NITEMS = len(ITEMS)


def energy_stage(nc, s, a):
    ctx = ExitStack()
    with ctx:
        def sb(name, shape, dt=fp32):
            return ctx.enter_context(nc.sbuf_tensor(name, shape, dt))

        def sem(name):
            return s.stage_semaphore(name)

        w_s = sb("en_w_s", [P, DJ, 3, EM], f32r)
        g_hi = sb("en_g_hi", [P, DJ, NT], f32r)
        g_lo = sb("en_g_lo", [P, 2, NT], f32r)
        g = sb("en_g", [P, 2, NT])
        wr = sb("en_wr", [P, 3, EMC, D])
        ln = sb("en_ln", [P, DJ, 2])
        x = s.u
        y = sb("en_y", [P, T, 2, D])
        q_c = sb("en_q", [P, 2, NT])
        k_c = sb("en_k", [P, 2, NT])
        q_s = sb("en_q_s", [P, 2, 2, NT], f32r)
        k_hi = sb("en_k_hi", [P, 2, 2, NT], f32r)
        k_lo = sb("en_k_lo", [P, 2, 2, NT], f32r)
        qn = sb("en_qn", [P, 3, T, P])
        kn = sb("en_kn", [P, 3, T, P])
        big = sb("en_big", [P, 3 * EC * NT])
        dqT, dkT, memT = (big[:, i * EC * NT:(i + 1) * EC * NT].rearrange("p (c n) -> p c n", c=EC) for i in range(3))
        wT = big[:, 0:DJ * 3 * EM].rearrange("p (j k e) -> p j k e", j=DJ, k=3)
        neg_max = sb("en_neg_max", [P, 6, TB])
        row_sum = sb("en_row_sum", [P, 6, TB])
        prob = [sb(f"en_prob{i}", [P, TB, SEQ]) for i in range(6)]
        probT = [sb(f"en_probT{i}", [P, TB, SEQ]) for i in range(4)]
        ps = s.ps
        HI = (slice(0, EY), slice(EY, P))
        LO = (slice(EY, P), slice(0, EY))

        weights_in = sem("en_weights_in")
        wr_in = sem("en_wr_in")
        k_lo_zeroed = sem("en_k_lo_zeroed")
        w_split = sem("en_w_split")
        var_ready, rstd_ready = sem("en_var_ready"), sem("en_rstd_ready")
        y_ready = sem("en_y_ready")
        y_transposed = sem("en_y_transposed")
        g_ready = sem("en_g_ready")
        g_hi_ready = sem("en_g_hi_ready")
        g_lo_ready = sem("en_g_lo_ready")
        item = sem("en_item")
        item_out = sem("en_item_out")
        q_hi_ready, k_hi_ready = sem("en_q_hi_ready"), sem("en_k_hi_ready")
        q_split, k_split = sem("en_q_split"), sem("en_k_split")
        scores = sem("en_scores")
        max_ready = sem("en_max_ready")
        exp_ready = sem("en_exp_ready")
        prob_ready = sem("en_prob_ready")
        transposed = sem("en_transposed")
        probT_ready = sem("en_probT_ready")
        pair_done = sem("en_pair_done")
        dq_ready, dk_ready = sem("en_dq_ready"), sem("en_dk_ready")
        grad_product = sem("en_grad_product")

        with nc.Block() as block:
            @block.sync
            def _(sp):
                for j, (lo, hi) in enumerate(((0, P), (EY, D))):
                    sp.dma_start(wT[:, 2 * j, :, :], a["en_wT"].rearrange("k p e -> p k e")[lo:hi, :, :]).then_inc(weights_in, 16)
                    sp.dma_start(ln[:, 2 * j, :], a["en_ln"][lo:hi, :]).then_inc(weights_in, 16)
                for at, (lo, hi) in ((slice(0, EY), (P, D)), (slice(EY, P), (0, EY))):
                    sp.dma_start(wT[at, 1, :, :], a["en_wT"].rearrange("k p e -> p k e")[lo:hi, :, :]).then_inc(weights_in, 16)
                    sp.dma_start(ln[at, 1, :], a["en_ln"][lo:hi, :]).then_inc(weights_in, 16)
                for k in range(3):
                    sp.dma_start(wr[:, k, :, :], a["en_w"][k].rearrange("(c p) d -> p c d", p=P)).then_inc(wr_in, 16)

            @block.gpsimd
            def _(pool):
                for r in range(2):
                    pool.memset(k_lo[LO[r], :, r, :].bitcast(fp32), 0.0).then_inc(k_lo_zeroed, 1)
                    pool.wait_ge(k_lo_zeroed, r + 1)

                def rstd(n):
                    for t in range(T):
                        pool.wait_ge(var_ready, n * T + t + 1)
                        pool.tensor_tensor(s.rstd[:, t:t + 1], s.var[:, t:t + 1], s.neghalf[:, 0:1], ALU.pow).then_inc(rstd_ready, 1)
                        pool.wait_ge(rstd_ready, n * T + t + 1)

                rstd(0)
                rstd(1)
                with pool.Fori(0, STEPS) as n:
                    for c in range(1, EC):
                        pool.wait_ge(q_hi_ready, n * EC + c + 1)
                        for r in range(2):
                            pool.tensor_tensor(q_s[LO[r], c % 2, r, :], q_c[HI[r], c % 2, :],
                                               q_s[HI[r], c % 2, r, :].bitcast(fp32), ALU.subtract).then_inc(q_split, 1)
                            pool.wait_ge(q_split, 2 * EC * n + 2 * c + r + 1)
                        pool.wait_ge(k_hi_ready, n * EC + c + 1)
                        for r in range(2):
                            pool.tensor_tensor(k_lo[HI[r], c % 2, r, :], k_c[HI[r], c % 2, :],
                                               k_hi[HI[r], c % 2, r, :].bitcast(fp32), ALU.subtract).then_inc(k_split, 1)
                            pool.wait_ge(k_split, 2 * EC * n + 2 * c + r + 1)
                    rstd(n + 2)

            @block.tensor
            def _(pe):
                pe.wait_ge(w_split, 1)
                pe.wait_ge(k_lo_zeroed, 2)
                pe.wait_ge(wr_in, 3 * 16)
                with pe.Fori(0, STEPS) as n:
                    for t in range(T):
                        pe.wait_ge(y_ready, n * T + t + 1)
                        for j in range(DJ):
                            last = pe.transpose(ps[:, Y_BANKS[j], t * P:(t + 1) * P],
                                                y[:, t, :, :].rearrange("p k d -> p (k d)")[:, j * P:(j + 1) * P], s.ident[:, :])
                    last.then_inc(y_transposed, 1)

                    def product(p, terms):
                        kind, c = ITEMS[p]
                        for j, part in terms:
                            if p == 0 and part is g_hi:
                                pe.wait_ge(g_hi_ready, n * DJ + j + 1)
                            if p == 0 and part is g_lo and j == 1:
                                pe.wait_ge(g_lo_ready, n * 2 + 1)
                            if p == 0 and part is g_lo and j == 0:
                                pe.wait_ge(g_lo_ready, n * 2 + 2)
                            last = pe.matmul(ps[:, p % 2, :], lhsT=w_s[:, j, ("q", "k", "mem").index(kind), c * P:(c + 1) * P],
                                             rhs=part[:, j, :], start=(part is g_hi and j == 0), stop=(part is g_lo and j == 0))
                        return last

                    hi_terms = tuple((j, g_hi) for j in range(DJ))
                    lo_terms = ((1, g_lo), (0, g_lo))

                    def make(p):
                        kind, c = ITEMS[p]
                        if p >= 2:
                            pe.wait_ge(item_out, n * NITEMS + p - 1)
                        bank = ps[:, p % 2, :]
                        if kind in ("q_tok", "k_tok"):
                            of = ITEMS.index((kind[0], c))
                            if of > p - 2:
                                pe.wait_ge(item_out, n * NITEMS + of + 1)
                            src = (q_c if kind == "q_tok" else k_c)[:, c % 2, :]
                            for t in range(T):
                                last = pe.transpose(bank[:, t * P:(t + 1) * P], src[:, t * P:(t + 1) * P], s.ident[:, :])
                        else:
                            last = product(p, hi_terms + lo_terms)
                        last.then_inc(item, 1)

                    def score(w, r):
                        c, b = w // BATCH, w % BATCH
                        if b == 0 and r == 0:
                            pe.wait_ge(q_split, 2 * EC * n + 2 * c + 2)
                            pe.wait_ge(k_split, 2 * EC * n + 2 * c + 2)
                        if w > 0:
                            pe.wait_ge(exp_ready, n * 2 * PAIRS + 2 * w + r - 1)
                        for i in range(TB):
                            lo = b * SEQ + i * P
                            for part in (k_hi, k_lo):
                                last = pe.matmul(ps[:, 2 + r, i * SEQ:(i + 1) * SEQ], lhsT=q_s[:, c % 2, r, lo:lo + P],
                                                 rhs=part[:, c % 2, r, b * SEQ:(b + 1) * SEQ], start=(part is k_hi), stop=(part is k_lo))
                        last.then_inc(scores, 1)

                    def transpose(w, r):
                        if w > 0:
                            pe.wait_ge(probT_ready, n * 2 * PAIRS + 2 * w + r - 1)
                        pe.wait_ge(prob_ready, n * 2 * PAIRS + 2 * w + r + 1)
                        for i in range(TB):
                            for j in range(TB):
                                last = pe.transpose(ps[:, 4 + r, j * SEQ + i * P:j * SEQ + (i + 1) * P],
                                                    prob[(2 * w + r) % 6][:, i, j * P:(j + 1) * P], s.ident[:, :])
                        last.then_inc(transposed, 1)

                    def combine(w):
                        c, b = w // BATCH, w % BATCH
                        if b == 0:
                            pe.wait_ge(item_out, n * NITEMS + ITEMS.index(("k_tok", c)) + 1)
                            if c >= 1:
                                pe.wait_ge(dq_ready, n * EC + c)
                                pe.wait_ge(dk_ready, n * EC + c)
                        seq = slice(b * SEQ, (b + 1) * SEQ)
                        for i in range(TB):
                            for r in range(2):
                                pe.matmul(ps[HI[r], OUT_K, seq], lhsT=qn[:, c % 3, b * TB + i, HI[r]],
                                          rhs=prob[(2 * w + r) % 6][:, i, :], start=(i == 0), stop=(i == TB - 1))
                        pe.wait_ge(probT_ready, n * 2 * PAIRS + 2 * w + 2)
                        for j in range(TB):
                            for r in range(2):
                                last = pe.matmul(ps[HI[r], OUT_Q, seq], lhsT=kn[:, c % 3, b * TB + j, HI[r]],
                                                 rhs=probT[(2 * w + r) % 4][:, j, :], start=(j == 0), stop=(j == TB - 1))
                        last.then_inc(pair_done, 1)

                    def back(t, lot, src, c, start=False, stop=False):
                        return pe.matmul(ps[:, 2 + t, 0:D], lhsT=src[:, c, t * P:(t + 1) * P], rhs=wr[:, lot, c, :],
                                         start=start, stop=stop)

                    def back_mem(t):
                        if t == 0:
                            pe.wait_ge(item_out, n * NITEMS + NITEMS)
                        if t < 2:
                            pe.wait_ge(exp_ready, n * 2 * PAIRS + 2 * PAIRS - 1 + t)
                        else:
                            pe.wait_ge(probT_ready, n * 2 * PAIRS + 2 * PAIRS - 3 + t)
                        for c in range(EMC):
                            back(t, 2, memT, c, start=(c == 0))

                    for terms in (hi_terms, lo_terms):
                        for p in range(2):
                            last = product(p, terms)
                            if terms is lo_terms:
                                last.then_inc(item, 1)
                    p = 2
                    for _ in ITEMS_OF[-1][2:]:
                        make(p)
                        p += 1
                    for slot in range(SLOTS_W):
                        if slot < PAIRS:
                            score(slot, 0)
                            score(slot, 1)
                        for _ in ITEMS_OF[slot][:1]:
                            make(p)
                            p += 1
                        if 1 <= slot <= PAIRS:
                            transpose(slot - 1, 0)
                            transpose(slot - 1, 1)
                        for _ in ITEMS_OF[slot][1:]:
                            make(p)
                            p += 1
                        if slot == PAIRS + 1:
                            back_mem(0)
                        if slot >= 2:
                            combine(slot - 2)
                    for t in range(1, T):
                        back_mem(t)
                    for t in range(T):
                        for c in range(EC):
                            pe.wait_ge(dq_ready, n * EC + c + 1)
                            back(t, 0, dqT, c)
                            pe.wait_ge(dk_ready, n * EC + c + 1)
                            last = back(t, 1, dkT, c, stop=(c == EC - 1))
                        last.then_inc(grad_product, 1)

            @block.scalar
            def _(act):
                act.wait_ge(weights_in, 8 * 16)
                with act.Fori(0, STEPS) as n:
                    act.wait_ge(y_transposed, n + 1)
                    for j in range(DJ):
                        if j == 1:
                            act.wait_ge(g_ready, n + 1)
                        act.activation(g_hi[:, j, :], ps[:, Y_BANKS[j], :], ACT.Identity, bias=ln[:, j, 1:2], scale=ln[:, j, 0:1]).then_inc(g_hi_ready, 1)

                    def take(p):
                        kind, c = ITEMS[p]
                        act.wait_ge(item, n * NITEMS + p + 1)
                        bank = ps[:, p % 2, :]
                        if kind in ("q", "k"):
                            if c >= 2:
                                act.wait_ge(q_split if kind == "q" else k_split, 2 * EC * n + 2 * c - 2)
                            last = act.copy((q_c if kind == "q" else k_c)[:, c % 2, :], bank)
                        elif kind == "mem":
                            last = act.activation(memT[:, c, :], bank, ACT.Relu)
                        else:
                            if c >= 3:
                                act.wait_ge(pair_done, n * PAIRS + BATCH * (c - 2))
                            last = act.copy((qn if kind == "q_tok" else kn)[:, c % 3, :, :], bank.rearrange("p (t n) -> p t n", t=T))
                        last.then_inc(item_out, 1)

                    def exponentiate(w, r):
                        u = (2 * w + r) % 6
                        act.wait_ge(max_ready, n * 2 * PAIRS + 2 * w + r + 1)
                        if w >= 3:
                            act.wait_ge(pair_done, n * PAIRS + w - 2)
                        for i in range(TB):
                            last = act.activation(prob[u][:, i, :], ps[:, 2 + r, i * SEQ:(i + 1) * SEQ], ACT.Exp,
                                                  bias=neg_max[:, u, i:i + 1], accum_out=row_sum[:, u, i:i + 1])
                        last.then_inc(exp_ready, 1)

                    p = 0
                    for _ in ITEMS_OF[-1]:
                        take(p)
                        p += 1
                    for slot in range(SLOTS_W):
                        if slot >= 4 and slot % 2 == 0:
                            c = slot // 2 - 2
                            act.wait_ge(pair_done, n * PAIRS + 2 * c + 2)
                            act.mul(dqT[:, c, :], ps[:, OUT_Q, :], 1.0 / BETA).then_inc(dq_ready, 1)
                        if slot < PAIRS:
                            exponentiate(slot, 0)
                            exponentiate(slot, 1)
                        for _ in ITEMS_OF[slot][:1]:
                            take(p)
                            p += 1
                        if 1 <= slot <= PAIRS:
                            w = slot - 1
                            for r in range(2):
                                act.wait_ge(transposed, n * 2 * PAIRS + 2 * w + r + 1)
                                if w >= 2:
                                    act.wait_ge(pair_done, n * PAIRS + w - 1)
                                act.copy(probT[(2 * w + r) % 4][:, :, :], ps[:, 4 + r, :].rearrange("p (j n) -> p j n", j=TB)).then_inc(probT_ready, 1)
                        for _ in ITEMS_OF[slot][1:]:
                            take(p)
                            p += 1
                    act.wait_ge(pair_done, n * PAIRS + PAIRS)
                    act.mul(dqT[:, EC - 1, :], ps[:, OUT_Q, :], 1.0 / BETA).then_inc(dq_ready, 1)

            @block.vector
            def _(dve):
                def normalised(y, x, t, n):
                    dve.bn_stats(s.stats[:, t, :], x)
                    dve.drain()
                    dve.bn_aggr(s.mv[:, t, :], s.stats[:, t, :])
                    dve.drain()
                    dve.tensor_scalar(s.var[:, t:t + 1], s.mv[:, t, 1:2], EPS, None, ALU.add).then_inc(var_ready, 1)
                    dve.wait_ge(rstd_ready, n * T + t + 1)
                    if len(y.shape) == 3:
                        x = x.unsqueeze(1).broadcast_to((P, 2, D))
                    return dve.tensor_scalar(y, x, s.mv[:, t, 0:1], s.rstd[:, t:t + 1], ALU.subtract, ALU.mult)

                for t in range(T):
                    normalised(x[:, t, :], s.h[:, t, :], t, 0)
                dve.drain()
                for t in range(T):
                    normalised(y[:, t, :, :], x[:, t, :], t, 1).then_inc(y_ready, 1)
                dve.wait_ge(weights_in, 8 * 16)
                dve.tensor_scalar(wT[:, :, 1, :], wT[:, :, 1, :], BETA, None, ALU.mult)
                dve.drain()
                dve.tensor_copy(w_s[:, :, :, :], wT)
                dve.drain()
                dve.tensor_tensor(w_s[EY:P, 1, :, :], wT[EY:P, 1, :, :], w_s[EY:P, 1, :, :].bitcast(fp32), ALU.subtract)
                dve.tensor_tensor(w_s[:, 2, :, :], wT[:, 2, :, :], w_s[:, 2, :, :].bitcast(fp32), ALU.subtract).then_inc(w_split, 1)
                with dve.Fori(0, STEPS) as n:
                    dve.wait_ge(y_transposed, n + 1)
                    for j in (1, 0):
                        if j == 0:
                            dve.wait_ge(g_hi_ready, n * DJ + 1)
                        last = dve.tensor_scalar(g[:, j, :], ps[:, Y_BANKS[j], :], ln[:, j, 0:1], ln[:, j, 1:2], ALU.mult, ALU.add)
                        if j == 1:
                            last.then_inc(g_ready, 1)
                    dve.wait_ge(g_hi_ready, n * DJ + 2)
                    for j in (1, 0):
                        if j == 0:
                            dve.drain()
                        dve.tensor_tensor(g_lo[:, j, :], g[:, j, :], g_hi[:, j, :].bitcast(fp32), ALU.subtract).then_inc(g_lo_ready, 1)

                    def split_q(c):
                        dve.wait_ge(item_out, n * NITEMS + ITEMS.index(("q", c)) + 1)
                        for r in range(2):
                            last = dve.tensor_copy(q_s[HI[r], c % 2, r, :], q_c[HI[r], c % 2, :])
                        last.then_inc(q_hi_ready, 1)
                        if c == 0:
                            dve.drain()
                            for r in range(2):
                                dve.tensor_tensor(q_s[LO[r], 0, r, :], q_c[HI[r], 0, :],
                                                  q_s[HI[r], 0, r, :].bitcast(fp32), ALU.subtract).then_inc(q_split, 1)

                    def split_k(c):
                        dve.wait_ge(item_out, n * NITEMS + ITEMS.index(("k", c)) + 1)
                        for r in range(2):
                            for at in (HI[r], LO[r]):
                                last = dve.tensor_copy(k_hi[at, c % 2, r, :], k_c[HI[r], c % 2, :])
                        last.then_inc(k_hi_ready, 1)
                        if c == 0:
                            dve.drain()
                            for r in range(2):
                                dve.tensor_tensor(k_lo[HI[r], 0, r, :], k_c[HI[r], 0, :],
                                                  k_hi[HI[r], 0, r, :].bitcast(fp32), ALU.subtract).then_inc(k_split, 1)

                    split_q(0)
                    split_k(0)
                    split_q(1)
                    for slot in range(SLOTS_W):
                        w = slot
                        if slot >= 4 and slot % 2 == 0:
                            c = slot // 2 - 2
                            dve.wait_ge(pair_done, n * PAIRS + 2 * c + 2)
                            dve.tensor_copy(dkT[:, c, :], ps[:, OUT_K, :]).then_inc(dk_ready, 1)
                        if slot < PAIRS:
                            for r in range(2):
                                dve.wait_ge(scores, n * 2 * PAIRS + 2 * w + r + 1)
                                dve.tensor_reduce(neg_max[:, (2 * w + r) % 6, :], ps[:, 2 + r, :].rearrange("p (i m) -> p i m", i=TB),
                                                  axis=AX.X, op=ALU.max, negate=True).then_inc(max_ready, 1)
                            c = slot // 2 + 1 + slot % 2
                            if c < EC:
                                (split_k, split_q)[slot % 2](c)
                            for r in range(2):
                                u = (2 * w + r) % 6
                                dve.wait_ge(exp_ready, n * 2 * PAIRS + 2 * w + r + 1)
                                dve.reciprocal(row_sum[:, u, :], row_sum[:, u, :])
                                dve.drain()
                                for i in range(TB):
                                    last = dve.tensor_scalar(prob[u][:, i, :], prob[u][:, i, :], row_sum[:, u, i:i + 1], None, ALU.mult)
                                last.then_inc(prob_ready, 1)
                    dve.wait_ge(pair_done, n * PAIRS + PAIRS)
                    dve.tensor_copy(dkT[:, EC - 1, :], ps[:, OUT_K, :]).then_inc(dk_ready, 1)
                    for t in range(T):
                        dve.wait_ge(grad_product, n * T + t + 1)
                        dve.scalar_tensor_tensor(out=x[:, t, :], in0=ps[:, 2 + t, 0:D], scalar=ALPHA, in1=x[:, t, :],
                                                 op0=ALU.mult, op1=ALU.add)
                        dve.drain()
                        normalised(y[:, t, :, :], x[:, t, :], t, n + 2).then_inc(y_ready, 1)
                dve.tensor_tensor(s.h[:, :, :], s.h[:, :, :], x[:, :, :], ALU.add)


SE = 8
SCAP = 5 * NT // (4 * SE)
SF = 768
SM = SF // P


def switch_stage(nc, s, a):
    ctx = ExitStack()
    with ctx:
        def sb(name, shape, dt=fp32):
            return ctx.enter_context(nc.sbuf_tensor(name, shape, dt))

        def sem(name):
            return s.stage_semaphore(name)

        slots = SE * SCAP
        w_switch = sb("sw_w_switch", [DK, DC, SE])
        b_switch = sb("sw_b_switch", [1, SE])
        w1 = [sb(f"sw_w1_{k}", [DK, DC, SF]) for k in range(2)]
        w2 = [sb(f"sw_w2_{k}", [P, SM, D]) for k in range(2)]
        b1 = [sb(f"sw_b1_{k}", [P, SM]) for k in range(2)]
        b2 = [sb(f"sw_b2_{k}", [1, D]) for k in range(2)]
        row_max = sb("sw_row_max", [P, T])
        prob = sb("sw_prob", [P, T, SE])
        top8 = sb("sw_top8", [P, T, 8])
        top8_at = sb("sw_top8_at", [P, T, 8], u32)
        p_max = sb("sw_p_max", [P, T])
        route = sb("sw_route", [P, T])
        all_p = sb("sw_all_p", [P, NT])
        all_r = sb("sw_all_r", [P, NT])
        iota_j = sb("sw_iota_j", [P, slots])
        tok_id = sb("sw_tok_id", [P, T])
        ahead = sb("sw_ahead", [P, T, NT])
        rank = sb("sw_rank", [P, T])
        keep = sb("sw_keep", [P, T])
        dest = sb("sw_dest", [P, T])
        select = sb("sw_select", [P, T, slots])
        selectT = sb("sw_selectT", [SCAP, SE, NT])
        xT = sb("sw_xT", [DK, DC, slots])
        pre = [sb(f"sw_pre{k}", [P, SM, SCAP]) for k in range(2)]
        hid = [sb(f"sw_hid{k}", [P, SM, SCAP]) for k in range(2)]
        out = sb("sw_out", [SCAP, SE, D])
        ps = s.ps

        small_in = sem("sw_small_in")
        w_in = [sem(f"sw_w_in{k}") for k in range(2)]
        var_ready, rstd_ready = sem("sw_var_ready"), sem("sw_rstd_ready")
        consts = sem("sw_consts")
        u_ready = sem("sw_u_ready")
        u_transposed = sem("sw_u_transposed")
        uT_ready = sem("sw_uT_ready")
        logits_ready = sem("sw_logits_ready")
        shifted = sem("sw_shifted")
        exp_ready = sem("sw_exp_ready")
        routed = sem("sw_routed")
        spread = sem("sw_spread")
        select_ready = sem("sw_select_ready")
        x_product = sem("sw_x_product")
        xT_ready = sem("sw_xT_ready")
        select_transposed = sem("sw_select_transposed")
        selectT_ready = sem("sw_selectT_ready")
        up_product = [sem(f"sw_up_product{k}") for k in range(2)]
        pre_ready = [sem(f"sw_pre_ready{k}") for k in range(2)]
        hid_ready = [sem(f"sw_hid_ready{k}") for k in range(2)]
        down_product = [sem(f"sw_down_product{k}") for k in range(2)]
        out_ready = [sem(f"sw_out_ready{k}") for k in range(2)]
        back_product = sem("sw_back_product")

        with nc.Block() as block:
            @block.sync
            def _(sp):
                sp.dma_start(w_switch[:, :, :], a["sw_w_switch"].rearrange("(c p) e -> p c e", p=DK)).then_inc(small_in, 16)
                sp.dma_start(b_switch[:, :], a["sw_b_switch"]).then_inc(small_in, 16)
                with sp.Fori(0, SE // 2) as i:
                    for k in range(2):
                        e = bass.ds(2 * i + k, 1)
                        sp.wait_ge(down_product[k], i + 1)
                        sp.dma_start(w1[k][:, :, :], a["sw_w1"][e, :, :].rearrange("o (c p) f -> p (o c) f", p=DK)).then_inc(w_in[k], 16)
                        sp.dma_start(b1[k][:, :], a["sw_b1"][e, :, :].rearrange("o p m -> p (o m)")).then_inc(w_in[k], 16)
                        sp.dma_start(w2[k][:, :, :], a["sw_w2"][e, :, :].rearrange("o (c p) d -> p (o c) d", p=P)).then_inc(w_in[k], 16)
                        sp.dma_start(b2[k][:, :], a["sw_b2"][e, :]).then_inc(w_in[k], 16)

            @block.gpsimd
            def _(pool):
                pool.iota(iota_j[:, :], [[1, slots]], base=0, channel_multiplier=0, allow_small_or_imprecise_dtypes=True).then_inc(consts, 1)
                pool.iota(tok_id[:, :], [[P, T]], base=0, channel_multiplier=1, allow_small_or_imprecise_dtypes=True).then_inc(consts, 1)
                ln_pool(pool, s, 0, var_ready, rstd_ready)

            @block.tensor
            def _(pe):
                for k in range(2):
                    pe.sem_inc(down_product[k], 1)
                pe.wait_ge(u_ready, 1)
                transpose_u(pe, s).then_inc(u_transposed, 1)
                pe.wait_ge(uT_ready, 1)
                pe.wait_ge(small_in, 32)
                for t in range(T):
                    at = slice(t * SE, (t + 1) * SE)
                    for c in range(DC):
                        pe.matmul(ps[:, 2, at], lhsT=s.uT[:, c, t * P:(t + 1) * P], rhs=w_switch[:, c, :], start=(c == 0), stop=False)
                    last = pe.matmul(ps[:, 2, at], lhsT=s.ones[0:1, :], rhs=b_switch[:, :], start=False, stop=True)
                last.then_inc(logits_ready, 1)
                pe.wait_ge(routed, 1)
                for bank, src in ((3, p_max), (4, route)):
                    for t in range(T):
                        last = pe.matmul(ps[:, bank, t * P:(t + 1) * P], lhsT=src[:, t:t + 1].broadcast_to((P, P)),
                                         rhs=s.ident[:, :], start=True, stop=True)
                last.then_inc(spread, 1)
                pe.wait_ge(select_ready, 1)
                for c in range(DC):
                    for half in range(2):
                        for t in range(T):
                            last = pe.matmul(ps[0:DK, 2 * c + half, 0:slots // 2], lhsT=s.u[:, t, c * DK:(c + 1) * DK],
                                             rhs=select[:, t, half * slots // 2:(half + 1) * slots // 2],
                                             start=(t == 0), stop=(t == T - 1))
                last.then_inc(x_product, 1)
                for e in range(SE):
                    if e >= 4:
                        pe.wait_ge(selectT_ready, e - 3)
                    for t in range(T):
                        last = pe.transpose(ps[0:SCAP, 4 + e % 4, t * P:(t + 1) * P], select[:, t, e * SCAP:(e + 1) * SCAP], s.ident[:, :])
                    last.then_inc(select_transposed, 1)
                pe.wait_ge(xT_ready, 1)
                pe.wait_ge(selectT_ready, SE)
                with pe.Fori(0, SE // 2) as i:
                    for k in range(2):
                        pe.wait_ge(w_in[k], i * 64 + 64)
                        pe.wait_ge(pre_ready[k], i + 1)
                        for m in range(SM):
                            for c in range(DC):
                                last = pe.matmul(ps[:, 4 + k, m * SCAP:(m + 1) * SCAP], lhsT=w1[k][:, c, m * P:(m + 1) * P],
                                                 rhs=xT[:, c, bass.ds((2 * i + k) * SCAP, SCAP)], start=(c == 0), stop=(c == DC - 1))
                        last.then_inc(up_product[k], 1)
                    for k in range(2):
                        pe.wait_ge(hid_ready[k], i + 2)
                        pe.wait_ge(out_ready[k], i + 1)
                        for m in range(SM):
                            pe.matmul(ps[0:SCAP, 6 + k, 0:D], lhsT=hid[k][:, m, :], rhs=w2[k][:, m, :], start=(m == 0), stop=False)
                        pe.matmul(ps[0:SCAP, 6 + k, 0:D], lhsT=s.ones[0:1, 0:SCAP], rhs=b2[k][:, :], start=False, stop=True).then_inc(down_product[k], 1)
                for k in range(2):
                    pe.wait_ge(out_ready[k], SE // 2 + 1)
                for t in range(T):
                    for e in range(SE):
                        last = pe.matmul(ps[:, t, 0:D], lhsT=selectT[:, e, t * P:(t + 1) * P], rhs=out[:, e, :],
                                         start=(e == 0), stop=(e == SE - 1))
                last.then_inc(back_product, 1)

            @block.scalar
            def _(act):
                for k in range(2):
                    act.sem_inc(hid_ready[k], 1)
                act.wait_ge(shifted, 1)
                act.activation(prob[:, :, :], prob[:, :, :], ACT.Exp).then_inc(exp_ready, 1)
                for e in range(SE):
                    act.wait_ge(select_transposed, e + 1)
                    act.copy(selectT[:, e, :], ps[0:SCAP, 4 + e % 4, :]).then_inc(selectT_ready, 1)
                with act.Fori(0, SE // 2) as i:
                    for k in range(2):
                        act.wait_ge(pre_ready[k], i + 2)
                        act.wait_ge(down_product[k], i + 1)
                        act.activation(hid[k][:, :, :], pre[k][:, :, :], ACT.Gelu).then_inc(hid_ready[k], 1)

            @block.vector
            def _(dve):
                for k in range(2):
                    dve.sem_inc(pre_ready[k], 1)
                    dve.sem_inc(out_ready[k], 1)
                ln_vector(dve, s, s.u, s.h, 0, var_ready, rstd_ready).then_inc(u_ready, 1)
                dve.wait_ge(u_transposed, 1)
                dve.tensor_copy(s.uT[:, :, :], ps[0:DK, 0:DC, :]).then_inc(uT_ready, 1)
                logits = ps[:, 2, 0:T * SE].rearrange("p (t e) -> p t e", t=T)
                dve.wait_ge(logits_ready, 1)
                dve.reduce_max(row_max[:, :], logits, AX.X)
                dve.drain()
                dve.tensor_tensor(prob[:, :, :], logits, row_max[:, :].unsqueeze(2).broadcast_to((P, T, SE)), ALU.subtract).then_inc(shifted, 1)
                dve.wait_ge(exp_ready, 1)
                dve.reduce_sum(row_max[:, :], prob[:, :, :], AX.X)
                dve.drain()
                dve.reciprocal(row_max[:, :], row_max[:, :])
                dve.drain()
                dve.tensor_tensor(prob[:, :, :], prob[:, :, :], row_max[:, :].unsqueeze(2).broadcast_to((P, T, SE)), ALU.mult)
                dve.drain()
                for t in range(T):
                    dve.max(top8[:, t, :], prob[:, t, :])
                dve.drain()
                for t in range(T):
                    dve.max_index(top8_at[:, t, :], top8[:, t, :], prob[:, t, :])
                dve.drain()
                dve.tensor_copy(p_max[:, :], top8[:, :, 0])
                dve.tensor_copy(route[:, :], top8_at[:, :, 0]).then_inc(routed, 1)
                dve.wait_ge(consts, 2)
                for t in range(T):
                    dve.tensor_scalar(ahead[:, t, :], iota_j[:, 0:NT], tok_id[:, t:t + 1], None, ALU.is_lt)
                dve.wait_ge(spread, 1)
                dve.tensor_copy(all_p[:, :], ps[:, 3, :])
                dve.tensor_copy(all_r[:, :], ps[:, 4, :])
                dve.drain()
                for src, value, how in ((all_p, p_max, (ALU.is_equal, ALU.mult)), (all_p, p_max, (ALU.is_gt, ALU.add)),
                                        (all_r, route, (ALU.is_equal, ALU.mult))):
                    for t in range(T):
                        dve.scalar_tensor_tensor(out=ahead[:, t, :], in0=src[:, :], scalar=value[:, t:t + 1], in1=ahead[:, t, :],
                                                 op0=how[0], op1=how[1])
                    dve.drain()
                dve.reduce_sum(rank[:, :], ahead[:, :, :], AX.X)
                dve.drain()
                dve.tensor_scalar(keep[:, :], rank[:, :], float(SCAP), None, ALU.is_lt)
                dve.scalar_tensor_tensor(out=dest[:, :], in0=route[:, :], scalar=float(SCAP), in1=rank[:, :], op0=ALU.mult, op1=ALU.add)
                dve.drain()
                dve.scalar_tensor_tensor(out=dest[:, :], in0=dest[:, :], scalar=1.0, in1=keep[:, :], op0=ALU.add, op1=ALU.mult)
                dve.drain()
                dve.tensor_scalar(dest[:, :], dest[:, :], -1.0, None, ALU.add)
                dve.drain()
                for t in range(T):
                    last = dve.tensor_scalar(select[:, t, :], iota_j[:, :], dest[:, t:t + 1], None, ALU.is_equal)
                last.then_inc(select_ready, 1)
                dve.wait_ge(x_product, 1)
                dve.tensor_copy(xT[:, :, :].rearrange("p c (h n) -> p (c h) n", h=2), ps[0:DK, 0:2 * DC, 0:slots // 2]).then_inc(xT_ready, 1)
                with dve.Fori(0, SE // 2) as i:
                    for k in range(2):
                        dve.wait_ge(up_product[k], i + 1)
                        dve.wait_ge(w_in[k], i * 64 + 64)
                        dve.wait_ge(hid_ready[k], i + 1)
                        dve.tensor_tensor(pre[k][:, :, :], ps[:, 4 + k, 0:SM * SCAP].rearrange("p (m n) -> p m n", m=SM),
                                          b1[k][:, :].unsqueeze(2).broadcast_to((P, SM, SCAP)), ALU.add).then_inc(pre_ready[k], 1)
                    for k in range(2):
                        dve.wait_ge(down_product[k], i + 2)
                        dve.tensor_copy(out[:, bass.ds(2 * i + k, 1), :], ps[0:SCAP, 6 + k, 0:D].unsqueeze(1)).then_inc(out_ready[k], 1)
                dve.tensor_scalar(keep[:, :], keep[:, :], -1.0, 1.0, ALU.mult, ALU.add)
                dve.drain()
                dve.wait_ge(back_product, 1)
                for t in range(T):
                    dve.scalar_tensor_tensor(out=s.u[:, t, :], in0=s.u[:, t, :], scalar=keep[:, t:t + 1], in1=ps[:, t, 0:D],
                                             op0=ALU.mult, op1=ALU.add)
                dve.drain()
                for t in range(T):
                    dve.scalar_tensor_tensor(out=s.h[:, t, :], in0=s.u[:, t, :], scalar=p_max[:, t:t + 1], in1=s.h[:, t, :],
                                             op0=ALU.mult, op1=ALU.add)


def laid_out(i):
    g = {k: np.asarray(v) for k, v in i.items()}
    put = {}

    def add(name, a):
        put[name] = np.ascontiguousarray(a)

    add("patches", g["x"].reshape(2, 32, 16, 8, 16, 8).transpose(1, 3, 5, 0, 2, 4).reshape(2048, NT))
    add("conv_w", g["L0_tok_conv_w"].reshape(TD, 2048).T)
    add("conv_b", g["L0_tok_conv_b"].reshape(1, TD))
    add("tok_cols", np.concatenate([np.stack([g["L0_tok_" + k] for k in ("ln1_g", "ln1_b", "ln2_g", "ln2_b")], axis=2),
                                    g["L0_tok_ff1_b"].reshape(LAYERS, FC, P).transpose(0, 2, 1)], axis=2))
    add("tok_rows", np.stack([g["L0_tok_out_b"], g["L0_tok_ff2_b"]], axis=1).reshape(LAYERS, 1, 2, TD))
    add("qkv_w", g["L0_tok_qkv_w"])
    add("out_w", g["L0_tok_out_w"])
    add("ff1_w", g["L0_tok_ff1_w"])
    add("ff2_w", g["L0_tok_ff2_w"])
    add("tok_lnf", np.stack([g["L0_tok_lnf_g"], g["L0_tok_lnf_b"]], axis=1))
    add("head_w", g["L0_tok_head_w"])
    add("head_b", g["L0_tok_head_b"].reshape(1, D))
    add("mb_w_in", g["L0_attn_w_in"].T)
    add("mb_cols", np.concatenate([g["L0_attn_w_conv"][:, 0, :]] + [g["L0_attn_" + k].reshape(DIN, 1)
                                   for k in ("b_conv", "b_dt", "D_param")], axis=1))
    add("mb_a_log", g["L0_attn_A_log"])
    add("mb_w_x", g["L0_attn_w_xproj"].T)
    add("mb_w_dt", g["L0_attn_w_dt"].T)
    add("mb_w_out", g["L0_attn_w_out"].T)
    add("mb_w_norm", g["L0_attn_w_norm"].reshape(1, D))
    add("moe_w_router", g["L0_ffn_Wg"].T)
    add("moe_e_bias", g["L0_ffn_e_bias"].reshape(1, NE))
    add("moe_w_gu", g["L0_ffn_W_gate_up"])
    add("moe_w_d", g["L0_ffn_W_down"])
    add("moe_w_sgu", np.stack([g["L0_ffn_Wsg"], g["L0_ffn_Wsu"]]))
    add("moe_w_sd", g["L0_ffn_Wsd"])
    add("en_ln", np.stack([g["L1_attn_ln_gamma"], g["L1_attn_ln_beta"]], axis=1))
    w = np.stack([g["L1_attn_wq"].reshape(EM, D), g["L1_attn_wk"].reshape(EM, D), g["L1_attn_xi"]])
    add("en_w", w)
    add("en_wT", w.transpose(0, 2, 1))
    add("sw_w_switch", g["L1_ffn_switch_w"])
    add("sw_b_switch", g["L1_ffn_switch_b"].reshape(1, SE))
    add("sw_w1", g["L1_ffn_w1"])
    add("sw_b1", g["L1_ffn_b1"].reshape(SE, SM, P).transpose(0, 2, 1))
    add("sw_w2", g["L1_ffn_w2"])
    add("sw_b2", g["L1_ffn_b2"])
    return put


def vit_tower(nc, a):
    with ExitStack() as ctx:
        s = Shared(nc, ctx)
        setup_stage(nc, s)
        s.end_stage()
        tok_stage(nc, s, a)
        s.end_stage()
        mamba_stage(nc, s, a)
        s.end_stage()
        moe_stage(nc, s, a)
        s.end_stage()
        energy_stage(nc, s, a)
        s.end_stage()
        switch_stage(nc, s, a)
        s.end_stage()
        h_stored = s.stage_semaphore("h_stored")
        with nc.Block() as block:
            @block.sync
            def _(sp):
                sp.dma_start(a["out"].rearrange("(t p) d -> p t d", p=P), s.h[:, :, :]).then_inc(h_stored, 16)
                sp.wait_ge(h_stored, 16)


def kernel(**inputs):
    import concourse.bacc as bacc
    from concourse.bass_utils import run_bass_kernel_spmd

    nc = bacc.Bacc("TRN2", target_bir_lowering=False, num_devices=1)
    put = laid_out(inputs)
    a = {name: nc.dram_tensor("in_" + name, v.shape, mybir.dt.from_np(v.dtype), kind="ExternalInput").ap()
         for name, v in put.items()}
    a["out"] = nc.dram_tensor("out_h", (NT, D), fp32, kind="ExternalOutput").ap()
    vit_tower(nc, a)
    r = run_bass_kernel_spmd(nc, [{"in_" + name: v for name, v in put.items()}], core_ids=[0])
    return r.results[0]["out_h"].reshape(BATCH, SEQ, D)
```

```python
from contextlib import ExitStack

import numpy as np

import concourse.bass as bass
from concourse import mybir
from concourse.alu_op_type import AluOpType as ALU

fp32 = mybir.dt.float32
f32r = mybir.dt.float32r
u32 = mybir.dt.uint32
ACT = mybir.ActivationFunctionType
AX = mybir.AxisListType

P = 128
BATCH, SEQ = 2, 256
NT = BATCH * SEQ
T = NT // P
TB = SEQ // P
D = 192
DK, DC = 96, 2
EPS = 1e-5
BANK = 512

NE = 128
TOP = 6
CAP = 192
SLOTS = 96
GROUPS = NE * CAP // SLOTS
SPARE = GROUPS
CLEARS = 12
CLEAR_COLS = (GROUPS + 1) * SLOTS * D // P // CLEARS


class Shared:

    def __init__(self, nc, ctx):
        self.nc = nc
        self.h = ctx.enter_context(nc.sbuf_tensor("h", [P, T, D], fp32))
        self.u = ctx.enter_context(nc.sbuf_tensor("u", [P, T, D], fp32))
        self.uT = ctx.enter_context(nc.sbuf_tensor("uT", [DK, DC, NT], fp32))
        self.ident = ctx.enter_context(nc.sbuf_tensor("ident", [P, P], fp32))
        self.ones = ctx.enter_context(nc.sbuf_tensor("ones", [P, P], fp32))
        self.neghalf = ctx.enter_context(nc.sbuf_tensor("neghalf", [P, T], fp32))
        self.stats = ctx.enter_context(nc.sbuf_tensor("stats", [P, T, 6], fp32))
        self.mv = ctx.enter_context(nc.sbuf_tensor("mv", [P, T, 2], fp32))
        self.var = ctx.enter_context(nc.sbuf_tensor("var", [P, T], fp32))
        self.rstd = ctx.enter_context(nc.sbuf_tensor("rstd", [P, T], fp32))
        self.ps = ctx.enter_context(nc.psum_tensor("ps", [P, 8, BANK], fp32))
        self.y_of_slot = nc.dram_tensor("y_of_slot", [(GROUPS + 1) * SLOTS, D], fp32).ap()
        self.stage_semaphores = []

    def stage_semaphore(self, name):
        self.stage_semaphores.append(self.nc.alloc_semaphore(name))
        return self.stage_semaphores[-1]

    def end_stage(self):
        self.nc.clear_and_free_semaphores(self.stage_semaphores)
        self.stage_semaphores = []
        self.nc.all_engine_barrier()


def setup_stage(nc, s):
    consts_set = s.stage_semaphore("consts_set")
    with nc.Block() as block:
        @block.gpsimd
        def _(pool):
            pool.memset(s.ident[:, :], 0.0).then_inc(consts_set, 1)
            pool.memset(s.ones[:, :], 1.0).then_inc(consts_set, 1)
            pool.memset(s.neghalf[:, :], -0.5).then_inc(consts_set, 1)
            pool.wait_ge(consts_set, 3)
            pool.affine_select(out=s.ident[:, :], in_=s.ident[:, :], compare_op=ALU.not_equal,
                               fill=1.0, base=0, pattern=[[-1, P]], channel_multiplier=1)


def clear_table(sp, s, zeros, cleared):
    lot = (GROUPS + 1) * SLOTS // CLEARS
    for n in range(CLEARS):
        sp.dma_start(s.y_of_slot[n * lot:(n + 1) * lot, :].rearrange("r d -> (r d)").rearrange("(p n) -> p n", p=P),
                     zeros[:, :]).then_inc(cleared, 16)


def ln_vector(dve, s, y, x, n, var_ready, rstd_ready):
    for t in range(T):
        dve.bn_stats(s.stats[:, t, :], x[:, t, :])
    dve.drain()
    for t in range(T):
        dve.bn_aggr(s.mv[:, t, :], s.stats[:, t, :])
    dve.drain()
    dve.tensor_scalar(s.var[:, :], s.mv[:, :, 1], EPS, None, ALU.add).then_inc(var_ready, 1)
    dve.wait_ge(rstd_ready, n + 1)
    for t in range(T):
        last = dve.tensor_scalar(y[:, t, :], x[:, t, :], s.mv[:, t, 0:1], s.rstd[:, t:t + 1],
                                 ALU.subtract, ALU.mult)
    return last


def ln_pool(pool, s, n, var_ready, rstd_ready):
    pool.wait_ge(var_ready, n + 1)
    pool.tensor_tensor(s.rstd[:, :], s.var[:, :], s.neghalf[:, :], ALU.pow).then_inc(rstd_ready, 1)


def transpose_u(pe, s):
    for c in range(DC):
        for t in range(T):
            last = pe.transpose(s.ps[0:DK, c, t * P:(t + 1) * P], s.u[:, t, c * DK:(c + 1) * DK],
                                s.ident[:, :])
    return last


TD = 128
HEADS, DH = 8, 64
INNER = HEADS * DH
IC = INNER // P
KC = 2048 // P
FM = 512
FC = FM // P
LAYERS = 2


def tok_stage(nc, s, a):
    ctx = ExitStack()
    with ctx:
        def sb(name, shape):
            return ctx.enter_context(nc.sbuf_tensor(name, shape, fp32))

        def sem(name):
            return s.stage_semaphore(name)

        patches = sb("patches", [P, KC, NT])
        conv_w = sb("conv_w", [P, KC, TD])
        conv_b = sb("conv_b", [1, TD])
        x = sb("tok_x", [P, T, TD])
        y = sb("tok_y", [P, T, TD])
        yT = sb("tok_yT", [P, NT])
        cols_all = sb("tok_cols_all", [P, LAYERS, 8])
        cols = sb("tok_cols", [P, 8])
        rows = sb("tok_rows", [1, LAYERS, 2, TD])
        wqkv = sb("tok_wqkv", [P, 3 * INNER])
        wo = sb("tok_wo", [P, IC, TD])
        w1 = sb("tok_w1", [P, FM])
        w2 = sb("tok_w2", [P, FC, TD])
        lnf = sb("tok_lnf", [P, 2])
        head_w = sb("tok_head_w", [P, D])
        head_b = sb("tok_head_b", [1, D])
        kT = sb("tok_kT", [P, IC, NT])
        kneg = sb("tok_kneg", [P, IC, BATCH])
        ksum = sb("tok_ksum", [P, IC, BATCH])
        krec = sb("tok_krec", [P, IC, BATCH])
        k = sb("tok_k", [P, T, INNER])
        q = sb("tok_q", [P, T, INNER])
        qmax = sb("tok_qmax", [P, T, HEADS])
        qsum = sb("tok_qsum", [P, T, HEADS])
        qT = sb("tok_qT", [P, IC, NT])
        v = sb("tok_v", [P, T, INNER])
        ctxT = sb("tok_ctx", [P, BATCH, IC, P])
        attT = sb("tok_attT", [P, IC, NT])
        hidT = sb("tok_hidT", [P, FC, NT])
        zeros = sb("tok_zeros", [P, CLEAR_COLS])
        ps = s.ps

        zeros_ready = sem("tok_zeros_ready")
        cleared = sem("tok_cleared")
        patch_in = [sem(f"patch_in{g}") for g in range(4)]
        head_in = sem("tok_head_in")
        cols_in = sem("tok_cols_in")
        qkv_in, wo_in, w1_in, w2_in = sem("tok_qkv_in"), sem("tok_wo_in"), sem("tok_w1_in"), sem("tok_w2_in")
        layer_done = sem("tok_layer_done")
        embedded = sem("tok_embedded")
        var_ready, rstd_ready = sem("tok_var_ready"), sem("tok_rstd_ready")
        y_ready = sem("tok_y_ready")
        y_transposed = sem("tok_y_transposed")
        yT_ready = sem("tok_yT_ready")
        kT_scores = sem("tok_kT_scores")
        k_max = sem("tok_k_max")
        k_exp = sem("tok_k_exp")
        q_scores = sem("tok_q_scores")
        q_shifted = sem("tok_q_shifted")
        q_exp = sem("tok_q_exp")
        q_normed = sem("tok_q_normed")
        v_product = sem("tok_v_product")
        v_ready = sem("tok_v_ready")
        k_transposed = sem("tok_k_transposed")
        k_ready = sem("tok_k_ready")
        q_transposed = sem("tok_q_transposed")
        qT_ready = sem("tok_qT_ready")
        ctx_zeroed = sem("tok_ctx_zeroed")
        ctx_product = sem("tok_ctx_product")
        ctx_ready = sem("tok_ctx_ready")
        att_product = sem("tok_att_product")
        att_ready = sem("tok_att_ready")
        out_product = sem("tok_out_product")
        hid_product = sem("tok_hid_product")
        hid_ready = sem("tok_hid_ready")
        ff_product = sem("tok_ff_product")
        head_product = sem("tok_head_product")

        with nc.Block() as block:
            @block.sync
            def _(sp):
                patch_v = a["patches"].rearrange("(k p) t -> p k t", p=P)
                conv_v = a["conv_w"].rearrange("(k p) d -> p k d", p=P)
                for g in range(4):
                    lot = slice(g * KC // 4, (g + 1) * KC // 4)
                    sp.dma_start(conv_w[:, lot, :], conv_v[:, lot, :]).then_inc(patch_in[g], 16)
                    sp.dma_start(patches[:, lot, :], patch_v[:, lot, :]).then_inc(patch_in[g], 16)
                for l in range(LAYERS):
                    sp.dma_start(cols_all[:, l, :], a["tok_cols"][l]).then_inc(cols_in, 16)
                    sp.dma_start(rows[:, l, :, :], a["tok_rows"][l]).then_inc(cols_in, 16)
                sp.dma_start(conv_b[:, :], a["conv_b"]).then_inc(head_in, 16)
                sp.dma_start(lnf[:, :], a["tok_lnf"]).then_inc(head_in, 16)
                sp.dma_start(head_w[:, :], a["head_w"]).then_inc(head_in, 16)
                sp.dma_start(head_b[:, :], a["head_b"]).then_inc(head_in, 16)
                for l in range(LAYERS):
                    if l:
                        sp.wait_ge(v_product, l * T)
                    sp.dma_start(wqkv[:, :], a["qkv_w"][l]).then_inc(qkv_in, 16)
                    if l:
                        sp.wait_ge(out_product, l)
                    sp.dma_start(wo[:, :, :], a["out_w"][l].rearrange("(c p) d -> p c d", p=P)).then_inc(wo_in, 16)
                    if l:
                        sp.wait_ge(hid_product, l * FC)
                    sp.dma_start(w1[:, :], a["ff1_w"][l]).then_inc(w1_in, 16)
                    if l:
                        sp.wait_ge(ff_product, l)
                    sp.dma_start(w2[:, :, :], a["ff2_w"][l].rearrange("(c p) d -> p c d", p=P)).then_inc(w2_in, 16)
                sp.wait_ge(zeros_ready, 1)
                clear_table(sp, s, zeros, cleared)
                sp.wait_ge(cleared, CLEARS * 16)

            @block.gpsimd
            def _(pool):
                pool.memset(ctxT[:, :, :, :], 0.0).then_inc(ctx_zeroed, 1)
                pool.wait_ge(ctx_zeroed, 1)
                pool.memset(zeros[:, :], 0.0).then_inc(zeros_ready, 1)
                pool.wait_ge(zeros_ready, 1)
                with pool.Fori(0, 2 * LAYERS + 1) as n:
                    ln_pool(pool, s, n, var_ready, rstd_ready)

            @block.tensor
            def _(pe):
                for g in range(4):
                    pe.wait_ge(patch_in[g], 32)
                    for kc in range(g * KC // 4, (g + 1) * KC // 4):
                        for t in range(T):
                            pe.matmul(ps[:, t, 0:TD], lhsT=patches[:, kc, t * P:(t + 1) * P],
                                      rhs=conv_w[:, kc, :], start=(kc == 0), stop=False)
                pe.wait_ge(head_in, 64)
                for t in range(T):
                    last = pe.matmul(ps[:, t, 0:TD], lhsT=s.ones[0:1, :], rhs=conv_b[:, :],
                                     start=False, stop=True)
                last.then_inc(embedded, 1)

                def transpose_y(n):
                    pe.wait_ge(y_ready, n + 1)
                    for t in range(T):
                        last = pe.transpose(ps[:, 0, t * P:(t + 1) * P], y[:, t, :], s.ident[:, :])
                    last.then_inc(y_transposed, 1)
                    pe.wait_ge(yT_ready, n + 1)

                pe.wait_ge(cols_in, LAYERS * 32)
                with pe.Fori(0, LAYERS) as l:
                    transpose_y(2 * l)
                    pe.wait_ge(qkv_in, l * 16 + 16)
                    for c in range(IC):
                        pe.matmul(ps[:, 1 + c, :], lhsT=wqkv[:, INNER + c * P:INNER + (c + 1) * P],
                                  rhs=yT[:, :], start=True, stop=True).then_inc(kT_scores, 1)
                    for t in range(T):
                        pe.matmul(ps[:, (5 + t) % 8, :], lhsT=yT[:, t * P:(t + 1) * P],
                                  rhs=wqkv[:, 0:INNER], start=True, stop=True).then_inc(q_scores, 1)
                    for t in range(T):
                        pe.wait_ge(k_exp, l * IC + t + 1)
                        pe.matmul(ps[:, 1 + t, :], lhsT=yT[:, t * P:(t + 1) * P],
                                  rhs=wqkv[:, 2 * INNER:3 * INNER], start=True, stop=True).then_inc(v_product, 1)
                    for t in range(T):
                        pe.wait_ge(q_shifted, l * T + t + 1)
                        for c in range(IC):
                            last = pe.transpose(ps[:, (5 + t) % 8, c * P:(c + 1) * P],
                                                kT[:, c, t * P:(t + 1) * P], s.ident[:, :])
                        last.then_inc(k_transposed, 1)
                    pe.wait_ge(k_ready, l * T + T)
                    pe.wait_ge(v_ready, l * T + T)
                    for b in range(BATCH):
                        for c in range(IC):
                            for i in range(TB):
                                last = pe.matmul(ps[:, 5 + b, c * P:(c + 1) * P],
                                                 lhsT=k[:, b * TB + i, c * P:(c + 1) * P],
                                                 rhs=v[:, b * TB + i, c * P:(c + 1) * P],
                                                 start=(i == 0), stop=(i == TB - 1))
                        last.then_inc(ctx_product, 1)
                    for c in range(IC):
                        pe.wait_ge(q_normed, l * T + T)
                        pe.wait_ge(v_ready, l * T + c + 1)
                        for t in range(T):
                            last = pe.transpose(ps[:, 1 + c, t * P:(t + 1) * P],
                                                q[:, t, c * P:(c + 1) * P], s.ident[:, :])
                        last.then_inc(q_transposed, 1)
                    pe.wait_ge(ctx_ready, l + 1)
                    for c in range(IC):
                        pe.wait_ge(qT_ready, l * IC + c + 1)
                        for b in range(BATCH):
                            last = pe.matmul(ps[:, 1 + c, b * SEQ:(b + 1) * SEQ], lhsT=ctxT[:, b, c, :],
                                             rhs=qT[:, c, b * SEQ:(b + 1) * SEQ], start=True, stop=True)
                        last.then_inc(att_product, 1)
                    pe.wait_ge(att_ready, l * IC + IC)
                    pe.wait_ge(wo_in, l * 16 + 16)
                    for t in range(T):
                        for c in range(IC):
                            pe.matmul(ps[:, 7, t * TD:(t + 1) * TD], lhsT=attT[:, c, t * P:(t + 1) * P],
                                      rhs=wo[:, c, :], start=(c == 0), stop=False)
                        last = pe.matmul(ps[:, 7, t * TD:(t + 1) * TD], lhsT=s.ones[0:1, :],
                                         rhs=rows[:, bass.ds(l, 1), 0, :], start=False, stop=True)
                    last.then_inc(out_product, 1)
                    transpose_y(2 * l + 1)
                    pe.wait_ge(w1_in, l * 16 + 16)
                    for m in range(FC):
                        pe.matmul(ps[:, 1 + m, :], lhsT=w1[:, m * P:(m + 1) * P], rhs=yT[:, :],
                                  start=True, stop=True).then_inc(hid_product, 1)
                    pe.wait_ge(hid_ready, l * FC + FC)
                    pe.wait_ge(w2_in, l * 16 + 16)
                    for t in range(T):
                        for m in range(FC):
                            pe.matmul(ps[:, 7, t * TD:(t + 1) * TD], lhsT=hidT[:, m, t * P:(t + 1) * P],
                                      rhs=w2[:, m, :], start=(m == 0), stop=False)
                        last = pe.matmul(ps[:, 7, t * TD:(t + 1) * TD], lhsT=s.ones[0:1, :],
                                         rhs=rows[:, bass.ds(l, 1), 1, :], start=False, stop=True)
                    last.then_inc(ff_product, 1)
                transpose_y(2 * LAYERS)
                for t in range(T):
                    pe.matmul(ps[:, 1 + t, 0:D], lhsT=yT[:, t * P:(t + 1) * P], rhs=head_w[:, :],
                              start=True, stop=False)
                    pe.matmul(ps[:, 1 + t, 0:D], lhsT=s.ones[0:1, :], rhs=head_b[:, :],
                              start=False, stop=True).then_inc(head_product, 1)

            @block.vector
            def _(dve):
                dve.sem_inc(layer_done, 1)
                dve.wait_ge(embedded, 1)
                dve.tensor_copy(x[:, :, :], ps[:, 0:T, 0:TD])
                dve.drain()

                def normalise(n, gain, shift):
                    ln_vector(dve, s, y, x, n, var_ready, rstd_ready).then_inc(y_ready, 1)
                    dve.wait_ge(y_transposed, n + 1)
                    dve.tensor_scalar(yT[:, :], ps[:, 0, :], gain, shift, ALU.mult, ALU.add).then_inc(yT_ready, 1)

                dve.wait_ge(cols_in, LAYERS * 32)
                with dve.Fori(0, LAYERS) as l:
                    dve.tensor_copy(cols[:, :], cols_all[:, bass.ds(l, 1), :].rearrange("p o k -> p (o k)"))
                    normalise(2 * l, cols[:, 0:1], cols[:, 1:2])
                    for c in range(IC):
                        dve.wait_ge(kT_scores, l * IC + c + 1)
                        dve.tensor_reduce(kneg[:, c, :], ps[:, 1 + c, :].rearrange("p (b n) -> p b n", b=BATCH),
                                          axis=AX.X, op=ALU.max, negate=True).then_inc(k_max, 1)
                    for t in range(T):
                        bank = ps[:, (5 + t) % 8, :].rearrange("p (h d) -> p h d", h=HEADS)
                        dve.wait_ge(q_scores, l * T + t + 1)
                        dve.reduce_max(qmax[:, t, :], bank, AX.X)
                        dve.drain()
                        dve.tensor_tensor(q[:, t, :].rearrange("p (h d) -> p h d", h=HEADS), bank,
                                          qmax[:, t, :].unsqueeze(2).broadcast_to((P, HEADS, DH)),
                                          ALU.subtract).then_inc(q_shifted, 1)
                    for t in range(T):
                        head = q[:, t, :].rearrange("p (h d) -> p h d", h=HEADS)
                        dve.wait_ge(q_exp, l * T + t + 1)
                        dve.reduce_sum(qsum[:, t, :], head, AX.X)
                        dve.drain()
                        dve.reciprocal(qsum[:, t, :], qsum[:, t, :])
                        dve.drain()
                        dve.tensor_tensor(head, head, qsum[:, t, :].unsqueeze(2).broadcast_to((P, HEADS, DH)),
                                          ALU.mult).then_inc(q_normed, 1)
                    dve.wait_ge(k_exp, l * IC + IC)
                    dve.reciprocal(krec[:, :, :], ksum[:, :, :])
                    dve.drain()
                    dve.tensor_scalar(krec[:, :, :], krec[:, :, :], float(DH) ** -0.5, None, ALU.mult)
                    dve.drain()
                    dve.wait_ge(ctx_zeroed, 1)
                    dve.wait_ge(ctx_product, l * BATCH + BATCH)
                    for b in range(BATCH):
                        for c in range(IC):
                            for r in (slice(0, DH), slice(DH, P)):
                                last = dve.tensor_scalar(ctxT[r, b, c, r], ps[r, 5 + b, c * P + r.start:c * P + r.stop],
                                                         krec[r, c, b:b + 1], None, ALU.mult)
                    last.then_inc(ctx_ready, 1)
                    for c in range(IC):
                        dve.wait_ge(att_product, l * IC + c + 1)
                        dve.tensor_copy(attT[:, c, :], ps[:, 1 + c, :]).then_inc(att_ready, 1)
                    dve.wait_ge(out_product, l + 1)
                    dve.tensor_tensor(x[:, :, :], x[:, :, :], ps[:, 7, :].rearrange("p (t d) -> p t d", t=T), ALU.add)
                    dve.drain()
                    normalise(2 * l + 1, cols[:, 2:3], cols[:, 3:4])
                    dve.wait_ge(ff_product, l + 1)
                    dve.tensor_tensor(x[:, :, :], x[:, :, :], ps[:, 7, :].rearrange("p (t d) -> p t d", t=T),
                                      ALU.add).then_inc(layer_done, 1)
                    dve.wait_ge(layer_done, l + 2)
                dve.wait_ge(head_in, 64)
                normalise(2 * LAYERS, lnf[:, 0:1], lnf[:, 1:2])
                for t in range(T):
                    dve.wait_ge(head_product, t + 1)
                    dve.tensor_copy(s.h[:, t, :], ps[:, 1 + t, 0:D])

            @block.scalar
            def _(act):
                with act.Fori(0, LAYERS) as l:
                    for c in range(IC):
                        act.wait_ge(k_max, l * IC + c + 1)
                        for b in range(BATCH):
                            last = act.activation(kT[:, c, b * SEQ:(b + 1) * SEQ], ps[:, 1 + c, b * SEQ:(b + 1) * SEQ],
                                                  ACT.Exp, bias=kneg[:, c, b:b + 1], accum_out=ksum[:, c, b:b + 1])
                        last.then_inc(k_exp, 1)
                    for t in range(T):
                        act.wait_ge(q_shifted, l * T + t + 1)
                        act.activation(q[:, t, :], q[:, t, :], ACT.Exp).then_inc(q_exp, 1)
                    for t in range(T):
                        act.wait_ge(v_product, l * T + t + 1)
                        act.copy(v[:, t, :], ps[:, 1 + t, :]).then_inc(v_ready, 1)
                    for t in range(T):
                        act.wait_ge(k_transposed, l * T + t + 1)
                        act.copy(k[:, t, :], ps[:, (5 + t) % 8, :]).then_inc(k_ready, 1)
                    for c in range(IC):
                        act.wait_ge(q_transposed, l * IC + c + 1)
                        act.copy(qT[:, c, :], ps[:, 1 + c, :]).then_inc(qT_ready, 1)
                    for m in range(FC):
                        act.wait_ge(hid_product, l * FC + m + 1)
                        act.activation(hidT[:, m, :], ps[:, 1 + m, :], ACT.Gelu, bias=cols[:, 4 + m:5 + m]).then_inc(hid_ready, 1)


DIN = 2 * D
MC = DIN // P
NS = 16
KW = 4
R = (D + 15) // 16
PAD = KW - 1
BC_SLOTS = 4


def mamba_stage(nc, s, a):
    ctx = ExitStack()
    with ctx:
        def sb(name, shape):
            return ctx.enter_context(nc.sbuf_tensor(name, shape, fp32))

        def sem(name):
            return s.stage_semaphore(name)

        w_in = sb("mb_w_in", [DK, DC, 2 * DIN])
        cols = sb("mb_cols", [P, MC, KW + 3])
        a_log = sb("mb_a_log", [P, MC, NS])
        w_x = sb("mb_w_x", [P, MC, R + 2 * NS])
        w_dt = sb("mb_w_dt", [R, DIN])
        w_out = sb("mb_w_out", [P, MC, D])
        w_norm = sb("mb_w_norm", [P, D])
        xp = sb("mb_xp", [P, MC, BATCH, PAD + SEQ])
        xc = sb("mb_xc", [P, MC, NT])
        z = sb("mb_z", [P, MC, NT])
        dbc = sb("mb_dbc", [R + 2 * NS, NT])
        dt = sb("mb_dt", [P, MC, NT])
        soft = sb("mb_soft", [P, MC, NT])
        dtx = sb("mb_dtx", [P, MC, NT])
        b_all = sb("mb_b_all", [P, BC_SLOTS, NT])
        c_all = sb("mb_c_all", [P, BC_SLOTS, NT])
        decay = sb("mb_decay", [P, 2, MC, NT])
        drive = sb("mb_drive", [P, MC, NT])
        state = sb("mb_state", [P, 2, MC, NT])
        out_n = sb("mb_out_n", [P, 2, MC, NT])
        r = sb("mb_r", [P, T, D])
        sq = sb("mb_sq", [P, T, D])
        bc_dram = nc.dram_tensor("bc_rows", [2 * NS, NT], fp32).ap()
        ps = s.ps

        weights_in = sem("mb_weights_in")
        var_ready, rstd_ready = sem("mb_var_ready"), sem("mb_rstd_ready")
        pad_zeroed = sem("mb_pad_zeroed")
        u_ready = sem("mb_u_ready")
        u_transposed = sem("mb_u_transposed")
        uT_ready = sem("mb_uT_ready")
        x_product = sem("mb_x_product")
        conv_done = sem("mb_conv_done")
        xc_ready = sem("mb_xc_ready")
        dbc_product = sem("mb_dbc_product")
        dbc_ready = sem("mb_dbc_ready")
        bc_stored = sem("mb_bc_stored")
        dt_product = sem("mb_dt_product")
        biased = sem("mb_biased")
        log_ready = sem("mb_log_ready")
        dt_ready = sem("mb_dt_ready")
        a_exp = sem("mb_a_exp")
        a_ready = sem("mb_a_ready")
        skip_ready = sem("mb_skip_ready")
        bc_in = [sem(f"mb_bc_in{k}") for k in range(BC_SLOTS)]
        decay_ready = sem("mb_decay_ready")
        decay_free = sem("mb_decay_free")
        b_free = sem("mb_b_free")
        c_free = sem("mb_c_free")
        state_ready = sem("mb_state_ready")
        out_ready = sem("mb_out_ready")
        out_summed = sem("mb_out_summed")
        gated = sem("mb_gated")
        out_product = sem("mb_out_product")

        with nc.Block() as block:
            @block.sync
            def _(sp):
                sp.dma_start(w_in[:, :, :], a["mb_w_in"].rearrange("(c p) e -> p c e", p=DK)).then_inc(weights_in, 16)
                sp.dma_start(cols[:, :, :], a["mb_cols"].rearrange("(c p) k -> p c k", p=P)).then_inc(weights_in, 16)
                sp.dma_start(a_log[:, :, :], a["mb_a_log"].rearrange("(c p) k -> p c k", p=P)).then_inc(weights_in, 16)
                sp.dma_start(w_x[:, :, :], a["mb_w_x"].rearrange("(c p) k -> p c k", p=P)).then_inc(weights_in, 16)
                sp.dma_start(w_dt[:, :], a["mb_w_dt"]).then_inc(weights_in, 16)
                sp.dma_start(w_out[:, :, :], a["mb_w_out"].rearrange("(c p) k -> p c k", p=P)).then_inc(weights_in, 16)
                sp.dma_start(w_norm[:, :], a["mb_w_norm"].broadcast_to((P, D))).then_inc(weights_in, 16)
                sp.wait_ge(dbc_ready, 1)
                sp.dma_start(bc_dram, dbc[R:R + 2 * NS, :]).then_inc(bc_stored, 16)
                sp.wait_ge(bc_stored, 16)
                with sp.Fori(0, NS // BC_SLOTS) as i:
                    for k in range(BC_SLOTS):
                        sp.wait_ge(b_free, i * BC_SLOTS + k + 1)
                        sp.wait_ge(c_free, i * BC_SLOTS + k + 1)
                        sp.dma_start(b_all[:, k, :], bc_dram[bass.ds(i * BC_SLOTS + k, 1), :].broadcast_to((P, NT))).then_inc(bc_in[k], 16)
                        sp.dma_start(c_all[:, k, :], bc_dram[bass.ds(i * BC_SLOTS + k + NS, 1), :].broadcast_to((P, NT))).then_inc(bc_in[k], 16)

            @block.gpsimd
            def _(pool):
                pool.memset(xp[:, :, :, 0:PAD], 0.0).then_inc(pad_zeroed, 1)
                ln_pool(pool, s, 0, var_ready, rstd_ready)
                pool.sem_inc(c_free, BC_SLOTS)
                with pool.Fori(0, NS // BC_SLOTS) as i:
                    for k in range(BC_SLOTS):
                        n = i * BC_SLOTS + k
                        pool.wait_ge(bc_in[k], i * 32 + 32)
                        for c in range(MC):
                            pool.wait_ge(state_ready, n * MC + c + 1)
                            pool.wait_ge(out_summed, n * MC + c + 1)
                            pool.tensor_tensor(out_n[:, k % 2, c, :], state[:, k % 2, c, :], c_all[:, k, :], ALU.mult).then_inc(out_ready, 1)
                            pool.wait_ge(out_ready, n * MC + c + 1)
                        pool.sem_inc(c_free, 1)
                ln_pool(pool, s, 1, var_ready, rstd_ready)

            @block.tensor
            def _(pe):
                pe.wait_ge(u_ready, 1)
                transpose_u(pe, s).then_inc(u_transposed, 1)
                pe.wait_ge(uT_ready, 1)
                pe.wait_ge(weights_in, 7 * 16)
                for c in range(2 * MC):
                    for kc in range(DC):
                        last = pe.matmul(ps[:, 2 + c, :], lhsT=w_in[:, kc, c * P:(c + 1) * P], rhs=s.uT[:, kc, :],
                                         start=(kc == 0), stop=(kc == DC - 1))
                    last.then_inc(x_product, 1)
                pe.wait_ge(xc_ready, MC)
                for c in range(MC):
                    last = pe.matmul(ps[0:R + 2 * NS, 0, :], lhsT=w_x[:, c, :], rhs=xc[:, c, :],
                                     start=(c == 0), stop=(c == MC - 1))
                last.then_inc(dbc_product, 1)
                pe.wait_ge(dbc_ready, 1)
                for c in range(MC):
                    pe.matmul(ps[:, 2 + c, :], lhsT=w_dt[:, c * P:(c + 1) * P], rhs=dbc[0:R, :],
                              start=True, stop=True).then_inc(dt_product, 1)
                pe.wait_ge(xc_ready, 2 * MC)
                for c in range(MC):
                    pe.wait_ge(skip_ready, c + 1)
                    pe.matmul(ps[:, 5 + c, :], lhsT=s.ident[:, :], rhs=soft[:, c, :], start=True, stop=False,
                                     skip_group_check=True)
                pe.sem_inc(out_summed, 2 * MC)
                with pe.Fori(0, NS // 2) as i:
                    for k in range(2):
                        for c in range(MC):
                            pe.wait_ge(out_ready, (2 * i + k) * MC + c + 1)
                            pe.matmul(ps[:, 5 + c, :], lhsT=s.ident[:, :], rhs=out_n[:, k, c, :], start=False, stop=False,
                                      skip_group_check=True).then_inc(out_summed, 1)
                pe.wait_ge(gated, 1)
                for t in range(T):
                    for c in range(MC):
                        last = pe.matmul(ps[:, t, 0:D], lhsT=xc[:, c, t * P:(t + 1) * P], rhs=w_out[:, c, :],
                                         start=(c == 0), stop=(c == MC - 1))
                last.then_inc(out_product, 1)

            @block.vector
            def _(dve):
                ln_vector(dve, s, s.u, s.h, 0, var_ready, rstd_ready).then_inc(u_ready, 1)
                dve.wait_ge(u_transposed, 1)
                dve.tensor_copy(s.uT[:, :, :], ps[0:DK, 0:DC, :]).then_inc(uT_ready, 1)
                dve.wait_ge(weights_in, 7 * 16)
                dve.wait_ge(pad_zeroed, 1)
                for c in range(MC):
                    dve.wait_ge(x_product, c + 1)
                    dve.tensor_copy(xp[:, c, :, PAD:], ps[:, 2 + c, :].rearrange("p (b n) -> p b n", b=BATCH))
                    dve.drain()
                    acc = xc[:, c, :].rearrange("p (b n) -> p b n", b=BATCH)
                    dve.tensor_scalar(acc, xp[:, c, :, 0:SEQ], cols[:, c, 0:1], None, ALU.mult)
                    for k in range(1, KW):
                        dve.drain()
                        last = dve.scalar_tensor_tensor(out=acc, in0=xp[:, c, :, k:k + SEQ], scalar=cols[:, c, k:k + 1],
                                                        in1=acc, op0=ALU.mult, op1=ALU.add)
                    last.then_inc(conv_done, 1)
                dve.wait_ge(a_exp, 1)
                dve.tensor_scalar(a_log[:, :, :], a_log[:, :, :], -1.0, None, ALU.mult).then_inc(a_ready, 1)
                for c in range(MC):
                    dve.wait_ge(dt_product, c + 1)
                    dve.tensor_scalar(dt[:, c, :], ps[:, 2 + c, :], cols[:, c, KW + 1:KW + 2], None, ALU.add).then_inc(biased, 1)
                for c in range(MC):
                    dve.wait_ge(log_ready, c + 1)
                    dve.scalar_tensor_tensor(out=dt[:, c, :], in0=dt[:, c, :], scalar=0.0, in1=soft[:, c, :],
                                             op0=ALU.max, op1=ALU.add).then_inc(dt_ready, 1)
                    dve.drain()
                    dve.tensor_tensor(dtx[:, c, :], dt[:, c, :], xc[:, c, :], ALU.mult)
                    dve.tensor_scalar(soft[:, c, :], xc[:, c, :], cols[:, c, KW + 2:KW + 3], None, ALU.mult).then_inc(skip_ready, 1)
                dve.drain()
                dve.sem_inc(decay_free, 2)
                dve.sem_inc(b_free, BC_SLOTS)
                with dve.Fori(0, NS // BC_SLOTS) as i:
                    for k in range(BC_SLOTS):
                        n = i * BC_SLOTS + k
                        dve.wait_ge(bc_in[k], i * 32 + 32)
                        for c in range(MC):
                            last = dve.tensor_tensor(drive[:, c, :], dtx[:, c, :], b_all[:, k, :], ALU.mult)
                        last.then_inc(b_free, 1)
                        dve.drain()
                        dve.wait_ge(c_free, n + BC_SLOTS - 1)
                        for c in range(MC):
                            dve.wait_ge(decay_ready, n * MC + c + 1)
                            for b in range(BATCH):
                                seq = slice(b * SEQ, (b + 1) * SEQ)
                                last = dve.tensor_tensor_scan(state[:, k % 2, c, seq], decay[:, k % 2, c, seq], drive[:, c, seq],
                                                              0.0, ALU.mult, ALU.add)
                            last.then_inc(state_ready, 1)
                        dve.drain()
                        dve.sem_inc(decay_free, 1)
                dve.wait_ge(out_summed, (NS + 2) * MC)
                for c in range(MC):
                    last = dve.tensor_tensor(xc[:, c, :], ps[:, 5 + c, :], z[:, c, :], ALU.mult)
                last.then_inc(gated, 1)
                dve.wait_ge(out_product, 1)
                dve.tensor_tensor(r[:, :, :], ps[:, 0:T, 0:D], s.u[:, :, :], ALU.add)
                dve.drain()
                dve.tensor_tensor(sq[:, :, :], r[:, :, :], r[:, :, :], ALU.mult)
                dve.drain()
                dve.reduce_sum(s.var[:, :], sq[:, :, :], AX.X)
                dve.drain()
                dve.tensor_scalar(s.var[:, :], s.var[:, :], 1.0 / D, EPS, ALU.mult, ALU.add).then_inc(var_ready, 1)
                dve.wait_ge(rstd_ready, 2)
                for t in range(T):
                    dve.scalar_tensor_tensor(out=r[:, t, :], in0=r[:, t, :], scalar=s.rstd[:, t:t + 1], in1=w_norm[:, :],
                                             op0=ALU.mult, op1=ALU.mult)
                dve.drain()
                dve.tensor_tensor(s.h[:, :, :], s.h[:, :, :], r[:, :, :], ALU.add)

            @block.scalar
            def _(act):
                act.wait_ge(weights_in, 7 * 16)
                for c in range(MC):
                    act.wait_ge(conv_done, c + 1)
                    act.activation(xc[:, c, :], xc[:, c, :], ACT.Silu, bias=cols[:, c, KW:KW + 1]).then_inc(xc_ready, 1)
                for c in range(MC):
                    act.wait_ge(x_product, MC + c + 1)
                    act.activation(z[:, c, :], ps[:, 5 + c, :], ACT.Silu).then_inc(xc_ready, 1)
                act.wait_ge(dbc_product, 1)
                act.copy(dbc[:, :], ps[0:R + 2 * NS, 0, :]).then_inc(dbc_ready, 1)
                act.activation(a_log[:, :, :], a_log[:, :, :], ACT.Exp).then_inc(a_exp, 1)
                for c in range(MC):
                    act.wait_ge(biased, c + 1)
                    act.activation(soft[:, c, :], dt[:, c, :], ACT.Abs)
                act.drain()
                for c in range(MC):
                    act.activation(soft[:, c, :], soft[:, c, :], ACT.Exp, scale=-1.0)
                act.drain()
                for c in range(MC):
                    act.activation(soft[:, c, :], soft[:, c, :], ACT.Ln, bias=1.0).then_inc(log_ready, 1)
                act.wait_ge(a_ready, 1)
                act.wait_ge(dt_ready, MC)
                with act.Fori(0, NS // 2) as i:
                    for k in range(2):
                        n = i * 2 + k
                        act.wait_ge(decay_free, n + 1)
                        for c in range(MC):
                            act.activation(decay[:, k, c, :], dt[:, c, :], ACT.Exp,
                                           scale=a_log[:, c, bass.ds(n, 1)]).then_inc(decay_ready, 1)


NI = 464
IK, IN_ = 116, 4
SI = 8
S_POOL = 5
ROUTED_SCALE = 2.5
S_BANKS = ((0, 1), (2, 7))


def moe_stage(nc, s, a, next_weights):
    ctx = ExitStack()
    with ctx:
        def sb(name, shape, dt=fp32):
            return ctx.enter_context(nc.sbuf_tensor(name, shape, dt))

        def sem(name):
            return s.stage_semaphore(name)

        w_router = sb("moe_w_router", [DK, DC, NE])
        e_bias = sb("moe_e_bias", [P, NE])
        sig = sb("moe_sig", [P, T, NE])
        choice = sb("moe_choice", [P, T, NE])
        top8 = sb("moe_top8", [P, T, 8])
        top8_at = sb("moe_top8_at", [P, T, 8], u32)
        expert = sb("moe_expert", [P, TOP, T])
        iota_j = sb("moe_iota_j", [P, GROUPS])
        iota_p = sb("moe_iota_p", [P, 1])
        tok_id = sb("moe_tok_id", [P, T])
        before = sb("moe_before", [P, P])
        onehot = sb("moe_onehot", [P, TOP, T, NE])
        picked = sb("moe_picked", [P, TOP // 2, T, NE])
        mask = sb("moe_mask", [P, T, NE])
        pos = sb("moe_pos", [P, T, NE])
        sig_k = sb("moe_sig_k", [P, TOP, T])
        pos_k = sb("moe_pos_k", [P, TOP, T])
        den = sb("moe_den", [P, T])
        weight = sb("moe_weight", [P, TOP, T])
        valid = sb("moe_valid", [P, TOP, T])
        slot_f = sb("moe_slot_f", [P, TOP, T])
        pos_v = sb("moe_pos_v", [P, TOP, T])
        tok_here = sb("moe_tok_here", [P, TOP, T, CAP])
        read_at = sb("moe_read_at", [P, TOP, T], u32)
        count = sb("moe_count", [P, 1])
        active = sb("moe_active", [P, 2])
        rank = sb("moe_rank", [P, 2])
        chosen = sb("moe_chosen", [P, 2, GROUPS])
        group_no = sb("moe_group_no", [P, 2])
        total = sb("moe_total", [1, 1])
        pairs = sb("moe_pairs", [1, GROUPS // 2])
        list_e = sb("moe_list_e", [1, GROUPS], u32)
        list_g = sb("moe_list_g", [1, GROUPS], u32)
        n_pairs_f = sb("moe_n_pairs_f", [1, 1])
        n_pairs = sb("moe_n_pairs", [1, 1], u32)
        tok_at = sb("moe_tok_at", [SLOTS, GROUPS + 1], u32)
        w_sgu = sb("moe_w_sgu", [DK, DC, 2, SI * IK])
        w_sd = sb("moe_w_sd", [IK, SI, D])
        s_act = sb("moe_s_act", [IK, 2, NT])
        s_hidT = sb("moe_s_hidT", [IK, SI, NT])
        acc = sb("moe_acc", [P, T, D])
        y_dram = s.y_of_slot
        u_dram = nc.dram_tensor("u_rows", [NT, D], fp32).ap()
        ps = s.ps

        weights_in = sem("moe_weights_in")
        shared_in = sem("moe_shared_in")
        var_ready, rstd_ready = sem("moe_var_ready"), sem("moe_rstd_ready")
        consts = sem("moe_consts")
        u_ready = sem("moe_u_ready")
        u_stored = sem("moe_u_stored")
        u_transposed = sem("moe_u_transposed")
        uT_ready = sem("moe_uT_ready")
        logits_ready = sem("moe_logits_ready")
        sig_ready = sem("moe_sig_ready")
        mask_ready = sem("moe_mask_ready")
        pos_product = sem("moe_pos_product")
        active_ready = sem("moe_active_ready")
        rank_product = sem("moe_rank_product")
        chosen_ready = sem("moe_chosen_ready")
        list_product = sem("moe_list_product")
        here_ready = sem("moe_here_ready")
        tok_product = sem("moe_tok_product")
        s_product = sem("moe_s_product")
        s_silu = sem("moe_s_silu")
        s_ready_g = sem("moe_s_ready_g")
        s_ready_v = sem("moe_s_ready_v")
        list_ready = sem("moe_list_ready")
        tok_at_ready = sem("moe_tok_at_ready")
        read_at_ready = sem("moe_read_at_ready")
        s_out = sem("moe_s_out")

        w_gu = [sb(f"moe_w_gu{k}", [DK, DC, 2 * NI]) for k in range(2)]
        sizes = (IN_ * D,) * 2 + (IN_ * SLOTS,) * 2
        lots = [next_weights.spare[:, sum(sizes[:i]):sum(sizes[:i + 1])] for i in range(len(sizes))]
        w_d = [lot[0:IK, :].rearrange("p (m d) -> p m d", m=IN_) for lot in lots[0:2]]
        act_g = [lot[0:IK, :].rearrange("p (m n) -> p m n", m=IN_) for lot in lots[2:4]]
        hidT = [sb(f"moe_hidT{k}", [IK, IN_, SLOTS]) for k in range(2)]
        row_at = [sb(f"moe_row_at{k}", [SLOTS, 1], u32) for k in range(2)]
        rows = [sb(f"moe_rows{k}", [SLOTS, D]) for k in range(2)]
        rowsT = [sb(f"moe_rowsT{k}", [DK, DC, SLOTS]) for k in range(2)]
        y = [sb(f"moe_y{k}", [SLOTS, D]) for k in range(2)]
        gu_in = [sem(f"moe_gu_in{k}") for k in range(2)]
        d_in = [sem(f"moe_d_in{k}") for k in range(2)]
        row_at_set = [sem(f"moe_row_at_set{k}") for k in range(2)]
        rows_in = [sem(f"moe_rows_in{k}") for k in range(2)]
        rows_transposed = [sem(f"moe_rows_transposed{k}") for k in range(2)]
        rowsT_ready = [sem(f"moe_rowsT_ready{k}") for k in range(2)]
        gu_product = [sem(f"moe_gu_product{k}") for k in range(2)]
        silu_ready = [sem(f"moe_silu_ready{k}") for k in range(2)]
        hid_ready = [sem(f"moe_hid_ready{k}") for k in range(2)]
        y_product = [sem(f"moe_y_product{k}") for k in range(2)]
        y_ready = [sem(f"moe_y_ready{k}") for k in range(2)]
        y_stored = [sem(f"moe_y_stored{k}") for k in range(2)]
        all_stored = sem("moe_all_stored")
        row_at_seen = sem("moe_row_at_seen")
        back = tok_here
        back_in = [sem(f"moe_back_in{k}") for k in range(TOP)]

        def s_used(eng, j):
            if j < S_POOL:
                eng.wait_ge(s_ready_g, j + 1)
            else:
                eng.wait_ge(s_ready_v, j + 1 - S_POOL)

        with nc.Block() as block:
            @block.sync
            def _(sp):
                sp.dma_start(w_router[:, :, :], a["moe_w_router"].rearrange("(c p) e -> p c e", p=DK)).then_inc(weights_in, 16)
                sp.dma_start(e_bias[:, :], a["moe_e_bias"].broadcast_to((P, NE))).then_inc(weights_in, 16)
                for k in range(2):
                    sp.dma_start(w_sgu[:, :, k, :], a["moe_w_sgu"][k].rearrange("(c p) e -> p c e", p=DK)).then_inc(shared_in, 16)
                sp.dma_start(w_sd[:, :, :], a["moe_w_sd"].rearrange("(c p) e -> p c e", p=IK)).then_inc(shared_in, 16)
                sp.wait_ge(u_ready, 1)
                sp.dma_start(u_dram.rearrange("(t p) d -> p t d", p=P), s.u[:, :, :]).then_inc(u_stored, 16)
                next_weights.load(sp, a)
                sp.wait_ge(list_ready, 1)
                with sp.Fori(0, sp.value_load(n_pairs[0:1, 0:1], min_val=1, max_val=GROUPS // 2)) as i:
                    for k in range(2):
                        e = sp.value_load(list_e[0:1, bass.ds(2 * i + k, 1)], min_val=0, max_val=NE - 1)
                        sp.wait_ge(gu_product[k], i + 1)
                        sp.dma_start(w_gu[k][:, :, :], a["moe_w_gu"][bass.ds(e, 1), :, :].rearrange("o (c p) f -> p (o c) f", p=DK)).then_inc(gu_in[k], 16)
                        sp.wait_ge(y_product[k], i + 1)
                        sp.dma_start(w_d[k][:, :, :], a["moe_w_d"][bass.ds(e, 1), :, :].rearrange("o (c p) f -> p (o c) f", p=IK)).then_inc(d_in[k], 16)


            @block.gpsimd
            def _(pool):
                pool.memset(before[:, :], 1.0).then_inc(consts, 1)
                pool.iota(iota_j[:, :], [[1, GROUPS]], base=0, channel_multiplier=0, allow_small_or_imprecise_dtypes=True).then_inc(consts, 1)
                pool.iota(iota_p[:, :], [[0, 1]], base=0, channel_multiplier=1, allow_small_or_imprecise_dtypes=True).then_inc(consts, 1)
                pool.iota(tok_id[:, :], [[P, T]], base=0, channel_multiplier=1, allow_small_or_imprecise_dtypes=True).then_inc(consts, 1)
                pool.iota(group_no[:, :], [[1, 2]], base=-SPARE, channel_multiplier=2, allow_small_or_imprecise_dtypes=True).then_inc(consts, 1)
                pool.wait_ge(consts, 5)
                pool.affine_select(out=before[:, :], in_=before[:, :], compare_op=ALU.is_gt, fill=0.0, base=0,
                                   pattern=[[1, P]], channel_multiplier=-1).then_inc(consts, 1)
                ln_pool(pool, s, 0, var_ready, rstd_ready)
                for j in range(S_POOL):
                    pool.wait_ge(s_silu, j + 1)
                    pool.tensor_tensor(s_hidT[:, j, :], s_act[:, j % 2, :], s_hidT[:, j, :], ALU.mult).then_inc(s_ready_g, 1)
                    pool.wait_ge(s_ready_g, j + 1)
                pool.wait_ge(u_stored, 16)
                pool.wait_ge(list_ready, 1)
                pool.wait_ge(tok_at_ready, 1)
                with pool.Fori(0, pool.value_load(n_pairs[0:1, 0:1], min_val=1, max_val=GROUPS // 2)) as i:
                    for k in range(2):
                        g = pool.value_load(list_g[0:1, bass.ds(2 * i + k, 1)], min_val=0, max_val=GROUPS)
                        pool.wait_ge(rows_transposed[k], i + 1)
                        pool.tensor_copy(row_at[k][:, :], tok_at[:, bass.ds(g, 1)]).then_inc(row_at_set[k], 1)
                        pool.wait_ge(row_at_set[k], i + 1)
                        pool.sem_inc(row_at_seen, 1)
                        pool.indirect_dma_start(out=rows[k][:, :], out_offset=None, in_=u_dram,
                                                in_offset=bass.IndirectOffsetOnAxis(ap=row_at[k][:, 0:1], axis=0),
                                                bounds_check=NT - 1, oob_is_err=False).then_inc(rows_in[k], 16)
                pool.wait_ge(read_at_ready, 1)
                pool.wait_ge(all_stored, 2)
                for k in range(TOP):
                    for t in range(T):
                        pool.indirect_dma_start(out=back[:, k, t, :], out_offset=None, in_=y_dram,
                                                in_offset=bass.IndirectOffsetOnAxis(ap=read_at[:, k, t:t + 1], axis=0),
                                                bounds_check=GROUPS * SLOTS - 1, oob_is_err=False).then_inc(back_in[k], 16)

            @block.tensor
            def _(pe):
                for k in range(2):
                    pe.sem_inc(gu_product[k], 1)
                    pe.sem_inc(y_product[k], 1)
                    pe.sem_inc(rows_transposed[k], 1)
                pe.wait_ge(u_ready, 1)
                transpose_u(pe, s).then_inc(u_transposed, 1)
                pe.wait_ge(uT_ready, 1)
                pe.wait_ge(weights_in, 32)
                for t in range(T):
                    for c in range(DC):
                        last = pe.matmul(ps[:, 2, t * NE:(t + 1) * NE], lhsT=s.uT[:, c, t * P:(t + 1) * P],
                                         rhs=w_router[:, c, :], start=(c == 0), stop=(c == DC - 1))
                last.then_inc(logits_ready, 1)

                def shared_up(j):
                    if j == 1:
                        pe.wait_ge(sig_ready, 1)
                    if j >= 2:
                        pe.wait_ge(s_silu, j - 1)
                    for k in range(2):
                        for c in range(DC):
                            last = pe.matmul(ps[0:IK, S_BANKS[j % 2][k], :], lhsT=w_sgu[:, c, k, j * IK:(j + 1) * IK],
                                             rhs=s.uT[:, c, :], start=(c == 0), stop=(c == DC - 1))
                    last.then_inc(s_product, 1)

                pe.wait_ge(shared_in, 48)
                for j in range(3):
                    shared_up(j)
                pe.wait_ge(mask_ready, 1)
                pe.wait_ge(consts, 6)
                for t in range(T):
                    for j in range(t + 1):
                        pe.matmul(ps[:, 3, t * NE:(t + 1) * NE], lhsT=(before if j == t else s.ones)[:, :],
                                  rhs=mask[:, j, :], start=(j == 0), stop=(j == t))
                for t in range(T):
                    last = pe.matmul(ps[:, 4, 0:1], lhsT=mask[:, t, :], rhs=s.ones[:, 0:1], start=(t == 0), stop=(t == T - 1))
                last.then_inc(pos_product, 1)
                for j in range(3, 5):
                    shared_up(j)
                pe.wait_ge(active_ready, 1)
                pe.matmul(ps[:, 5, 0:1], lhsT=before[:, :], rhs=active[:, 0:1], start=True, stop=True)
                pe.matmul(ps[:, 5, 1:2], lhsT=s.ones[:, :], rhs=active[:, 0:1], start=True, stop=False)
                pe.matmul(ps[:, 5, 1:2], lhsT=before[:, :], rhs=active[:, 1:2], start=False, stop=True)
                for k in range(2):
                    last = pe.matmul(ps[0:1, 5, 2:3], lhsT=s.ones[:, 0:1], rhs=active[:, k:k + 1], start=(k == 0), stop=(k == 1))
                last.then_inc(rank_product, 1)
                pe.wait_ge(chosen_ready, 1)
                for at, col in ((0, [iota_p[:, 0:1]] * 2), (GROUPS, [group_no[:, 0:1], group_no[:, 1:2]])):
                    for k in range(2):
                        last = pe.matmul(ps[0:1, 6, at:at + GROUPS], lhsT=col[k], rhs=chosen[:, k, :], start=(k == 0), stop=(k == 1))
                last.then_inc(list_product, 1)
                for k in range(TOP):
                    pe.wait_ge(here_ready, k + 1)
                    for t in range(T):
                        for half in range(2):
                            last = pe.matmul(ps[0:SLOTS, 3 + half, 0:NE], lhsT=tok_here[:, k, t, half * SLOTS:(half + 1) * SLOTS],
                                             rhs=onehot[:, k, t, :], start=(k == 0 and t == 0), stop=(k == TOP - 1 and t == T - 1))
                last.then_inc(tok_product, 1)
                pe.wait_ge(tok_at_ready, 1)
                with pe.Fori(0, pe.value_load(n_pairs[0:1, 0:1], min_val=1, max_val=GROUPS // 2)) as i:
                    for k in range(2):
                        pe.wait_ge(rows_in[k], i * 16 + 16)
                        for c in range(DC):
                            last = pe.transpose(ps[0:DK, 7 * k, c * SLOTS:(c + 1) * SLOTS], rows[k][:, c * DK:(c + 1) * DK],
                                                s.ident[0:SLOTS, 0:SLOTS])
                        last.then_inc(rows_transposed[k], 1)
                    for k in range(2):
                        pe.wait_ge(rowsT_ready[k], i + 1)
                        pe.wait_ge(gu_in[k], i * 16 + 16)
                        for half in range(2):
                            for m in range(IN_):
                                at = half * NI + m * IK
                                for c in range(DC):
                                    last = pe.matmul(ps[0:IK, 1 + 2 * k + half, m * SLOTS:(m + 1) * SLOTS],
                                                     lhsT=w_gu[k][:, c, at:at + IK], rhs=rowsT[k][:, c, :],
                                                     start=(c == 0), stop=(c == DC - 1))
                        last.then_inc(gu_product[k], 1)
                    for k in range(2):
                        pe.wait_ge(hid_ready[k], i + 2)
                        pe.wait_ge(d_in[k], i * 16 + 16)
                        pe.wait_ge(y_ready[k], i + 1)
                        for m in range(IN_):
                            last = pe.matmul(ps[0:SLOTS, 5 + k, 0:D], lhsT=hidT[k][:, m, :], rhs=w_d[k][:, m, :],
                                             start=(m == 0), stop=(m == IN_ - 1))
                        last.then_inc(y_product[k], 1)
                for j in range(S_POOL, SI):
                    shared_up(j)
                s_used(pe, SI - 1)
                for t in range(T):
                    for j in range(SI):
                        last = pe.matmul(ps[:, t, 0:D], lhsT=s_hidT[:, j, t * P:(t + 1) * P], rhs=w_sd[:, j, :],
                                         start=(j == 0), stop=(j == SI - 1))
                last.then_inc(s_out, 1)

            @block.scalar
            def _(act):
                act.wait_ge(logits_ready, 1)
                act.activation(sig[:, :, :], ps[:, 2, :].rearrange("p (t e) -> p t e", t=T), ACT.Sigmoid).then_inc(sig_ready, 1)

                def s_silu_of(j):
                    act.wait_ge(s_product, j + 1)
                    if j >= 2:
                        s_used(act, j - 2)
                    act.activation(s_act[:, j % 2, :], ps[0:IK, S_BANKS[j % 2][0], :], ACT.Silu)
                    act.copy(s_hidT[:, j, :], ps[0:IK, S_BANKS[j % 2][1], :]).then_inc(s_silu, 1)

                for j in range(S_POOL):
                    s_silu_of(j)
                act.wait_ge(list_ready, 1)
                for k in range(2):
                    act.sem_inc(y_ready[k], 1)
                    act.sem_inc(y_stored[k], 16)
                n = act.value_load(n_pairs[0:1, 0:1], min_val=1, max_val=GROUPS // 2)
                with act.Fori(0, n) as i:
                    for k in range(2):
                        act.wait_ge(gu_product[k], i + 2)
                        act.wait_ge(hid_ready[k], i + 1)
                        act.activation(act_g[k][:, :, :], ps[0:IK, 1 + 2 * k, 0:IN_ * SLOTS].rearrange("p (m n) -> p m n", m=IN_),
                                       ACT.Silu).then_inc(silu_ready[k], 1)
                    for k in range(2):
                        g = act.value_load(list_g[0:1, bass.ds(2 * i + k, 1)], min_val=0, max_val=GROUPS)
                        act.wait_ge(y_stored[k], i * 16 + 16)
                        act.wait_ge(y_product[k], i + 2)
                        act.copy(y[k][:, :], ps[0:SLOTS, 5 + k, 0:D]).then_inc(y_ready[k], 1)
                        act.wait_ge(y_ready[k], i + 2)
                        act.dma_start(y_dram.rearrange("(g c) d -> g c d", c=SLOTS)[bass.ds(g, 1), :, :].rearrange("o c d -> (o c) d"),
                                      y[k][:, :]).then_inc(y_stored[k], 16)
                for k in range(2):
                    act.wait_ge(y_stored[k], n * 16 + 16)
                    act.sem_inc(all_stored, 1)
                for j in range(S_POOL, SI):
                    s_silu_of(j)
                next_weights.split_hi(act)

            @block.vector
            def _(dve):
                def pick(out, table):
                    for lot in range(2):
                        ks = slice(lot * TOP // 2, (lot + 1) * TOP // 2)
                        for k in range(TOP // 2):
                            dve.tensor_tensor(picked[:, k, :, :], onehot[:, ks.start + k, :, :], table[:, :, :], ALU.mult)
                        dve.drain()
                        dve.reduce_sum(out[:, ks, :], picked[:, :, :, :], AX.X)
                        dve.drain()

                ln_vector(dve, s, s.u, s.h, 0, var_ready, rstd_ready).then_inc(u_ready, 1)
                dve.wait_ge(u_transposed, 1)
                dve.tensor_copy(s.uT[:, :, :], ps[0:DK, 0:DC, :]).then_inc(uT_ready, 1)
                dve.wait_ge(weights_in, 32)
                dve.wait_ge(sig_ready, 1)
                dve.tensor_tensor(choice[:, :, :], sig[:, :, :], e_bias[:, :].unsqueeze(1).broadcast_to((P, T, NE)), ALU.add)
                dve.drain()
                for t in range(T):
                    dve.max(top8[:, t, :], choice[:, t, :])
                dve.drain()
                for t in range(T):
                    dve.max_index(top8_at[:, t, :], top8[:, t, :], choice[:, t, :])
                dve.drain()
                dve.tensor_copy(expert[:, :, :], top8_at[:, :, 0:TOP].rearrange("p t k -> p k t"))
                dve.drain()
                dve.wait_ge(consts, 6)
                for k in range(TOP):
                    dve.tensor_tensor(onehot[:, k, :, :], iota_j[:, 0:NE].unsqueeze(1).broadcast_to((P, T, NE)),
                                      expert[:, k, :].unsqueeze(2).broadcast_to((P, T, NE)), ALU.is_equal)
                dve.drain()
                dve.reduce_sum(mask[:, :, :], onehot[:, :, :, :].rearrange("p k t e -> p t e k"), AX.X).then_inc(mask_ready, 1)
                dve.wait_ge(pos_product, 1)
                dve.tensor_copy(pos[:, :, :], ps[:, 3, :].rearrange("p (t e) -> p t e", t=T))
                dve.tensor_copy(count[:, :], ps[:, 4, 0:1])
                dve.drain()
                dve.tensor_scalar(active[:, 0:1], count[:, :], 0.0, None, ALU.is_gt)
                dve.tensor_scalar(active[:, 1:2], count[:, :], float(SLOTS), None, ALU.is_gt).then_inc(active_ready, 1)
                pick(pos_k, pos)
                dve.wait_ge(rank_product, 1)
                dve.tensor_copy(rank[:, :], ps[:, 5, 0:2])
                dve.tensor_copy(total[:, :], ps[0:1, 5, 2:3])
                dve.drain()
                for k in range(2):
                    last = dve.tensor_scalar(chosen[:, k, :], iota_j[:, :], rank[:, k:k + 1], active[:, k:k + 1], ALU.is_equal, ALU.mult)
                last.then_inc(chosen_ready, 1)
                for k in range(TOP):
                    for t in range(T):
                        last = dve.tensor_scalar(tok_here[:, k, t, :], iota_j[:, 0:CAP], pos_k[:, k, t:t + 1], tok_id[:, t:t + 1],
                                                 ALU.is_equal, ALU.mult)
                    last.then_inc(here_ready, 1)
                dve.tensor_scalar(pairs[:, :], iota_j[0:1, ::2], total[:, :], None, ALU.is_lt)
                dve.drain()
                dve.reduce_sum(n_pairs_f[:, :], pairs[:, :], AX.X)
                dve.drain()
                dve.tensor_copy(n_pairs[:, :], n_pairs_f[:, :])
                dve.wait_ge(list_product, 1)
                dve.tensor_copy(list_e[:, :], ps[0:1, 6, 0:GROUPS])
                dve.tensor_scalar(list_g[:, :], ps[0:1, 6, GROUPS:2 * GROUPS], float(SPARE), None, ALU.add)
                dve.drain()
                dve.sem_inc(list_ready, 1)
                dve.memset(tok_at[:, SPARE:SPARE + 1], 0)
                dve.wait_ge(tok_product, 1)
                for half in range(2):
                    dve.tensor_copy(tok_at[:, half:GROUPS:2], ps[0:SLOTS, 3 + half, 0:NE])
                dve.drain()
                dve.sem_inc(tok_at_ready, 1)
                dve.tensor_scalar(valid[:, :, :], pos_k[:, :, :], float(CAP), None, ALU.is_lt)
                dve.tensor_scalar(slot_f[:, :, :], expert[:, :, :], float(CAP), None, ALU.mult)
                dve.drain()
                dve.tensor_tensor(pos_v[:, :, :], pos_k[:, :, :], valid[:, :, :], ALU.mult)
                dve.drain()
                dve.tensor_tensor(read_at[:, :, :], pos_v[:, :, :], slot_f[:, :, :], ALU.add).then_inc(read_at_ready, 1)
                for k in range(2):
                    dve.sem_inc(hid_ready[k], 1)
                with dve.Fori(0, dve.value_load(n_pairs[0:1, 0:1], min_val=1, max_val=GROUPS // 2)) as i:
                    for k in range(2):
                        dve.wait_ge(rows_transposed[k], i + 2)
                        dve.tensor_copy(rowsT[k][:, :, :], ps[0:DK, 7 * k, 0:DC * SLOTS].rearrange("p (c n) -> p c n", c=DC)).then_inc(rowsT_ready[k], 1)
                    for k in range(2):
                        dve.wait_ge(silu_ready[k], i + 1)
                        dve.tensor_tensor(hidT[k][:, :, :], act_g[k][:, :, :],
                                          ps[0:IK, 2 + 2 * k, 0:IN_ * SLOTS].rearrange("p (m n) -> p m n", m=IN_), ALU.mult).then_inc(hid_ready[k], 1)
                for j in range(S_POOL, SI):
                    dve.wait_ge(s_silu, j + 1)
                    dve.tensor_tensor(s_hidT[:, j, :], s_act[:, j % 2, :], s_hidT[:, j, :], ALU.mult).then_inc(s_ready_v, 1)
                pick(sig_k, sig)
                dve.reduce_sum(den[:, :], sig_k[:, :, :].rearrange("p k t -> p t k"), AX.X)
                dve.drain()
                dve.tensor_scalar(den[:, :], den[:, :], 1e-20, None, ALU.add)
                dve.drain()
                dve.reciprocal(den[:, :], den[:, :])
                dve.drain()
                dve.tensor_tensor(weight[:, :, :], sig_k[:, :, :], den[:, :].unsqueeze(1).broadcast_to((P, TOP, T)), ALU.mult)
                dve.drain()
                dve.scalar_tensor_tensor(out=weight[:, :, :], in0=weight[:, :, :], scalar=ROUTED_SCALE, in1=valid[:, :, :],
                                         op0=ALU.mult, op1=ALU.mult)
                dve.drain()
                for k in range(TOP):
                    if k == TOP - 2:
                        next_weights.split_lo(dve)
                    dve.wait_ge(back_in[k], T * 16)
                    for t in range(T):
                        dve.scalar_tensor_tensor(out=acc[:, t, :], in0=back[:, k, t, :], scalar=weight[:, k, t:t + 1],
                                                 in1=(s.h if k == 0 else acc)[:, t, :], op0=ALU.mult, op1=ALU.add)
                    dve.drain()
                dve.wait_ge(s_out, 1)
                dve.tensor_tensor(s.h[:, :, :], acc[:, :, :], ps[:, 0:T, 0:D], ALU.add)


EH, EY = 12, 64
EC = EH * EY // P
EM = 768
DJ = 3
EMC = EM // P
STEPS = 12
ALPHA = 0.1
BETA = 0.125
SCALE = (1.0, BETA, 1.0)
PAIRS = EC * BATCH
SLOTS_W = PAIRS + 2
OUT_Q, OUT_K = 6, 7
Y_BANKS = ((6, 7, 2), (3, 4, 5))
ITEMS_OF = {-1: [("q", 0), ("k", 0), ("q", 1), ("k", 1), ("q_tok", 0), ("mem", 0), ("mem", 1), ("mem", 2)]}
for _s in range(SLOTS_W):
    _c = _s // 2
    ITEMS_OF[_s] = [("q_tok", _c + 1), ("k", _c + 2)] if _s % 2 else [("k_tok", _c), ("q", _c + 2)]
    ITEMS_OF[_s] = [_i for _i in ITEMS_OF[_s] if _i[1] < EC]
for _c, _s in ((3, 10), (4, PAIRS), (5, PAIRS)):
    ITEMS_OF[_s].append(("mem", _c))
ITEMS = [_i for _s in range(-1, SLOTS_W) for _i in ITEMS_OF[_s]]
NITEMS = len(ITEMS)
ITEM_BANK = [0, 1, OUT_Q, OUT_K] + [_i % 2 for _i in range(4, NITEMS)]


def held_before(p):
    return max(i for i in range(p) if ITEM_BANK[i] == ITEM_BANK[p])


class EnergyWeights:

    def __init__(self, nc, ctx):
        self.big = ctx.enter_context(nc.sbuf_tensor("en_big", [P, 3 * EC * NT], fp32))
        self.wT = self.big[:, 0:DJ * 3 * EM].rearrange("p (j k e) -> p j k e", j=DJ, k=3)
        self.spare = self.big[:, DJ * 3 * EM:]
        self.wr = ctx.enter_context(nc.sbuf_tensor("en_wr", [P, 3, EMC, D], fp32))
        self.ln = ctx.enter_context(nc.sbuf_tensor("en_ln", [P, DJ, 2], fp32))
        self.w_s = ctx.enter_context(nc.sbuf_tensor("en_w_s", [P, DJ * 3 * EM], f32r))
        self.split = self.w_s[:, :].rearrange("p (j k e) -> p j k e", j=DJ, k=3)
        self.hi_split = nc.alloc_semaphore("en_hi_split")
        self.loaded = nc.alloc_semaphore("en_weights_in")
        self.wr_loaded = nc.alloc_semaphore("en_wr_in")

    def load(self, sp, a):
        rows = a["en_wT"].rearrange("k p e -> p k e")
        for at, j, lo, hi in ((slice(0, P), 0, 0, P), (slice(0, EY), 1, P, D), (slice(EY, P), 1, 0, EY), (slice(0, P), 2, EY, D)):
            sp.dma_start(self.wT[at, j, :, :], rows[lo:hi, :, :]).then_inc(self.loaded, 16)
            sp.dma_start(self.ln[at, j, :], a["en_ln"][lo:hi, :]).then_inc(self.loaded, 16)
        for k in range(3):
            sp.dma_start(self.wr[:, k, :, :], a["en_w"][k].rearrange("(c p) d -> p c d", p=P)).then_inc(self.wr_loaded, 16)

    def split_hi(self, act):
        act.wait_ge(self.loaded, 8 * 16)
        for j in (2, 1, 0):
            for k in range(3):
                last = act.mul(self.split[:, j, k, :], self.wT[:, j, k, :], SCALE[k])
            last.then_inc(self.hi_split, 1)

    def split_lo(self, dve):
        for i, (at, j) in enumerate(((slice(0, P), 2), (slice(EY, P), 1))):
            dve.wait_ge(self.hi_split, i + 1)
            for k in range(3):
                dve.scalar_tensor_tensor(out=self.split[at, j, k, :], in0=self.wT[at, j, k, :], scalar=SCALE[k],
                                         in1=self.split[at, j, k, :].bitcast(fp32), op0=ALU.mult, op1=ALU.subtract)


def energy_stage(nc, s, a, weights):
    ctx = ExitStack()
    with ctx:
        def sb(name, shape, dt=fp32):
            return ctx.enter_context(nc.sbuf_tensor(name, shape, dt))

        def sem(name):
            return s.stage_semaphore(name)

        g_hi = sb("en_g_hi", [P, DJ, NT], f32r)
        g_lo = sb("en_g_lo", [P, 2, NT], f32r)
        g = sb("en_g", [P, 2, NT])
        big, w_s, wr, ln = weights.big, weights.split, weights.wr, weights.ln
        x = s.u
        y = sb("en_y", [P, T, 2, D])
        q_c = sb("en_q", [P, 2, NT])
        k_c = sb("en_k", [P, 2, NT])
        q_s = sb("en_q_s", [P, 2, 2, NT], f32r)
        k_hi = sb("en_k_hi", [P, 2, 2, NT], f32r)
        k_lo = sb("en_k_lo", [P, 2, 2, NT], f32r)
        qn = sb("en_qn", [P, 3, T, P])
        kn = sb("en_kn", [P, 3, T, P])
        dqT, dkT, memT = (big[:, i * EC * NT:(i + 1) * EC * NT].rearrange("p (c n) -> p c n", c=EC) for i in range(3))
        neg_max = sb("en_neg_max", [P, 6, TB])
        row_sum = sb("en_row_sum", [P, 6, TB])
        prob = [sb(f"en_prob{i}", [P, TB, SEQ]) for i in range(6)]
        probT = [sb(f"en_probT{i}", [P, TB, SEQ]) for i in range(4)]
        ps = s.ps
        HI = (slice(0, EY), slice(EY, P))
        LO = (slice(EY, P), slice(0, EY))

        wr_in = weights.wr_loaded
        s.stage_semaphores += [weights.loaded, weights.wr_loaded, weights.hi_split]
        k_lo_zeroed = sem("en_k_lo_zeroed")
        var_ready, rstd_ready = sem("en_var_ready"), sem("en_rstd_ready")
        rows_var_ready, rows_rstd_ready = sem("en_rows_var_ready"), sem("en_rows_rstd_ready")
        y_ready = sem("en_y_ready")
        y_transposed = sem("en_y_transposed")
        g_ready = sem("en_g_ready")
        g_hi_ready = sem("en_g_hi_ready")
        g_lo_ready = sem("en_g_lo_ready")
        item = sem("en_item")
        item_out = sem("en_item_out")
        q_hi_ready, k_hi_ready = sem("en_q_hi_ready"), sem("en_k_hi_ready")
        q_split, k_split = sem("en_q_split"), sem("en_k_split")
        scores = sem("en_scores")
        max_ready = sem("en_max_ready")
        exp_ready = sem("en_exp_ready")
        prob_ready = sem("en_prob_ready")
        transposed = sem("en_transposed")
        probT_ready = sem("en_probT_ready")
        pair_done = sem("en_pair_done")
        dq_ready, dk_ready = sem("en_dq_ready"), sem("en_dk_ready")
        grad_product = sem("en_grad_product")

        def half_of(h):
            return slice(h * NT // 2, (h + 1) * NT // 2)

        with nc.Block() as block:
            @block.gpsimd
            def _(pool):
                for r in range(2):
                    pool.memset(k_lo[LO[r], :, r, :].bitcast(fp32), 0.0).then_inc(k_lo_zeroed, 1)
                    pool.wait_ge(k_lo_zeroed, r + 1)

                def rstd(n):
                    for t in range(T):
                        pool.wait_ge(var_ready, n * T + t + 1)
                        pool.tensor_tensor(s.rstd[:, t:t + 1], s.var[:, t:t + 1], s.neghalf[:, 0:1], ALU.pow).then_inc(rstd_ready, 1)
                        pool.wait_ge(rstd_ready, n * T + t + 1)

                for n in range(2):
                    ln_pool(pool, s, n, rows_var_ready, rows_rstd_ready)
                    pool.wait_ge(rows_rstd_ready, n + 1)
                with pool.Fori(0, STEPS) as n:
                    for c in range(EC):
                        pool.wait_ge(q_hi_ready, n * EC + c + 1)
                        for r in range(2):
                            pool.tensor_tensor(q_s[LO[r], c % 2, r, :], q_c[HI[r], c % 2, :],
                                               q_s[HI[r], c % 2, r, :].bitcast(fp32), ALU.subtract).then_inc(q_split, 1)
                            pool.wait_ge(q_split, 2 * EC * n + 2 * c + r + 1)
                        if c == 0:
                            continue
                        pool.wait_ge(k_hi_ready, n * EC + c + 1)
                        for r in range(2):
                            pool.tensor_tensor(k_lo[HI[r], c % 2, r, :], k_c[HI[r], c % 2, :],
                                               k_hi[HI[r], c % 2, r, :].bitcast(fp32), ALU.subtract).then_inc(k_split, 1)
                            pool.wait_ge(k_split, 2 * EC * n + 2 * c + r + 1)
                    rstd(n)

            @block.tensor
            def _(pe):
                pe.wait_ge(k_lo_zeroed, 2)
                pe.wait_ge(wr_in, 3 * 16)

                def transpose_y(h, n):
                    pe.wait_ge(y_ready, n * T + (h + 1) * T // 2)
                    for t in range(T // 2):
                        for j in range(DJ):
                            last = pe.transpose(ps[:, Y_BANKS[h][j], t * P:(t + 1) * P],
                                                y[:, h * T // 2 + t, :, :].rearrange("p k d -> p (k d)")[:, j * P:(j + 1) * P], s.ident[:, :])
                    last.then_inc(y_transposed, 1)

                transpose_y(0, 0)
                with pe.Fori(0, STEPS) as n:
                    def product(p, terms, h=None):
                        kind, c = ITEMS[p]
                        at = slice(0, NT) if h is None else half_of(h)
                        for j, part in terms:
                            if p == 0 and part is g_hi:
                                pe.wait_ge(g_hi_ready, n * 2 * DJ + h * DJ + j + 1)
                            if p == 0 and part is g_lo:
                                pe.wait_ge(g_lo_ready, n * 4 + 2 * h + 2 - j)
                            last = pe.matmul(ps[:, ITEM_BANK[p], at], lhsT=w_s[:, j, ("q", "k", "mem").index(kind), c * P:(c + 1) * P],
                                             rhs=part[:, j, at], start=(part is g_hi and j == 0), stop=(part is g_lo and j == 0))
                        return last

                    hi_terms = tuple((j, g_hi) for j in range(DJ))
                    lo_terms = ((1, g_lo), (0, g_lo))

                    def make(p):
                        kind, c = ITEMS[p]
                        pe.wait_ge(item_out, n * NITEMS + held_before(p) + 1)
                        bank = ps[:, ITEM_BANK[p], :]
                        if kind in ("q_tok", "k_tok"):
                            of = ITEMS.index((kind[0], c))
                            if of > held_before(p):
                                pe.wait_ge(item_out, n * NITEMS + of + 1)
                            src = (q_c if kind == "q_tok" else k_c)[:, c % 2, :]
                            for t in range(T):
                                last = pe.transpose(bank[:, t * P:(t + 1) * P], src[:, t * P:(t + 1) * P], s.ident[:, :])
                        else:
                            last = product(p, hi_terms + lo_terms)
                        last.then_inc(item, 1)

                    def score(w, r):
                        c, b = w // BATCH, w % BATCH
                        if b == 0 and r == 0:
                            pe.wait_ge(q_split, 2 * EC * n + 2 * c + 2)
                            pe.wait_ge(k_split, 2 * EC * n + 2 * c + 2)
                        if w > 0:
                            pe.wait_ge(exp_ready, n * 2 * PAIRS + 2 * w + r - 1)
                        for i in range(TB):
                            lo = b * SEQ + i * P
                            for part in (k_hi, k_lo):
                                last = pe.matmul(ps[:, 2 + r, i * SEQ:(i + 1) * SEQ], lhsT=q_s[:, c % 2, r, lo:lo + P],
                                                 rhs=part[:, c % 2, r, b * SEQ:(b + 1) * SEQ], start=(part is k_hi), stop=(part is k_lo))
                        last.then_inc(scores, 1)

                    def transpose(w, r):
                        if w > 0:
                            pe.wait_ge(probT_ready, n * 2 * PAIRS + 2 * w + r - 1)
                        pe.wait_ge(prob_ready, n * 2 * PAIRS + 2 * w + r + 1)
                        for i in range(TB):
                            for j in range(TB):
                                last = pe.transpose(ps[:, 4 + r, j * SEQ + i * P:j * SEQ + (i + 1) * P],
                                                    prob[(2 * w + r) % 6][:, i, j * P:(j + 1) * P], s.ident[:, :])
                        last.then_inc(transposed, 1)

                    def combine(w):
                        c, b = w // BATCH, w % BATCH
                        if b == 0:
                            pe.wait_ge(item_out, n * NITEMS + ITEMS.index(("k_tok", c)) + 1)
                            if c >= 1:
                                pe.wait_ge(dq_ready, n * EC + c)
                                pe.wait_ge(dk_ready, n * EC + c)
                        seq = slice(b * SEQ, (b + 1) * SEQ)
                        for i in range(TB):
                            for r in range(2):
                                pe.matmul(ps[HI[r], OUT_K, seq], lhsT=qn[:, c % 3, b * TB + i, HI[r]],
                                          rhs=prob[(2 * w + r) % 6][:, i, :], start=(i == 0), stop=(i == TB - 1))
                        pe.wait_ge(probT_ready, n * 2 * PAIRS + 2 * w + 2)
                        for j in range(TB):
                            for r in range(2):
                                last = pe.matmul(ps[HI[r], OUT_Q, seq], lhsT=kn[:, c % 3, b * TB + j, HI[r]],
                                                 rhs=probT[(2 * w + r) % 4][:, j, :], start=(j == 0), stop=(j == TB - 1))
                        last.then_inc(pair_done, 1)

                    def back(t, lot, src, c, start=False, stop=False):
                        return pe.matmul(ps[:, 2 + t, 0:D], lhsT=src[:, c, t * P:(t + 1) * P], rhs=wr[:, lot, c, :],
                                         start=start, stop=stop)

                    def back_mem(t):
                        if t == 0:
                            pe.wait_ge(item_out, n * NITEMS + NITEMS)
                        if t < 2:
                            pe.wait_ge(exp_ready, n * 2 * PAIRS + 2 * PAIRS - 1 + t)
                        else:
                            pe.wait_ge(probT_ready, n * 2 * PAIRS + 2 * PAIRS - 3 + t)
                        for c in range(EMC):
                            back(t, 2, memT, c, start=(c == 0))

                    for h in range(2):
                        if h == 1:
                            transpose_y(1, n)
                        for lot, terms in (((0, 1), hi_terms), ((0, 1), lo_terms), ((2, 3), hi_terms + lo_terms)):
                            for p in lot:
                                last = product(p, terms, h)
                                if h == 1 and terms is not hi_terms:
                                    last.then_inc(item, 1)
                    p = 4
                    for _ in ITEMS_OF[-1][4:]:
                        make(p)
                        p += 1
                    for slot in range(SLOTS_W):
                        if slot < PAIRS:
                            score(slot, 0)
                            score(slot, 1)
                        for _ in ITEMS_OF[slot][:1]:
                            make(p)
                            p += 1
                        if 1 <= slot <= PAIRS:
                            transpose(slot - 1, 0)
                            transpose(slot - 1, 1)
                        for _ in ITEMS_OF[slot][1:]:
                            make(p)
                            p += 1
                        if slot == PAIRS + 1:
                            back_mem(0)
                        if slot >= 2:
                            combine(slot - 2)
                    for t in range(1, T):
                        back_mem(t)
                    for t in range(T):
                        if t == T - 1:
                            transpose_y(0, n + 1)
                        for c in range(EC):
                            pe.wait_ge(dq_ready, n * EC + c + 1)
                            back(t, 0, dqT, c)
                            pe.wait_ge(dk_ready, n * EC + c + 1)
                            last = back(t, 1, dkT, c, stop=(c == EC - 1))
                        last.then_inc(grad_product, 1)

            @block.scalar
            def _(act):

                def g_parts(h, n):
                    act.wait_ge(y_transposed, n * 2 + h + 1)
                    for j in range(DJ):
                        if j == 1:
                            act.wait_ge(g_ready, n * 2 + h + 1)
                        act.activation(g_hi[:, j, half_of(h)], ps[:, Y_BANKS[h][j], 0:NT // 2], ACT.Identity,
                                       bias=ln[:, j, 1:2], scale=ln[:, j, 0:1]).then_inc(g_hi_ready, 1)

                g_parts(0, 0)
                with act.Fori(0, STEPS) as n:
                    g_parts(1, n)

                    def take(p):
                        kind, c = ITEMS[p]
                        act.wait_ge(item, n * NITEMS + p + 1)
                        bank = ps[:, ITEM_BANK[p], :]
                        if kind in ("q", "k"):
                            if c >= 2:
                                act.wait_ge(q_split if kind == "q" else k_split, 2 * EC * n + 2 * c - 2)
                            last = act.copy((q_c if kind == "q" else k_c)[:, c % 2, :], bank)
                        elif kind == "mem":
                            last = act.activation(memT[:, c, :], bank, ACT.Relu)
                        else:
                            if c >= 3:
                                act.wait_ge(pair_done, n * PAIRS + BATCH * (c - 2))
                            last = act.copy((qn if kind == "q_tok" else kn)[:, c % 3, :, :], bank.rearrange("p (t n) -> p t n", t=T))
                        last.then_inc(item_out, 1)

                    def exponentiate(w, r):
                        u = (2 * w + r) % 6
                        act.wait_ge(max_ready, n * 2 * PAIRS + 2 * w + r + 1)
                        if w >= 3:
                            act.wait_ge(pair_done, n * PAIRS + w - 2)
                        for i in range(TB):
                            last = act.activation(prob[u][:, i, :], ps[:, 2 + r, i * SEQ:(i + 1) * SEQ], ACT.Exp,
                                                  bias=neg_max[:, u, i:i + 1], accum_out=row_sum[:, u, i:i + 1])
                        last.then_inc(exp_ready, 1)

                    p = 0
                    for _ in ITEMS_OF[-1]:
                        take(p)
                        p += 1
                    for slot in range(SLOTS_W):
                        if slot >= 4 and slot % 2 == 0:
                            c = slot // 2 - 2
                            act.wait_ge(pair_done, n * PAIRS + 2 * c + 2)
                            act.mul(dqT[:, c, :], ps[:, OUT_Q, :], 1.0 / BETA).then_inc(dq_ready, 1)
                        if slot < PAIRS:
                            exponentiate(slot, 0)
                            exponentiate(slot, 1)
                        for _ in ITEMS_OF[slot][:1]:
                            take(p)
                            p += 1
                        if 1 <= slot <= PAIRS:
                            w = slot - 1
                            for r in range(2):
                                act.wait_ge(transposed, n * 2 * PAIRS + 2 * w + r + 1)
                                if w >= 2:
                                    act.wait_ge(pair_done, n * PAIRS + w - 1)
                                act.copy(probT[(2 * w + r) % 4][:, :, :], ps[:, 4 + r, :].rearrange("p (j n) -> p j n", j=TB)).then_inc(probT_ready, 1)
                        for _ in ITEMS_OF[slot][1:]:
                            take(p)
                            p += 1
                    act.wait_ge(pair_done, n * PAIRS + PAIRS)
                    act.mul(dqT[:, EC - 1, :], ps[:, OUT_Q, :], 1.0 / BETA).then_inc(dq_ready, 1)
                    g_parts(0, n + 1)

            @block.vector
            def _(dve):
                def normalised(y, x, t, n):
                    dve.bn_stats(s.stats[:, t, :], x)
                    dve.drain()
                    dve.bn_aggr(s.mv[:, t, :], s.stats[:, t, :])
                    dve.drain()
                    dve.tensor_scalar(s.var[:, t:t + 1], s.mv[:, t, 1:2], EPS, None, ALU.add).then_inc(var_ready, 1)
                    dve.wait_ge(rstd_ready, n * T + t + 1)
                    if len(y.shape) == 3:
                        x = x.unsqueeze(1).broadcast_to((P, 2, D))
                    return dve.tensor_scalar(y, x, s.mv[:, t, 0:1], s.rstd[:, t:t + 1], ALU.subtract, ALU.mult)

                ln_vector(dve, s, x, s.h, 0, rows_var_ready, rows_rstd_ready)
                dve.drain()
                ln_vector(dve, s, y[:, :, 0, :], x, 1, rows_var_ready, rows_rstd_ready)
                dve.drain()
                dve.tensor_copy(y[:, :, 1, :], y[:, :, 0, :])
                dve.drain()
                dve.sem_inc(y_ready, T)

                def g_parts(h, n):
                    dve.wait_ge(y_transposed, n * 2 + h + 1)
                    for j in (1, 0):
                        if j == 0:
                            dve.wait_ge(g_hi_ready, n * 2 * DJ + h * DJ + 1)
                        last = dve.tensor_scalar(g[:, j, half_of(h)], ps[:, Y_BANKS[h][j], 0:NT // 2],
                                                 ln[:, j, 0:1], ln[:, j, 1:2], ALU.mult, ALU.add)
                        if j == 1:
                            last.then_inc(g_ready, 1)
                    dve.wait_ge(g_hi_ready, n * 2 * DJ + h * DJ + 2)
                    for j in (1, 0):
                        if j == 0:
                            dve.drain()
                        dve.tensor_tensor(g_lo[:, j, half_of(h)], g[:, j, half_of(h)], g_hi[:, j, half_of(h)].bitcast(fp32),
                                          ALU.subtract).then_inc(g_lo_ready, 1)

                g_parts(0, 0)
                with dve.Fori(0, STEPS) as n:
                    g_parts(1, n)

                    def split_q(c):
                        dve.wait_ge(item_out, n * NITEMS + ITEMS.index(("q", c)) + 1)
                        for r in range(2):
                            last = dve.tensor_copy(q_s[HI[r], c % 2, r, :], q_c[HI[r], c % 2, :])
                        last.then_inc(q_hi_ready, 1)

                    def split_k(c):
                        dve.wait_ge(item_out, n * NITEMS + ITEMS.index(("k", c)) + 1)
                        for r in range(2):
                            for at in (HI[r], LO[r]):
                                last = dve.tensor_copy(k_hi[at, c % 2, r, :], k_c[HI[r], c % 2, :])
                        last.then_inc(k_hi_ready, 1)
                        if c == 0:
                            dve.drain()
                            for r in range(2):
                                dve.tensor_tensor(k_lo[HI[r], 0, r, :], k_c[HI[r], 0, :],
                                                  k_hi[HI[r], 0, r, :].bitcast(fp32), ALU.subtract).then_inc(k_split, 1)

                    split_q(0)
                    split_k(0)
                    split_q(1)
                    for slot in range(SLOTS_W):
                        w = slot
                        if slot >= 4 and slot % 2 == 0:
                            c = slot // 2 - 2
                            dve.wait_ge(pair_done, n * PAIRS + 2 * c + 2)
                            dve.tensor_copy(dkT[:, c, :], ps[:, OUT_K, :]).then_inc(dk_ready, 1)
                        if slot < PAIRS:
                            for r in range(2):
                                dve.wait_ge(scores, n * 2 * PAIRS + 2 * w + r + 1)
                                dve.tensor_reduce(neg_max[:, (2 * w + r) % 6, :], ps[:, 2 + r, :].rearrange("p (i m) -> p i m", i=TB),
                                                  axis=AX.X, op=ALU.max, negate=True).then_inc(max_ready, 1)
                            c = slot // 2 + 1 + slot % 2
                            if c < EC:
                                (split_k, split_q)[slot % 2](c)
                            for r in range(2):
                                u = (2 * w + r) % 6
                                dve.wait_ge(exp_ready, n * 2 * PAIRS + 2 * w + r + 1)
                                dve.reciprocal(row_sum[:, u, :], row_sum[:, u, :])
                                dve.drain()
                                for i in range(TB):
                                    last = dve.tensor_scalar(prob[u][:, i, :], prob[u][:, i, :], row_sum[:, u, i:i + 1], None, ALU.mult)
                                last.then_inc(prob_ready, 1)
                    dve.wait_ge(pair_done, n * PAIRS + PAIRS)
                    dve.tensor_copy(dkT[:, EC - 1, :], ps[:, OUT_K, :]).then_inc(dk_ready, 1)
                    for t in range(T):
                        if t == T - 1:
                            g_parts(0, n + 1)
                        dve.wait_ge(grad_product, n * T + t + 1)
                        dve.scalar_tensor_tensor(out=x[:, t, :], in0=ps[:, 2 + t, 0:D], scalar=ALPHA, in1=x[:, t, :],
                                                 op0=ALU.mult, op1=ALU.add)
                        dve.drain()
                        normalised(y[:, t, :, :], x[:, t, :], t, n).then_inc(y_ready, 1)
                dve.tensor_tensor(s.h[:, :, :], s.h[:, :, :], x[:, :, :], ALU.add)


SE = 8
SCAP = 5 * NT // (4 * SE)
SF = 768
SM = SF // P
BUFS = 4


def switch_stage(nc, s, a):
    ctx = ExitStack()
    with ctx:
        def sb(name, shape, dt=fp32):
            return ctx.enter_context(nc.sbuf_tensor(name, shape, dt))

        def sem(name):
            return s.stage_semaphore(name)

        slots = SE * SCAP
        w_switch = sb("sw_w_switch", [DK, DC, SE])
        b_switch = sb("sw_b_switch", [1, SE])
        w1 = [sb(f"sw_w1_{k}", [DK, DC, SF]) for k in range(BUFS)]
        w2 = [sb(f"sw_w2_{k}", [P, SM, D]) for k in range(BUFS)]
        b1 = [sb(f"sw_b1_{k}", [P, SM]) for k in range(BUFS)]
        b2 = [sb(f"sw_b2_{k}", [1, D]) for k in range(BUFS)]
        row_max = sb("sw_row_max", [P, T])
        prob = sb("sw_prob", [P, T, SE])
        top8 = sb("sw_top8", [P, T, 8])
        top8_at = sb("sw_top8_at", [P, T, 8], u32)
        p_max = sb("sw_p_max", [P, T])
        route = sb("sw_route", [P, T])
        all_p = sb("sw_all_p", [P, NT])
        all_r = sb("sw_all_r", [P, NT])
        iota_j = sb("sw_iota_j", [P, slots])
        tok_id = sb("sw_tok_id", [P, T])
        ahead = sb("sw_ahead", [P, T, NT])
        lower = sb("sw_lower", [P, T, P])
        rank = sb("sw_rank", [P, T])
        keep = sb("sw_keep", [P, T])
        dest = sb("sw_dest", [P, T])
        select = sb("sw_select", [P, T, slots])
        selectT = sb("sw_selectT", [SCAP, SE, NT])
        xT = sb("sw_xT", [DK, DC, slots])
        pre = [sb(f"sw_pre{k}", [P, SM, SCAP]) for k in range(2)]
        hid = [sb(f"sw_hid{k}", [P, SM, SCAP]) for k in range(2)]
        out = sb("sw_out", [SCAP, SE, D])
        ps = s.ps

        small_in = sem("sw_small_in")
        up_in = [sem(f"sw_up_in{k}") for k in range(BUFS)]
        down_in = [sem(f"sw_down_in{k}") for k in range(BUFS)]
        var_ready, rstd_ready = sem("sw_var_ready"), sem("sw_rstd_ready")
        consts = sem("sw_consts")
        u_ready = sem("sw_u_ready")
        u_transposed = sem("sw_u_transposed")
        uT_ready = sem("sw_uT_ready")
        logits_ready = sem("sw_logits_ready")
        shifted = sem("sw_shifted")
        exp_ready = sem("sw_exp_ready")
        routed = sem("sw_routed")
        spread = sem("sw_spread")
        select_ready = sem("sw_select_ready")
        x_product = sem("sw_x_product")
        xT_ready = sem("sw_xT_ready")
        select_transposed = sem("sw_select_transposed")
        selectT_ready = sem("sw_selectT_ready")
        up_product = [sem(f"sw_up_product{k}") for k in range(2)]
        pre_ready = [sem(f"sw_pre_ready{k}") for k in range(2)]
        hid_ready = [sem(f"sw_hid_ready{k}") for k in range(2)]
        w_used = [sem(f"sw_w_used{k}") for k in range(BUFS)]
        down_product = [sem(f"sw_down_product{k}") for k in range(2)]
        out_ready = [sem(f"sw_out_ready{k}") for k in range(2)]
        back_product = sem("sw_back_product")

        with nc.Block() as block:
            @block.sync
            def _(sp):
                sp.dma_start(w_switch[:, :, :], a["sw_w_switch"].rearrange("(c p) e -> p c e", p=DK)).then_inc(small_in, 16)
                sp.dma_start(b_switch[:, :], a["sw_b_switch"]).then_inc(small_in, 16)
                with sp.Fori(0, SE // BUFS) as i:
                    for k in range(BUFS):
                        e = bass.ds(BUFS * i + k, 1)
                        sp.wait_ge(w_used[k], i + 1)
                        sp.dma_start(w1[k][:, :, :], a["sw_w1"][e, :, :].rearrange("o (c p) f -> p (o c) f", p=DK)).then_inc(up_in[k], 16)
                        sp.dma_start(b1[k][:, :], a["sw_b1"][e, :, :].rearrange("o p m -> p (o m)")).then_inc(up_in[k], 16)
                        sp.dma_start(w2[k][:, :, :], a["sw_w2"][e, :, :].rearrange("o (c p) d -> p (o c) d", p=P)).then_inc(down_in[k], 16)
                        sp.dma_start(b2[k][:, :], a["sw_b2"][e, :]).then_inc(down_in[k], 16)

            @block.gpsimd
            def _(pool):
                pool.iota(iota_j[:, :], [[1, slots]], base=0, channel_multiplier=0, allow_small_or_imprecise_dtypes=True).then_inc(consts, 1)
                pool.iota(tok_id[:, :], [[P, T]], base=0, channel_multiplier=1, allow_small_or_imprecise_dtypes=True).then_inc(consts, 1)
                ln_pool(pool, s, 0, var_ready, rstd_ready)

            @block.tensor
            def _(pe):
                for k in range(BUFS):
                    pe.sem_inc(w_used[k], 1)
                for k in range(2):
                    pe.sem_inc(down_product[k], 1)
                pe.wait_ge(u_ready, 1)
                transpose_u(pe, s).then_inc(u_transposed, 1)
                pe.wait_ge(uT_ready, 1)
                pe.wait_ge(small_in, 32)
                for t in range(T):
                    at = slice(t * SE, (t + 1) * SE)
                    for c in range(DC):
                        pe.matmul(ps[:, 2, at], lhsT=s.uT[:, c, t * P:(t + 1) * P], rhs=w_switch[:, c, :], start=(c == 0), stop=False)
                    last = pe.matmul(ps[:, 2, at], lhsT=s.ones[0:1, :], rhs=b_switch[:, :], start=False, stop=True)
                last.then_inc(logits_ready, 1)
                pe.wait_ge(routed, 1)
                for bank, src in ((3, p_max), (4, route)):
                    for t in range(T):
                        last = pe.matmul(ps[:, bank, t * P:(t + 1) * P], lhsT=src[:, t:t + 1].broadcast_to((P, P)),
                                         rhs=s.ident[:, :], start=True, stop=True)
                last.then_inc(spread, 1)
                pe.wait_ge(select_ready, 1)
                for c in range(DC):
                    for half in range(2):
                        for t in range(T):
                            last = pe.matmul(ps[0:DK, 2 * c + half, 0:slots // 2], lhsT=s.u[:, t, c * DK:(c + 1) * DK],
                                             rhs=select[:, t, half * slots // 2:(half + 1) * slots // 2],
                                             start=(t == 0), stop=(t == T - 1))
                last.then_inc(x_product, 1)
                for e in range(SE):
                    if e >= 4:
                        pe.wait_ge(selectT_ready, e - 3)
                    for t in range(T):
                        last = pe.transpose(ps[0:SCAP, 4 + e % 4, t * P:(t + 1) * P], select[:, t, e * SCAP:(e + 1) * SCAP], s.ident[:, :])
                    last.then_inc(select_transposed, 1)
                pe.wait_ge(xT_ready, 1)
                pe.wait_ge(selectT_ready, SE)
                with pe.Fori(0, SE // BUFS) as i:
                    for j in range(BUFS // 2):
                        n = i * (BUFS // 2) + j
                        for k in range(2):
                            w = 2 * j + k
                            pe.wait_ge(up_in[w], i * 32 + 32)
                            pe.wait_ge(pre_ready[k], n + 1)
                            for m in range(SM):
                                for c in range(DC):
                                    last = pe.matmul(ps[:, 4 + k, m * SCAP:(m + 1) * SCAP], lhsT=w1[w][:, c, m * P:(m + 1) * P],
                                                     rhs=xT[:, c, bass.ds((BUFS * i + w) * SCAP, SCAP)], start=(c == 0), stop=(c == DC - 1))
                            last.then_inc(up_product[k], 1)
                        for k in range(2):
                            w = 2 * j + k
                            pe.wait_ge(hid_ready[k], n + 2)
                            pe.wait_ge(down_in[w], i * 32 + 32)
                            pe.wait_ge(out_ready[k], n + 1)
                            for m in range(SM):
                                pe.matmul(ps[0:SCAP, 6 + k, 0:D], lhsT=hid[k][:, m, :], rhs=w2[w][:, m, :], start=(m == 0), stop=False)
                            pe.matmul(ps[0:SCAP, 6 + k, 0:D], lhsT=s.ones[0:1, 0:SCAP], rhs=b2[w][:, :], start=False, stop=True).then_inc(down_product[k], 1)
                            pe.wait_ge(down_product[k], n + 2)
                            pe.sem_inc(w_used[w], 1)
                for k in range(2):
                    pe.wait_ge(out_ready[k], SE // 2 + 1)
                for t in range(T):
                    for e in range(SE):
                        last = pe.matmul(ps[:, t, 0:D], lhsT=selectT[:, e, t * P:(t + 1) * P], rhs=out[:, e, :],
                                         start=(e == 0), stop=(e == SE - 1))
                last.then_inc(back_product, 1)

            @block.scalar
            def _(act):
                for k in range(2):
                    act.sem_inc(hid_ready[k], 1)
                act.wait_ge(shifted, 1)
                act.activation(prob[:, :, :], prob[:, :, :], ACT.Exp).then_inc(exp_ready, 1)
                for e in range(SE):
                    act.wait_ge(select_transposed, e + 1)
                    act.copy(selectT[:, e, :], ps[0:SCAP, 4 + e % 4, :]).then_inc(selectT_ready, 1)
                with act.Fori(0, SE // 2) as i:
                    for k in range(2):
                        act.wait_ge(pre_ready[k], i + 2)
                        act.wait_ge(down_product[k], i + 1)
                        act.activation(hid[k][:, :, :], pre[k][:, :, :], ACT.Gelu).then_inc(hid_ready[k], 1)

            @block.vector
            def _(dve):
                for k in range(2):
                    dve.sem_inc(pre_ready[k], 1)
                    dve.sem_inc(out_ready[k], 1)
                ln_vector(dve, s, s.u, s.h, 0, var_ready, rstd_ready).then_inc(u_ready, 1)
                dve.wait_ge(u_transposed, 1)
                dve.tensor_copy(s.uT[:, :, :], ps[0:DK, 0:DC, :]).then_inc(uT_ready, 1)
                logits = ps[:, 2, 0:T * SE].rearrange("p (t e) -> p t e", t=T)
                dve.wait_ge(logits_ready, 1)
                dve.reduce_max(row_max[:, :], logits, AX.X)
                dve.drain()
                dve.tensor_tensor(prob[:, :, :], logits, row_max[:, :].unsqueeze(2).broadcast_to((P, T, SE)), ALU.subtract).then_inc(shifted, 1)
                dve.wait_ge(exp_ready, 1)
                dve.reduce_sum(row_max[:, :], prob[:, :, :], AX.X)
                dve.drain()
                dve.reciprocal(row_max[:, :], row_max[:, :])
                dve.drain()
                dve.tensor_tensor(prob[:, :, :], prob[:, :, :], row_max[:, :].unsqueeze(2).broadcast_to((P, T, SE)), ALU.mult)
                dve.drain()
                for t in range(T):
                    dve.max(top8[:, t, :], prob[:, t, :])
                dve.drain()
                for t in range(T):
                    dve.max_index(top8_at[:, t, :], top8[:, t, :], prob[:, t, :])
                dve.drain()
                dve.tensor_copy(p_max[:, :], top8[:, :, 0])
                dve.tensor_copy(route[:, :], top8_at[:, :, 0]).then_inc(routed, 1)
                dve.wait_ge(consts, 2)
                for t in range(T):
                    dve.tensor_scalar(lower[:, t, :], iota_j[:, t * P:(t + 1) * P], tok_id[:, t:t + 1], None, ALU.is_lt)
                dve.wait_ge(spread, 1)
                dve.tensor_copy(all_p[:, :], ps[:, 3, :])
                dve.tensor_copy(all_r[:, :], ps[:, 4, :])
                dve.drain()
                for t in range(T):
                    own = slice(t * P, (t + 1) * P)
                    if t > 0:
                        dve.tensor_scalar(ahead[:, t, 0:t * P], all_p[:, 0:t * P], p_max[:, t:t + 1], None, ALU.is_ge)
                    if t < T - 1:
                        dve.tensor_scalar(ahead[:, t, (t + 1) * P:], all_p[:, (t + 1) * P:], p_max[:, t:t + 1], None, ALU.is_gt)
                    dve.scalar_tensor_tensor(out=ahead[:, t, own], in0=all_p[:, own], scalar=p_max[:, t:t + 1], in1=lower[:, t, :],
                                             op0=ALU.is_equal, op1=ALU.mult)
                dve.drain()
                for t in range(T):
                    own = slice(t * P, (t + 1) * P)
                    dve.scalar_tensor_tensor(out=ahead[:, t, own], in0=all_p[:, own], scalar=p_max[:, t:t + 1], in1=ahead[:, t, own],
                                             op0=ALU.is_gt, op1=ALU.add)
                dve.drain()
                for t in range(T):
                    dve.scalar_tensor_tensor(out=ahead[:, t, :], in0=all_r[:, :], scalar=route[:, t:t + 1], in1=ahead[:, t, :],
                                             op0=ALU.is_equal, op1=ALU.mult)
                dve.drain()
                dve.reduce_sum(rank[:, :], ahead[:, :, :], AX.X)
                dve.drain()
                dve.tensor_scalar(keep[:, :], rank[:, :], float(SCAP), None, ALU.is_lt)
                dve.scalar_tensor_tensor(out=dest[:, :], in0=route[:, :], scalar=float(SCAP), in1=rank[:, :], op0=ALU.mult, op1=ALU.add)
                dve.drain()
                dve.scalar_tensor_tensor(out=dest[:, :], in0=dest[:, :], scalar=1.0, in1=keep[:, :], op0=ALU.add, op1=ALU.mult)
                dve.drain()
                dve.tensor_scalar(dest[:, :], dest[:, :], -1.0, None, ALU.add)
                dve.drain()
                for t in range(T):
                    last = dve.tensor_scalar(select[:, t, :], iota_j[:, :], dest[:, t:t + 1], None, ALU.is_equal)
                last.then_inc(select_ready, 1)
                dve.wait_ge(x_product, 1)
                dve.tensor_copy(xT[:, :, :].rearrange("p c (h n) -> p (c h) n", h=2), ps[0:DK, 0:2 * DC, 0:slots // 2]).then_inc(xT_ready, 1)
                with dve.Fori(0, SE // BUFS) as i:
                    for j in range(BUFS // 2):
                        n = i * (BUFS // 2) + j
                        for k in range(2):
                            dve.wait_ge(up_product[k], n + 1)
                            dve.wait_ge(up_in[2 * j + k], i * 32 + 32)
                            dve.wait_ge(hid_ready[k], n + 1)
                            dve.tensor_tensor(pre[k][:, :, :], ps[:, 4 + k, 0:SM * SCAP].rearrange("p (m n) -> p m n", m=SM),
                                              b1[2 * j + k][:, :].unsqueeze(2).broadcast_to((P, SM, SCAP)), ALU.add).then_inc(pre_ready[k], 1)
                        for k in range(2):
                            dve.wait_ge(down_product[k], n + 2)
                            dve.tensor_copy(out[:, bass.ds(BUFS * i + 2 * j + k, 1), :], ps[0:SCAP, 6 + k, 0:D].unsqueeze(1)).then_inc(out_ready[k], 1)
                dve.tensor_scalar(keep[:, :], keep[:, :], -1.0, 1.0, ALU.mult, ALU.add)
                dve.drain()
                dve.wait_ge(back_product, 1)
                for t in range(T):
                    dve.scalar_tensor_tensor(out=s.u[:, t, :], in0=s.u[:, t, :], scalar=keep[:, t:t + 1], in1=ps[:, t, 0:D],
                                             op0=ALU.mult, op1=ALU.add)
                dve.drain()
                for t in range(T):
                    dve.scalar_tensor_tensor(out=s.h[:, t, :], in0=s.u[:, t, :], scalar=p_max[:, t:t + 1], in1=s.h[:, t, :],
                                             op0=ALU.mult, op1=ALU.add)


def laid_out(i):
    g = {k: np.asarray(v) for k, v in i.items()}
    put = {}

    def add(name, a):
        put[name] = np.ascontiguousarray(a)

    add("patches", g["x"].reshape(2, 32, 16, 8, 16, 8).transpose(1, 3, 5, 0, 2, 4).reshape(2048, NT))
    add("conv_w", g["L0_tok_conv_w"].reshape(TD, 2048).T)
    add("conv_b", g["L0_tok_conv_b"].reshape(1, TD))
    add("tok_cols", np.concatenate([np.stack([g["L0_tok_" + k] for k in ("ln1_g", "ln1_b", "ln2_g", "ln2_b")], axis=2),
                                    g["L0_tok_ff1_b"].reshape(LAYERS, FC, P).transpose(0, 2, 1)], axis=2))
    add("tok_rows", np.stack([g["L0_tok_out_b"], g["L0_tok_ff2_b"]], axis=1).reshape(LAYERS, 1, 2, TD))
    add("qkv_w", g["L0_tok_qkv_w"])
    add("out_w", g["L0_tok_out_w"])
    add("ff1_w", g["L0_tok_ff1_w"])
    add("ff2_w", g["L0_tok_ff2_w"])
    add("tok_lnf", np.stack([g["L0_tok_lnf_g"], g["L0_tok_lnf_b"]], axis=1))
    add("head_w", g["L0_tok_head_w"])
    add("head_b", g["L0_tok_head_b"].reshape(1, D))
    add("mb_w_in", g["L0_attn_w_in"].T)
    add("mb_cols", np.concatenate([g["L0_attn_w_conv"][:, 0, :]] + [g["L0_attn_" + k].reshape(DIN, 1)
                                   for k in ("b_conv", "b_dt", "D_param")], axis=1))
    add("mb_a_log", g["L0_attn_A_log"])
    add("mb_w_x", g["L0_attn_w_xproj"].T)
    add("mb_w_dt", g["L0_attn_w_dt"].T)
    add("mb_w_out", g["L0_attn_w_out"].T)
    add("mb_w_norm", g["L0_attn_w_norm"].reshape(1, D))
    add("moe_w_router", g["L0_ffn_Wg"].T)
    add("moe_e_bias", g["L0_ffn_e_bias"].reshape(1, NE))
    add("moe_w_gu", g["L0_ffn_W_gate_up"])
    add("moe_w_d", g["L0_ffn_W_down"])
    add("moe_w_sgu", np.stack([g["L0_ffn_Wsg"], g["L0_ffn_Wsu"]]))
    add("moe_w_sd", g["L0_ffn_Wsd"])
    add("en_ln", np.stack([g["L1_attn_ln_gamma"], g["L1_attn_ln_beta"]], axis=1))
    w = np.stack([g["L1_attn_wq"].reshape(EM, D), g["L1_attn_wk"].reshape(EM, D), g["L1_attn_xi"]])
    add("en_w", w)
    add("en_wT", w.transpose(0, 2, 1))
    add("sw_w_switch", g["L1_ffn_switch_w"])
    add("sw_b_switch", g["L1_ffn_switch_b"].reshape(1, SE))
    add("sw_w1", g["L1_ffn_w1"])
    add("sw_b1", g["L1_ffn_b1"].reshape(SE, SM, P).transpose(0, 2, 1))
    add("sw_w2", g["L1_ffn_w2"])
    add("sw_b2", g["L1_ffn_b2"])
    return put


def vit_tower(nc, a):
    with ExitStack() as ctx:
        s = Shared(nc, ctx)
        setup_stage(nc, s)
        s.end_stage()
        tok_stage(nc, s, a)
        s.end_stage()
        mamba_stage(nc, s, a)
        s.end_stage()
        energy_weights = EnergyWeights(nc, ctx)
        moe_stage(nc, s, a, energy_weights)
        s.end_stage()
        energy_stage(nc, s, a, energy_weights)
        s.end_stage()
        switch_stage(nc, s, a)
        s.end_stage()
        h_stored = s.stage_semaphore("h_stored")
        with nc.Block() as block:
            @block.sync
            def _(sp):
                sp.dma_start(a["out"].rearrange("(t p) d -> p t d", p=P), s.h[:, :, :]).then_inc(h_stored, 16)
                sp.wait_ge(h_stored, 16)


def kernel(**inputs):
    import concourse.bacc as bacc
    from concourse.bass_utils import run_bass_kernel_spmd

    nc = bacc.Bacc("TRN2", target_bir_lowering=False, num_devices=1)
    put = laid_out(inputs)
    a = {name: nc.dram_tensor("in_" + name, v.shape, mybir.dt.from_np(v.dtype), kind="ExternalInput").ap()
         for name, v in put.items()}
    a["out"] = nc.dram_tensor("out_h", (NT, D), fp32, kind="ExternalOutput").ap()
    vit_tower(nc, a)
    r = run_bass_kernel_spmd(nc, [{"in_" + name: v for name, v in put.items()}], core_ids=[0])
    return r.results[0]["out_h"].reshape(BATCH, SEQ, D)
```
